# Optimizing a Trainium2 kernel written in Bass

```python
import numpy as np
import jax
import jax.numpy as jnp

def _softmax(x, axis=-1):
    return jax.nn.softmax(x, axis=axis)

def _gelu(x):
    return jax.nn.gelu(x, approximate=True)

def _silu(x):
    return jax.nn.silu(x)

def _sigmoid(x):
    return jax.nn.sigmoid(x)

def _layernorm(x, axis=-1, eps=1e-05):
    m = jnp.mean(x, axis=axis, keepdims=True)
    v = jnp.var(x, axis=axis, keepdims=True)
    return (x - m) / jnp.sqrt(v + eps)

def _scatter_add(tgt, idx, src, axis=0):
    return tgt.at[idx].add(src)

def _segment_sum(src, seg, n):
    return jax.ops.segment_sum(src, seg, n)
kernel_name = 'mk_flamingo_gated_d2_seqx_r4_d26c5f'

def setup_inputs(seed: int=0):
    np.random.seed(seed)
    _w = jnp.asarray

    def _rec_inputs():
        import jax
        import jax.numpy as jnp
        _rk = jax.random.key(seed)
        x = 0.002226 + 0.9996 * jax.random.normal(jax.random.fold_in(_rk, 1), (1, 2048, 256), jnp.float32)
        _lenS = 2048 - jax.random.randint(jax.random.fold_in(_rk, 7), (1,), 0, max(1, 2048 // 4) + 1, jnp.int32)
        _lenS2 = 1601 - jax.random.randint(jax.random.fold_in(_rk, 8), (1,), 0, max(1, 1601 // 4) + 1, jnp.int32)
        _ctx_1024P = jax.random.normal(jax.random.fold_in(_rk, 11), (1, 16, 256), jnp.float32)
        _ctx_1024c = jax.random.dirichlet(jax.random.fold_in(_rk, 511), 0.3 * jnp.ones((16,), jnp.float32), (1, 1601))
        _ctx_1024t = jnp.einsum('bsk,bkd->bsd', _ctx_1024c, _ctx_1024P)
        _ctx_1024t = _ctx_1024t * jax.lax.rsqrt(jnp.mean(jnp.square(_ctx_1024t)) + 1e-12) * 0.953939
        ctx_1024 = -0.000125008 + 0.999885 * (_ctx_1024t + 0.3 * jax.random.normal(jax.random.fold_in(_rk, 611), (1, 1601, 256), jnp.float32))
        _validS = jnp.arange(2048)[None, :] < _lenS[:, None]
        _validS2 = jnp.arange(1601)[None, :] < _lenS2[:, None]
        _causal = jnp.tril(jnp.ones((2048, 2048), dtype=bool))
        mask_BxS2_bk0 = jnp.logical_not(jnp.broadcast_to(_validS2[:, :], (1, 1601)))
        _g = jax.random.normal(jax.random.fold_in(_rk, 9001), (2, 2), jnp.float32)
        _g = jnp.sign(_g) * jnp.maximum(jnp.abs(_g), 1.0) + (_g == 0) * 1.0
        g_xattn = _g[0]
        g_ffn = _g[1]
        return (x, ctx_1024, mask_BxS2_bk0, g_xattn, g_ffn)
    x, ctx_1024, mask_BxS2_bk0, g_xattn, g_ffn = _rec_inputs()

    def _L0_xattn_setup():
        import jax, jax.numpy as jnp
        import numpy as np
        EPS = 1e-05

        def layer_norm(x, g, b):
            mu = jnp.mean(x, axis=-1, keepdims=True)
            var = jnp.mean((x - mu) ** 2, axis=-1, keepdims=True)
            return (x - mu) * jax.lax.rsqrt(var + EPS) * g + b
        key = jax.random.key(seed)
        ks = jax.random.split(key, 8)
        b, n, l, D = (8, 1024, 64, 256)
        heads, dim_head = (16, 64)
        inner = heads * dim_head
        x = jax.random.normal(ks[0], (b, n, D), dtype=jnp.float32)
        latents = jax.random.normal(ks[1], (b, l, D), dtype=jnp.float32)
        mask = jax.random.randint(ks[2], (b, n), 0, 2) > 0
        Wq = jax.random.normal(ks[3], (D, inner), dtype=jnp.float32) * D ** (-0.5)
        Wkv = jax.random.normal(ks[4], (D, 2 * inner), dtype=jnp.float32) * D ** (-0.5)
        Wout = jax.random.normal(ks[5], (inner, D), dtype=jnp.float32) * inner ** (-0.5)
        g1 = jnp.ones((D,), jnp.float32)
        b1 = jnp.zeros((D,), jnp.float32)
        g2 = jnp.ones((D,), jnp.float32)
        b2 = jnp.zeros((D,), jnp.float32)
        return {'x': x, 'latents': latents, 'mask': mask, 'g1': g1, 'b1': b1, 'g2': g2, 'b2': b2, 'Wq': Wq, 'Wkv': Wkv, 'Wout': Wout}
    _L0_xattn_all = _L0_xattn_setup()
    _L0_xattn_in = {k: v for k, v in _L0_xattn_all.items() if k in ('g1', 'b1', 'g2', 'b2', 'Wq', 'Wkv', 'Wout')}
    del _L0_xattn_all

    def _L0_ffn_setup():
        import jax, jax.numpy as jnp
        import numpy as np
        D_MODEL = 256
        D_FF = 1024
        N_EXPERTS = 8
        TOP_K = 2
        D_FF_PER = D_FF // N_EXPERTS
        B, T = (4, 512)
        key = jax.random.key(seed)
        ks = jax.random.split(key, 7)
        b1_bound = 1.0 / np.sqrt(D_MODEL)
        b2_bound = 1.0 / np.sqrt(D_FF_PER)
        return {'x': jax.random.normal(ks[0], (B, T, D_MODEL), dtype=jnp.float32), 'router_w': jax.random.uniform(ks[1], (D_MODEL, N_EXPERTS), minval=-b1_bound, maxval=b1_bound, dtype=jnp.float32), 'router_b': jax.random.uniform(ks[2], (N_EXPERTS,), minval=-b1_bound, maxval=b1_bound, dtype=jnp.float32), 'W1': jax.random.uniform(ks[3], (N_EXPERTS, D_MODEL, D_FF_PER), minval=-b1_bound, maxval=b1_bound, dtype=jnp.float32), 'b1': jax.random.uniform(ks[4], (N_EXPERTS, D_FF_PER), minval=-b1_bound, maxval=b1_bound, dtype=jnp.float32), 'W2': jax.random.uniform(ks[5], (N_EXPERTS, D_FF_PER, D_MODEL), minval=-b2_bound, maxval=b2_bound, dtype=jnp.float32), 'b2': jax.random.uniform(ks[6], (N_EXPERTS, D_MODEL), minval=-b2_bound, maxval=b2_bound, dtype=jnp.float32)}
    _L0_ffn_all = _L0_ffn_setup()
    _L0_ffn_in = {k: v for k, v in _L0_ffn_all.items() if k in ('router_w', 'router_b', 'W1', 'b1', 'W2', 'b2')}
    del _L0_ffn_all

    def _L1_xattn_setup():
        import jax, jax.numpy as jnp
        import numpy as np
        DIM = 256
        HEADS = 16
        HEAD_DIM = DIM // HEADS
        key = jax.random.key(seed)
        ks = jax.random.split(key, 10)
        B, N, M = (4, 512, 512)
        s = 1.0 / np.sqrt(DIM)
        return {'x': jax.random.normal(ks[0], (B, N, DIM), jnp.float32), 'context': jax.random.normal(ks[1], (B, M, DIM), jnp.float32), 'Wq': jax.random.normal(ks[2], (DIM, DIM), jnp.float32) * s, 'bq': jnp.zeros((DIM,), jnp.float32), 'Wk': jax.random.normal(ks[3], (DIM, DIM), jnp.float32) * s, 'bk': jnp.zeros((DIM,), jnp.float32), 'Wv': jax.random.normal(ks[4], (DIM, DIM), jnp.float32) * s, 'bv': jnp.zeros((DIM,), jnp.float32), 'Wo': jax.random.normal(ks[5], (DIM, DIM), jnp.float32) * s, 'bo': jnp.zeros((DIM,), jnp.float32)}
    _L1_xattn_all = _L1_xattn_setup()
    _L1_xattn_in = {k: v for k, v in _L1_xattn_all.items() if k in ('Wq', 'bq', 'Wk', 'bk', 'Wv', 'bv', 'Wo', 'bo')}
    del _L1_xattn_all

    def _L1_ffn_setup():
        import jax, jax.numpy as jnp
        import numpy as np
        HIDDEN = 256
        INNER = 1024

        def _weight_quant(w):
            scale = 1.0 / jnp.clip(jnp.mean(jnp.abs(w)), 1e-05)
            wq = jnp.clip(jnp.round(w * scale), -1.0, 1.0) / scale
            return w + jax.lax.stop_gradient(wq - w)

        def _act_quant(x):
            scale = 127.0 / jnp.clip(jnp.max(jnp.abs(x), axis=-1, keepdims=True), 1e-05)
            xq = jnp.clip(jnp.round(x * scale), -128.0, 127.0) / scale
            return x + jax.lax.stop_gradient(xq - x)

        def _bitlinear(x, w):
            return jnp.einsum('bsi,oi->bso', _act_quant(x), _weight_quant(w))
        key = jax.random.key(seed)
        k0, k1, k2, k3 = jax.random.split(key, 4)
        x = jax.random.normal(k0, (4, 512, HIDDEN), dtype=jnp.float32)
        w_gate = jax.random.normal(k1, (INNER, HIDDEN), dtype=jnp.float32) / np.sqrt(HIDDEN)
        w_up = jax.random.normal(k2, (INNER, HIDDEN), dtype=jnp.float32) / np.sqrt(HIDDEN)
        w_down = jax.random.normal(k3, (HIDDEN, INNER), dtype=jnp.float32) / np.sqrt(INNER)
        return {'x': x, 'w_gate': w_gate, 'w_up': w_up, 'w_down': w_down}
    _L1_ffn_all = _L1_ffn_setup()
    _L1_ffn_in = {k: v for k, v in _L1_ffn_all.items() if k in ('w_gate', 'w_up', 'w_down')}
    del _L1_ffn_all
    return {'x': x, 'ctx_1024': ctx_1024, 'mask_BxS2_bk0': mask_BxS2_bk0, 'g_xattn': g_xattn, 'g_ffn': g_ffn, 'L0_xattn_g1': _L0_xattn_in['g1'], 'L0_xattn_b1': _L0_xattn_in['b1'], 'L0_xattn_g2': _L0_xattn_in['g2'], 'L0_xattn_b2': _L0_xattn_in['b2'], 'L0_xattn_Wq': _L0_xattn_in['Wq'], 'L0_xattn_Wkv': _L0_xattn_in['Wkv'], 'L0_xattn_Wout': _L0_xattn_in['Wout'], 'L0_ffn_router_w': _L0_ffn_in['router_w'], 'L0_ffn_router_b': _L0_ffn_in['router_b'], 'L0_ffn_W1': _L0_ffn_in['W1'], 'L0_ffn_b1': _L0_ffn_in['b1'], 'L0_ffn_W2': _L0_ffn_in['W2'], 'L0_ffn_b2': _L0_ffn_in['b2'], 'L1_xattn_Wq': _L1_xattn_in['Wq'], 'L1_xattn_bq': _L1_xattn_in['bq'], 'L1_xattn_Wk': _L1_xattn_in['Wk'], 'L1_xattn_bk': _L1_xattn_in['bk'], 'L1_xattn_Wv': _L1_xattn_in['Wv'], 'L1_xattn_bv': _L1_xattn_in['bv'], 'L1_xattn_Wo': _L1_xattn_in['Wo'], 'L1_xattn_bo': _L1_xattn_in['bo'], 'L1_ffn_w_gate': _L1_ffn_in['w_gate'], 'L1_ffn_w_up': _L1_ffn_in['w_up'], 'L1_ffn_w_down': _L1_ffn_in['w_down']}

def reference(x, ctx_1024, mask_BxS2_bk0, g_xattn, g_ffn, L0_xattn_g1, L0_xattn_b1, L0_xattn_g2, L0_xattn_b2, L0_xattn_Wq, L0_xattn_Wkv, L0_xattn_Wout, L0_ffn_router_w, L0_ffn_router_b, L0_ffn_W1, L0_ffn_b1, L0_ffn_W2, L0_ffn_b2, L1_xattn_Wq, L1_xattn_bq, L1_xattn_Wk, L1_xattn_bk, L1_xattn_Wv, L1_xattn_bv, L1_xattn_Wo, L1_xattn_bo, L1_ffn_w_gate, L1_ffn_w_up, L1_ffn_w_down):
    import jax
    import jax.numpy as jnp

    def _L0_xattn_ref(x, latents, mask, g1, b1, g2, b2, Wq, Wkv, Wout):
        import jax, jax.numpy as jnp
        import numpy as np
        EPS = 1e-05

        def layer_norm(x, g, b):
            mu = jnp.mean(x, axis=-1, keepdims=True)
            var = jnp.mean((x - mu) ** 2, axis=-1, keepdims=True)
            return (x - mu) * jax.lax.rsqrt(var + EPS) * g + b
        heads, dim_head = (16, 64)
        b, n, D = x.shape
        l = latents.shape[1]
        xn = layer_norm(x, g1, b1)
        ln_lat = layer_norm(latents, g2, b2)
        q = ln_lat @ Wq
        kv = jnp.concatenate([xn, ln_lat], axis=1) @ Wkv
        k, v = jnp.split(kv, 2, axis=-1)

        def to_heads(t):
            return t.reshape(t.shape[0], t.shape[1], heads, dim_head).transpose(0, 2, 1, 3)
        q, k, v = (to_heads(q), to_heads(k), to_heads(v))
        scale = 1.0 / np.sqrt(np.sqrt(dim_head)).astype(np.float32)
        weight = jnp.einsum('bhld,bhnd->bhln', q * scale, k * scale)
        full_mask = jnp.concatenate([mask, jnp.ones((b, l), dtype=bool)], axis=1)
        neg = -jnp.finfo(weight.dtype).max
        weight = jnp.where(full_mask[:, None, None, :], weight, neg)
        weight = jax.nn.softmax(weight.astype(jnp.float32), axis=-1).astype(q.dtype)
        out = jnp.einsum('bhln,bhnd->bhld', weight, v)
        out = out.transpose(0, 2, 1, 3).reshape(b, l, heads * dim_head)
        return out @ Wout

    def _L0_ffn_ref(x, router_w, router_b, W1, b1, W2, b2):
        import jax, jax.numpy as jnp
        import numpy as np
        D_MODEL = 256
        D_FF = 1024
        N_EXPERTS = 8
        TOP_K = 2
        D_FF_PER = D_FF // N_EXPERTS
        B, T = (4, 512)
        router_logits = x @ router_w + router_b
        routing_weights = jax.nn.softmax(router_logits, axis=-1)
        top_k_weights, top_k_indices = jax.lax.top_k(routing_weights, TOP_K)
        top_k_weights = top_k_weights / jnp.sum(top_k_weights, axis=-1, keepdims=True)
        routing_mask = jnp.zeros_like(routing_weights)
        routing_mask = jnp.take_along_axis(routing_mask, top_k_indices, axis=-1)
        b_idx = jnp.arange(x.shape[0])[:, None, None]
        t_idx = jnp.arange(x.shape[1])[None, :, None]
        routing_mask = jnp.zeros_like(routing_weights).at[b_idx, t_idx, top_k_indices].set(top_k_weights)
        h1 = jnp.einsum('btd,nde->btne', x, W1) + b1
        h1 = jax.nn.gelu(h1, approximate=False)
        out_per_expert = jnp.einsum('btne,nef->btnf', h1, W2) + b2
        output = jnp.sum(out_per_expert * routing_mask[..., None], axis=-2)
        return output

    def _L1_xattn_ref(x, context, Wq, bq, Wk, bk, Wv, bv, Wo, bo):
        import jax, jax.numpy as jnp
        import numpy as np
        DIM = 256
        HEADS = 16
        HEAD_DIM = DIM // HEADS
        B, N, C = x.shape
        M = context.shape[1]
        scale = HEAD_DIM ** (-0.5)
        q = (x @ Wq.T + bq).reshape(B, N, HEADS, HEAD_DIM).transpose(0, 2, 1, 3)
        k = (context @ Wk.T + bk).reshape(B, M, HEADS, HEAD_DIM).transpose(0, 2, 1, 3)
        v = (context @ Wv.T + bv).reshape(B, M, HEADS, HEAD_DIM).transpose(0, 2, 1, 3)
        attn = jax.nn.softmax(jnp.einsum('bhnd,bhmd->bhnm', q, k) * scale, axis=-1)
        out = jnp.einsum('bhnm,bhmd->bhnd', attn, v)
        out = out.transpose(0, 2, 1, 3).reshape(B, N, C)
        return out @ Wo.T + bo

    def _L1_ffn_ref(x, w_gate, w_up, w_down):
        import jax, jax.numpy as jnp
        import numpy as np
        HIDDEN = 256
        INNER = 1024

        def _weight_quant(w):
            scale = 1.0 / jnp.clip(jnp.mean(jnp.abs(w)), 1e-05)
            wq = jnp.clip(jnp.round(w * scale), -1.0, 1.0) / scale
            return w + jax.lax.stop_gradient(wq - w)

        def _act_quant(x):
            scale = 127.0 / jnp.clip(jnp.max(jnp.abs(x), axis=-1, keepdims=True), 1e-05)
            xq = jnp.clip(jnp.round(x * scale), -128.0, 127.0) / scale
            return x + jax.lax.stop_gradient(xq - x)

        def _bitlinear(x, w):
            return jnp.einsum('bsi,oi->bso', _act_quant(x), _weight_quant(w))
        gate = jax.nn.silu(_bitlinear(x, w_gate))
        up = _bitlinear(x, w_up)
        return _bitlinear(gate * up, w_down)
    x = x + jnp.tanh(g_xattn[0]) * _L0_xattn_ref(ctx_1024, _layernorm(x, axis=-1), mask_BxS2_bk0, L0_xattn_g1, L0_xattn_b1, L0_xattn_g2, L0_xattn_b2, L0_xattn_Wq, L0_xattn_Wkv, L0_xattn_Wout)
    x = x + jnp.tanh(g_ffn[0]) * _L0_ffn_ref(_layernorm(x, axis=-1), L0_ffn_router_w, L0_ffn_router_b, L0_ffn_W1, L0_ffn_b1, L0_ffn_W2, L0_ffn_b2)
    x = x + jnp.tanh(g_xattn[1]) * _L1_xattn_ref(_layernorm(x, axis=-1), ctx_1024, L1_xattn_Wq, L1_xattn_bq, L1_xattn_Wk, L1_xattn_bk, L1_xattn_Wv, L1_xattn_bv, L1_xattn_Wo, L1_xattn_bo)
    x = x + jnp.tanh(g_ffn[1]) * _L1_ffn_ref(_layernorm(x, axis=-1), L1_ffn_w_gate, L1_ffn_w_up, L1_ffn_w_down)
    return x

_drawn_inputs = setup_inputs


def setup_inputs(seed=0):
    import zlib

    import numpy as np

    out = dict(_drawn_inputs(seed))
    spreads = {'g_ffn': (-1.0, 0.6),
     'L0_xattn_g1': (1.0, 0.6),
     'L0_xattn_b1': (0.0, 0.483),
     'L0_xattn_g2': (1.0, 0.6),
     'L0_xattn_b2': (0.0, 0.1),
     'L1_xattn_bq': (0.0, 0.421),
     'L1_xattn_bk': (0.0, 0.8),
     'L1_xattn_bv': (0.0, 0.1),
     'L1_xattn_bo': (0.0, 0.1)}
    factors = {'L0_ffn_router_b': 2.934, 'L0_ffn_b1': 8.0}
    for name, (base, spread) in spreads.items():
        noise = np.random.default_rng([zlib.crc32(name.encode()), seed]).standard_normal(out[name].shape)
        drawn = base * np.exp(spread * noise) if base else spread * noise
        out[name] = jnp.asarray(drawn.astype(out[name].dtype))
    for name, factor in factors.items():
        out[name] = (out[name] * factor).astype(out[name].dtype)
    return out
```

```python
import concourse.bass as bass
from concourse import mybir
from contextlib import ExitStack

FP32 = mybir.dt.float32
FP16 = mybir.dt.float16
BF16 = mybir.dt.bfloat16
ALU = mybir.AluOpType
ACT = mybir.ActivationFunctionType
AX = mybir.AxisListType

P = 128
D = 256
DC = D // P
TOK = 2048
NX = TOK // P
CTX = 1601
NCT = -(-CTX // P)
CTXP = NCT * P
CTX_LAST = CTX - (NCT - 1) * P
NPAIR = 8
QB = 512
NU = TOK // QB
HB = 64
EPS = 1e-5
WSCALE = 16.0
MASKED = -1e30
RP = 5
RY = 3
NE, EF = 8, 128
FF = 1024
ROUND = 1.5 * 2.0 ** 23


def wait(eng, sem, value):
    if not isinstance(value, int) or value > 0:
        eng.wait_ge(sem, value)


def split_even(n, parts):
    return [(j + 1) * n // parts - j * n // parts for j in range(parts)]


class Semaphores:

    def __init__(self, nc, tag):
        self.nc, self.tag, self.all = nc, tag, []

    def __call__(self, name):
        self.all.append(self.nc.alloc_semaphore(f"{self.tag}_{name}"))
        return self.all[-1]

    def __enter__(self):
        return self

    def __exit__(self, kind, *rest):
        if kind is None:
            self.nc.clear_and_free_semaphores(self.all)
            self.nc.all_engine_barrier()


class Memory:
    pass


def allocate(nc, ctx):
    m = Memory()

    def sb(name, shape, dt=FP32):
        return ctx.enter_context(nc.sbuf_tensor(name, shape, dt))

    m.x = sb("x_res", [P, NX, D])
    m.xh = sb("xt_hi", [P, DC, TOK], FP16)
    m.xl = sb("xt_lo", [P, DC, TOK], FP16)
    m.ch = sb("ct_hi", [P, DC, CTXP], FP16)
    m.cl = sb("ct_lo", [P, DC, CTXP], FP16)
    m.ident = sb("ident", [P, P])
    m.tg = sb("tanh_gates", [P, 4])
    m.slot = [ctx.enter_context(nc.psum_tensor(f"slot{n}", [P, 1024], FP32)) for n in range(2)]
    m.bank = [ctx.enter_context(nc.psum_tensor(f"bank{n}", [P, 512], FP32)) for n in range(2)]
    m.wide = ctx.enter_context(nc.psum_tensor("wide", [P, 1024], FP32))
    return m


def stage_setup(nc, m, x_in, gates_in):
    with Semaphores(nc, "setup") as sem, ExitStack() as ctx:
        gates = ctx.enter_context(nc.sbuf_tensor("gates_raw", [P, 4], FP32))
        x_in_sem = sem("x_loaded")
        gates_sem = sem("gates_loaded")
        zeroed = sem("identity_zeroed")
        block = ctx.enter_context(nc.Block())

        @block.sync
        def _(sp):
            sp.dma_start(gates[:, :], gates_in[0:1, :].broadcast_to([P, 4])).then_inc(gates_sem, 16)
            sp.dma_start(m.x[:, :, :], x_in.rearrange("(t p) d -> p t d", p=P)).then_inc(x_in_sem, 16)
            sp.wait_ge(x_in_sem, 16)

        @block.gpsimd
        def _(pool):
            nc.gpsimd.memset(m.ident[:, :], 0.0).then_inc(zeroed, 1)
            pool.wait_ge(zeroed, 1)
            nc.gpsimd.affine_select(out=m.ident[:, :], in_=m.ident[:, :], compare_op=ALU.not_equal, fill=1.0,
                                    base=0, pattern=[[-1, P]], channel_multiplier=1)

        @block.scalar
        def _(act):
            act.wait_ge(gates_sem, 16)
            nc.scalar.activation(m.tg[:, :], gates[:, :], ACT.Tanh)


def stage_norm(nc, m, tag, src, nt, hi=None, lo=None, norms=1, affine=None, load=None, rows=None):
    groups = [list(range(a, min(a + 4, nt))) for a in range(0, nt, 4)] if rows is None else []
    with Semaphores(nc, tag) as sem, ExitStack() as ctx:
        def sb(name, shape, dt=FP32):
            return ctx.enter_context(nc.sbuf_tensor(f"{tag}_{name}", shape, dt))

        stats = sb("stats", [P, nt, 6])
        mv = sb("mv", [P, nt, 2])
        std = sb("std", [P, nt])
        rstd = sb("rstd", [P, nt])
        eps = sb("eps", [P, 1])
        xn = sb("xn", [P, nt, D]) if rows is None else rows
        y = sb("y", [P, 2, 512])
        gb = sb("gb", [P, 2, DC])
        loaded, gb_loaded = sem("loaded"), sem("gb_loaded")
        padded, eps_set, stats_done = sem("padded"), sem("eps_set"), sem("stats_done")
        aggregated, std_done, rstd_done, normed = sem("aggregated"), sem("std_done"), sem("rstd_done"), sem("normed")
        turned, y_ready, hi_done, lo_done = sem("turned"), sem("y_ready"), sem("hi_done"), sem("lo_done")
        block = ctx.enter_context(nc.Block())
        n_load = 0
        if load is not None:
            n_load = 1 + (CTX_LAST < P)

        @block.sync
        def _(sp):
            if load is not None:
                full = (nt - 1) * P
                sp.dma_start(src[:, 0:nt - 1, :], load[0:full, :].rearrange("(t p) d -> p t d", p=P)).then_inc(loaded, 16)
                sp.wait_ge(padded, 1)
                sp.dma_start(src[0:CTX_LAST, nt - 1, :], load[full:full + CTX_LAST, :]).then_inc(loaded, 16)
            if affine is not None:
                sp.dma_start(gb[:, :, :], affine).then_inc(gb_loaded, 16)

        @block.vector
        def _(dve):
            nc.vector.memset(eps[:, :], EPS).then_inc(eps_set, 1)
            if load is not None:
                nc.vector.memset(src[:, nt - 1, :], 0.0).then_inc(padded, 1)
                dve.wait_ge(loaded, 16 * n_load)
            for r in range(norms):
                a = src if r == 0 else xn
                if r:
                    dve.wait_ge(normed, nt * r)
                for t in range(nt):
                    nc.vector.bn_stats(stats[:, t, :], a[:, t, :]).then_inc(stats_done, 1)
                for t in range(nt):
                    dve.wait_ge(stats_done, r * nt + t + 1)
                    nc.vector.bn_aggr(mv[:, t, :], stats[:, t, :]).then_inc(aggregated, 1)
                dve.wait_ge(std_done, r + 1)
                nc.vector.reciprocal(rstd[:, :], std[:, :]).then_inc(rstd_done, 1)
                dve.wait_ge(rstd_done, r + 1)
                dve.wait_ge(aggregated, (r + 1) * nt)
                for t in range(nt):
                    nc.vector.tensor_scalar(xn[:, t, :], a[:, t, :], mv[:, t, 0:1], rstd[:, t:t + 1],
                                            ALU.subtract, ALU.mult).then_inc(normed, 1)
            for g, tiles in enumerate(groups):
                w = len(tiles) * P
                for c in range(DC):
                    n = g * DC + c
                    dve.wait_ge(hi_done, n + 1)
                    nc.vector.tensor_tensor(lo[:, c, g * 512:g * 512 + w], y[:, n % 2, 0:w],
                                            hi[:, c, g * 512:g * 512 + w], ALU.subtract).then_inc(lo_done, 1)

        @block.scalar
        def _(act):
            act.wait_ge(eps_set, 1)
            for r in range(norms):
                act.wait_ge(aggregated, (r + 1) * nt)
                nc.scalar.activation(std[:, :], mv[:, :, 1], ACT.Sqrt, bias=eps[:, 0:1]).then_inc(std_done, 1)
            if affine is not None:
                act.wait_ge(gb_loaded, 16)
            for g, tiles in enumerate(groups):
                w = len(tiles) * P
                for c in range(DC):
                    n = g * DC + c
                    act.wait_ge(turned, n + 1)
                    if n >= 2:
                        act.wait_ge(lo_done, n - 1)
                    if affine is None:
                        nc.scalar.activation(y[:, n % 2, 0:w], m.slot[n % 2][:, 0:w], ACT.Copy).then_inc(y_ready, 1)
                    else:
                        nc.scalar.activation(y[:, n % 2, 0:w], m.slot[n % 2][:, 0:w], ACT.Identity,
                                             bias=gb[:, 1, c:c + 1], scale=gb[:, 0, c:c + 1]).then_inc(y_ready, 1)
                    act.wait_ge(y_ready, n + 1)
                    nc.scalar.activation(hi[:, c, g * 512:g * 512 + w], y[:, n % 2, 0:w], ACT.Copy).then_inc(hi_done, 1)

        @block.tensor
        def _(pe):
            for g, tiles in enumerate(groups):
                pe.wait_ge(normed, (norms - 1) * nt + tiles[-1] + 1)
                for c in range(DC):
                    n = g * DC + c
                    if n >= 2:
                        pe.wait_ge(y_ready, n - 1)
                    for j, t in enumerate(tiles):
                        last = nc.tensor.transpose(m.slot[n % 2][:, j * P:(j + 1) * P], xn[:, t, c * P:(c + 1) * P],
                                                   m.ident[:, :])
                    last.then_inc(turned, 1)


class Attention:

    def __init__(self, name, latents, head, q_scale, biased, gate):
        self.name = name
        self.latents = latents
        self.head = head
        self.stacked = head < HB
        self.q_scale = q_scale
        self.biased = biased
        self.gate = gate
        self.nl = NX if latents else 0
        self.nt = self.nl + NCT
        self.keys = self.nt * P
        self.kchunks = [(a, 512, True) for a in range(0, self.nl * P, 512)]
        self.kchunks += [(self.nl * P + a, min(512, CTXP - a), False) for a in range(0, CTXP, 512)]
        self.vgroups = [list(range(a, min(a + 4, self.nt))) for a in range(0, self.nt, 4)]
        self.mchunks = [(a, 512, False) for a in range(0, self.nl * P, 512)]
        self.mchunks += [(a, CTXP // 4, True) for a in range(0, CTXP, CTXP // 4)]
        self.msteps = len(self.mchunks) * (QB // P)
        n = 4 if latents else 2
        self.kparts = [(j * self.nt // n, (j + 1) * self.nt // n) for j in range(n)]
        self.pool_tiles = [t for t in range(self.nt) if t * 17 // 29 != (t + 1) * 17 // 29] if not self.stacked else []
        self.dve_tiles = [t for t in range(self.nt) if t not in self.pool_tiles] if not self.stacked else []
        self.den_after, self.out_after = (2, 6)


def stage_attention(nc, m, a, w_in, wo_in, mask_in, bv_in=None, bo_in=None):
    NT, NL, KEYS = a.nt, a.nl, a.keys
    NK, NV = len(a.kchunks), len(a.vgroups)
    NKQ = NK + NU
    MS = a.msteps
    TILES = NU * NT
    n_pass = 1 if a.stacked else 2
    with Semaphores(nc, a.name) as sem, ExitStack() as ctx:
        def sb(name, shape, dt=FP32):
            return ctx.enter_context(nc.sbuf_tensor(f"{a.name}_{name}", shape, dt))

        nb = 2 if a.biased else 0
        w_st = sb("w_staged", [P, 3 * DC * P + nb])
        w_hi, w_lo = sb("w_hi", [P, 3 * DC * P], FP16), sb("w_lo", [P, 3 * DC * P], FP16)
        w16 = sb("w_scaled", [P, 3 * DC * P])
        wscale = sb("w_scale", [P, 1])

        def weights(half, what, c):
            at = (what * DC + c) * P
            return half[:, at:at + P]

        wo = sb("wo", [P, D])
        y = sb("y", [P, RY, 512])
        kn_hi, kn_lo = sb("kn_hi", [P, KEYS], FP16), sb("kn_lo", [P, KEYS], FP16)
        qn_hi, qn_lo = sb("qn_hi", [P, TOK], FP16), sb("qn_lo", [P, TOK], FP16)
        kmask = sb("k_masked", [P, CTXP], FP16)
        qdiag = sb("q_diag", [P, TOK // HB, 2, HB], FP16)
        part_max = sb("part_max", [P, 8, len(a.mchunks)])
        neg_max = sb("neg_max", [P, 8])
        shift = sb("shift", [8, 2, QB], FP16)
        diag8 = sb("diag8", [8, 8, HB])
        k_op = [[sb(f"k_op{h}{n}", [P, KEYS], FP16) for n in range(n_pass)] for h in range(2)]
        q_op = [[sb(f"q_op{h}{n}", [P, TOK], FP16) for n in range(n_pass)] for h in range(2)]
        val = sb("val", [P, NT, P])
        prob = sb("prob", [P, RP, 2 * QB])
        if not a.stacked:
            acc_v, acc_p = sb("acc_v", [P, 2, 2 * QB]), sb("acc_p", [P, 2, 2 * QB])
            ones = sb("ones", [P, HB])
        rden = sb("rden", [P, QB])
        att = sb("att", [P, QB])
        valid_u8 = sb("valid_u8", [P, CTXP], mybir.dt.uint8)
        valid = sb("valid", [P, CTXP], FP16)
        mcol_u8 = sb("mcol_u8", [P, NCT], mybir.dt.uint8)
        mbias = sb("mask_bias", [P, NT])
        if a.biased:
            qk_bias, bscale = sb("qk_bias", [P, 2]), sb("bias_scale", [P, 2])
            bv = sb("bv", [P, NPAIR, P])
            bo = sb("bo", [P, D])
            bos = sb("bo_gated", [P, D])

        w_loaded, w_split, wo_loaded = sem("w_loaded"), sem("w_split"), sem("wo_loaded")
        split16, wscale_set = sem("w_scaled"), sem("wscale_set")
        mask_loaded, bias_loaded = sem("mask_loaded"), sem("bias_loaded")
        zeros_set, prep = sem("zeros_set"), sem("prep")
        proj_done, proj_read = sem("proj_done"), sem("proj_read")
        y_used, y_hi = sem("y_used"), sem("y_hi")
        next_ready, kmask_part = sem("next_ready"), sem("kmask_part")
        k_laid = [sem(f"k_laid{c}") for c in range(len(a.kparts))]
        q_laid = [sem(f"q_laid{u}") for u in range(NU)]
        scores_ready, probs_ready, av_done = sem("scores_ready"), sem("probs_ready"), sem("av_done")
        added_v, added_p = sem("added_v"), sem("added_p")
        den_ready, den_used = sem("den_ready"), sem("den_used")
        att_ready, out_ready, out_used = sem("att_ready"), sem("out_ready"), sem("out_used")
        max_ready, max_used = sem("max_ready"), sem("max_used")
        neg_ready, neg_turned, shift_ready = sem("neg_ready"), sem("neg_turned"), sem("shift_ready")
        block = ctx.enter_context(nc.Block())


        def summed(tiles, i, u, n):
            return (i * NU + u) * (len(tiles) - 1) + n

        n_den = 0 if a.stacked else 1
        slots = []
        for u in range(NU):
            for t in range(NT):
                slots.append(("scores", u, t))
                if u and t == a.den_after and n_den:
                    slots.append(("den", u - 1, 0))
                if u and t == a.out_after:
                    slots.append(("out", u - 1, 0))
        if n_den:
            slots.append(("den", NU - 1, 0))
        slots.append(("out", NU - 1, 0))
        places = split_even(MS, NT)
        TURN = 4

        def bank_of(n):
            return m.slot[(n // 2) % 2][:, (n % 2) * 512:(n % 2) * 512 + 512]

        def consumed(k, i):
            kind, u, t = slots[k]
            if kind == "scores":
                return probs_ready, i * TILES + u * NT + t + 1
            if kind == "den":
                return den_used, i * NU + u + 1
            return out_used, i * NU + u + 2

        def groups_before(it):
            return it * NKQ + (it - 1) * NV if not isinstance(it, int) or it else 0

        def y_before(it):
            return groups_before(it) if a.biased else it * NKQ

        @block.sync
        def _(sp):
            sp.dma_start(w_st[:, :], w_in[0, :, :]).then_inc(w_loaded, 16)
            sp.dma_start(valid_u8[:, :], mask_in[0][0:1, :].broadcast_to([P, CTXP])).then_inc(mask_loaded, 16)
            sp.dma_start(mcol_u8[:, :], mask_in[1]).then_inc(mask_loaded, 16)
            if a.biased:
                sp.dma_start(bv[:, :, :].rearrange("p n c -> p (n c)"), bv_in[0:1, :].broadcast_to([P, NPAIR * P])).then_inc(bias_loaded, 16)
                sp.dma_start(bo[:, :], bo_in[0:1, :].broadcast_to([P, D])).then_inc(bias_loaded, 16)
            sp.wait_ge(zeros_set, 1)

            def lay_q(u, i, it):
                sp.wait_ge(shift_ready, u + 1 if it is None else it * NU + u + 1)
                c = slice(u * QB, (u + 1) * QB)
                for h in range(2):
                    r = slice(h * HB, h * HB + a.head)
                    if a.stacked:
                        parts = [(q_op[h][0][0:a.head, c], qn_hi[r, c]),
                                 (q_op[h][0][a.head:2 * a.head, c], qn_lo[r, c]),
                                 (q_op[h][0][2 * a.head:3 * a.head, c], qn_hi[r, c]),
                                 (q_op[h][0][HB:HB + 8, c], shift[:, h, :])]
                    else:
                        parts = [(q_op[h][0][0:HB, c], qn_hi[r, c]), (q_op[h][0][HB:P, c], qn_lo[r, c]),
                                 (q_op[h][1][0:HB, c], qn_hi[r, c]), (q_op[h][1][HB:HB + 8, c], shift[:, h, :])]
                    for dst, src in parts:
                        sp.dma_start(dst, src).then_inc(q_laid[u], 16)

            def lay_k(n, i, it):
                lo, hi = a.kparts[n]
                wait(sp, scores_ready, i * TILES + (NU - 1) * NT + hi if it is not None else 0)
                c = slice(lo * P, hi * P)
                for h in range(2):
                    r = slice(h * HB, h * HB + a.head)
                    if a.stacked:
                        parts = [(k_op[h][0][0:a.head, c], kn_hi[r, c]),
                                 (k_op[h][0][a.head:2 * a.head, c], kn_hi[r, c]),
                                 (k_op[h][0][2 * a.head:3 * a.head, c], kn_lo[r, c])]
                    else:
                        parts = [(k_op[h][0][0:HB, c], kn_hi[r, c]), (k_op[h][0][HB:P, c], kn_hi[r, c]),
                                 (k_op[h][1][0:HB, c], kn_lo[r, c])]
                    for dst, src in parts:
                        sp.dma_start(dst, src).then_inc(k_laid[n], 16)

            def pair(i, first=False, last=False):
                it = None if first else i + 1
                if not first:
                    sp.wait_ge(proj_done, groups_before(i + 1) + 1)
                    sp.wait_ge(zeros_set, 1)
                    sp.dma_start(wo[:, :], wo_in[i, :, :]).then_inc(wo_loaded, 16)
                if last:
                    return
                sp.wait_ge(w_split, 1 if first else i + 2)
                sp.wait_ge(zeros_set, 1)
                sp.dma_start(w_st[:, :], w_in[1 if first else i + 2, :, :]).then_inc(w_loaded, 16)
                sp.wait_ge(next_ready, 1 if first else i + 2)
                if first:
                    for n in range(len(a.kparts)):
                        lay_k(n, 0, None)
                    for u in range(NU):
                        lay_q(u, 0, None)
                else:
                    for u in range(NU - 1):
                        lay_q(u, i, it)
                    for n in range(len(a.kparts)):
                        lay_k(n, i, it)
                    lay_q(NU - 1, i, it)

            pair(0, first=True)
            with sp.Fori(0, NPAIR - 1) as i:
                pair(i)
            pair(NPAIR - 1, last=True)

        @block.gpsimd
        def _(pool):
            def split(n):
                scale = wscale[:, 0:1].broadcast_to([P, 3 * DC * P])
                pool.wait_ge(w_loaded, n * 16 + 16)
                nc.gpsimd.tensor_tensor(w_hi[:, :], w_st[:, 0:3 * DC * P], scale, ALU.mult)
                if a.biased:
                    nc.gpsimd.tensor_tensor(qk_bias[:, :], w_st[:, 3 * DC * P:], bscale[:, :], ALU.mult)
                nc.gpsimd.tensor_tensor(w16[:, :], w_st[:, 0:3 * DC * P], scale, ALU.mult).then_inc(split16, 1)
                pool.wait_ge(split16, n + 1)
                nc.gpsimd.tensor_tensor(w_lo[:, :], w16[:, :], w_hi[:, :], ALU.subtract).then_inc(w_split, 1)

            def pair(i, last=False):
                for u in range(NU):
                    if u == 0 and not last:
                        pool.wait_ge(proj_read, groups_before(i + 2))
                        split(i + 2)
                    for n, t in enumerate(a.pool_tiles[1:]):
                        k = u * NT + t
                        if n == 0 and u >= 2:
                            pool.wait_ge(den_ready, i * NU + u - 1)
                        pool.wait_ge(probs_ready, i * TILES + k + 1)
                        if n == 0:
                            before = prob[:, (u * NT + a.pool_tiles[0]) % RP, :]
                        else:
                            before = acc_p[:, u % 2, :]
                            pool.wait_ge(added_p, summed(a.pool_tiles, i, u, n))
                        nc.gpsimd.tensor_tensor(acc_p[:, u % 2, :], before, prob[:, k % RP, :], ALU.add).then_inc(added_p, 1)

            nc.gpsimd.memset(wscale[:, :], WSCALE)
            if a.biased:
                nc.gpsimd.memset(bscale[:, 1:2], 1.0)
                nc.gpsimd.memset(bscale[:, 0:1], a.q_scale)
            nc.gpsimd.memset(w16[:, 0:1], 0.0).then_inc(wscale_set, 1)
            pool.wait_ge(wscale_set, 1)
            split(0)
            pool.wait_ge(proj_read, NKQ)
            split(1)
            with pool.Fori(0, NPAIR - 1) as i:
                pair(i)
            if a.pool_tiles:
                pair(NPAIR - 1, last=True)

        @block.scalar
        def _(act):
            def project(it, kq, values):
                g0, y0 = groups_before(it), y_before(it)
                n = 0
                if kq:
                    for j in range(NKQ):
                        w = a.kchunks[j][1] if j < NK else QB
                        act.wait_ge(proj_done, g0 + n + 1)
                        wait(act, y_used, y0 + n - RY + 1)
                        src = bank_of(n)[:, 0:w]
                        scale = (1.0 if j < NK else a.q_scale) / WSCALE
                        if a.biased:
                            b = qk_bias[:, 1:2] if j < NK else qk_bias[:, 0:1]
                            nc.scalar.activation(y[:, n % RY, 0:w], src, ACT.Identity, bias=b, scale=scale).then_inc(proj_read, 1)
                        else:
                            nc.scalar.activation(y[:, n % RY, 0:w], src, ACT.Copy, scale=scale).then_inc(proj_read, 1)
                        n += 1
                if values:
                    for tiles in a.vgroups:
                        w = len(tiles) * P
                        act.wait_ge(proj_done, g0 + n + 1)
                        src = bank_of(n)[:, 0:w]
                        if a.biased:
                            wait(act, y_used, y0 + n - RY + 1)
                            nc.scalar.activation(y[:, n % RY, 0:w], src, ACT.Copy, scale=1.0 / WSCALE).then_inc(proj_read, 1)
                        else:
                            dst = val[:, tiles[0]:tiles[-1] + 1, :].rearrange("p t c -> p (t c)")
                            nc.scalar.activation(dst, src, ACT.Copy, scale=1.0 / WSCALE).then_inc(proj_read, 1)
                        n += 1

            def pair(i, last=False):
                project(i + 1, not last, True)
                for u in range(NU):
                    for t in range(NT):
                        k = u * NT + t
                        act.wait_ge(scores_ready, i * TILES + k + 1)
                        if k >= RP:
                            o = k - RP
                            act.wait_ge(av_done, i * TILES + o + 1)
                            for tiles, added in ((a.pool_tiles, added_p), (a.dve_tiles, added_v)):
                                if o % NT in tiles:
                                    act.wait_ge(added, summed(tiles, i, o // NT, max(tiles.index(o % NT), 1)))
                        slot = slots.index(("scores", u, t))
                        nc.scalar.activation(prob[:, k % RP, :], m.slot[slot % 2][:, :], ACT.Exp,
                                             bias=mbias[:, t:t + 1]).then_inc(probs_ready, 1)

            act.wait_ge(prep, 1)
            project(0, True, False)
            with act.Fori(0, NPAIR - 1) as i:
                pair(i)
            pair(NPAIR - 1, last=True)

        @block.vector
        def _(dve):
            chain = [0]
            link_sem = sem("dve_chain")

            def link(ins):
                chain[0] += 1
                ins.then_inc(link_sem, 1)
                dve.wait_ge(link_sem, chain[0])

            nc.vector.memset(mbias[:, :], 0.0)
            nc.vector.memset(qdiag[:, :, :, :], 0.0)
            nc.vector.memset(att[:, :], 0.0)
            if not a.stacked:
                nc.vector.memset(ones[:, :], 1.0)
            for h in range(2):
                for op, v in ((k_op, 1.0), (q_op, 0.0)):
                    t = op[h][-1]
                    lo = 0 if a.stacked else HB
                    link(nc.vector.memset(t[lo:P, :], 0.0))
                    link(nc.vector.memset(t[HB:HB + 8, :], v))
            nc.vector.memset(rden[:, :], 0.0).then_inc(zeros_set, 1)
            link(nc.vector.tensor_copy(diag8[:, :, :], m.ident[0:8, 0:8].rearrange("p (j o) -> p j o", o=1).broadcast_to([8, 8, HB])))
            dve.wait_ge(mask_loaded, 32)
            nc.vector.tensor_copy(valid[:, :], valid_u8[:, :])
            link(nc.vector.tensor_scalar(mbias[:, NL:NT], mcol_u8[:, :], -1.0, -MASKED, ALU.add, ALU.mult))
            if a.biased:
                dve.wait_ge(bias_loaded, 32)
                ones_cols = bv[:, :, :].rearrange("p n (h c) -> p (n h) c", c=HB)[:, :, 32:32 + a.head]
                link(nc.vector.memset(ones_cols, 1.0))
                link(nc.vector.tensor_scalar(bos[:, :], bo[:, :], m.tg[:, a.gate:a.gate + 1], None, ALU.mult))
                for t in range(NX):
                    ins = nc.vector.tensor_tensor(m.x[:, t, :], m.x[:, t, :], bos[:, :], ALU.add)
                link(ins)
            nc.vector.memset(rden[:, :], 0.0).then_inc(prep, 1)
            nc.vector.memset(att[:, :], 0.0).then_inc(out_used, 1)

            def project(it, kq, values, pair_v):
                g0, y0 = groups_before(it), y_before(it)
                n = 0
                if kq:
                    for c in range(len(a.kparts)):
                        wait(dve, k_laid[c], it * 16 * 6)
                    for u in range(NU):
                        wait(dve, q_laid[u], it * 16 * 8)
                    for j in range(NKQ):
                        key = j < NK
                        c0, w = a.kchunks[j][:2] if key else ((j - NK) * QB, QB)
                        hi, lo = (kn_hi, kn_lo) if key else (qn_hi, qn_lo)
                        dve.wait_ge(proj_read, g0 + n + 1)
                        nc.vector.tensor_copy(hi[:, c0:c0 + w], y[:, n % RY, 0:w]).then_inc(y_hi, 1)
                        dve.wait_ge(y_hi, it * NKQ + j + 1)
                        nc.vector.tensor_tensor(lo[:, c0:c0 + w], y[:, n % RY, 0:w], hi[:, c0:c0 + w], ALU.subtract).then_inc(y_used, 1)
                        if key and not a.kchunks[j][2]:
                            b0 = c0 - NL * P
                            km = kmask[:, b0:b0 + w]
                            nc.vector.scalar_tensor_tensor(km, hi[:, c0:c0 + w], k0[:, 0:1], valid[:, b0:b0 + w],
                                                           ALU.subtract, ALU.mult).then_inc(kmask_part, 1)
                            dve.wait_ge(kmask_part, it * (NK - NL // 4) + (j - NL // 4) + 1)
                            nc.vector.tensor_scalar(km, km, k0[:, 0:1], None, ALU.add)
                        if not key:
                            for h in range(2):
                                r = slice(h * HB, h * HB + HB)
                                b = c0 // HB
                                ins = nc.vector.tensor_copy(qdiag[r, b:b + QB // HB, h, :],
                                                            hi[r, c0:c0 + w].rearrange("p (b q) -> p b q", q=HB))
                        n += 1
                    ins.then_inc(next_ready, 1)
                if values and a.biased:
                    for tiles in a.vgroups:
                        w = len(tiles)
                        dve.wait_ge(proj_read, g0 + n + 1)
                        row = bv[:, pair_v:pair_v + 1, :] if isinstance(pair_v, int) else bv[:, bass.ds(pair_v, 1), :]
                        nc.vector.tensor_tensor(val[:, tiles[0]:tiles[-1] + 1, :],
                                                y[:, n % RY, 0:w * P].rearrange("p (t c) -> p t c", c=P),
                                                row.broadcast_to([P, w, P]), ALU.add).then_inc(y_used, 1)
                        n += 1

            def max_step(it, u, s):
                c, jp = s // (QB // P), s % (QB // P)
                w = a.mchunks[c][1]
                if s == 0:
                    wait(dve, neg_ready, it * NU + u)
                dve.wait_ge(max_ready, it * NU * MS + u * MS + s + 1)
                nc.vector.reduce_max(part_max[:, 2 * jp:2 * jp + 2, c],
                                     m.wide[:, :].rearrange("p (a b) -> p a b", a=2)[:, :, 0:w], AX.X).then_inc(max_used, 1)

            def max_of_unit(it, u):
                dve.wait_ge(max_used, it * NU * MS + (u + 1) * MS)
                nc.vector.tensor_reduce(neg_max[:, :], part_max[:, :, :], AX.X, ALU.max, negate=True).then_inc(neg_ready, 1)

            def shift_of_unit(it, u):
                dve.wait_ge(neg_turned, it * NU + u + 1)
                if u:
                    dve.wait_ge(q_laid[u - 1], (it + 1) * 16 * 8)
                rows = m.wide[0:8, 0:2 * HB].rearrange("j (h o q) -> j h o q", h=2, o=1).broadcast_to([8, 2, 8, HB])
                mask = diag8[:, :, :].rearrange("j (o k) q -> j o k q", o=1).broadcast_to([8, 2, 8, HB])
                for h in range(2):
                    ins = nc.vector.tensor_tensor(shift[:, h, :].rearrange("j (k q) -> j k q", q=HB), rows[:, h], mask[:, h], ALU.mult)
                ins.then_inc(shift_ready, 1)

            def add(i, u, t):
                if t not in a.dve_tiles[1:]:
                    return
                n, k = a.dve_tiles.index(t) - 1, u * NT + t
                if n == 0 and u >= 2:
                    dve.wait_ge(den_ready, i * NU + u - 1)
                dve.wait_ge(probs_ready, i * TILES + k + 1)
                if n == 0:
                    before = prob[:, (u * NT + a.dve_tiles[0]) % RP, :]
                else:
                    before = acc_v[:, u % 2, :]
                    dve.wait_ge(added_v, summed(a.dve_tiles, i, u, n))
                nc.vector.tensor_tensor(acc_v[:, u % 2, :], before, prob[:, k % RP, :], ALU.add).then_inc(added_v, 1)

            def normalise(i, u):
                if a.stacked:
                    dve.wait_ge(av_done, i * TILES + (u + 1) * NT)
                    for h in range(2):
                        ins = nc.vector.reciprocal(rden[h * HB:h * HB + a.head, :], m.bank[u % 2][h * HB + 32:h * HB + 32 + a.head, :])
                    ins.then_inc(den_used, 1)
                    dve.wait_ge(den_used, i * NU + u + 1)
                    for h in range(2):
                        r = slice(h * HB, h * HB + a.head)
                        ins = nc.vector.tensor_tensor(att[r, :], m.bank[u % 2][r, :], rden[r, :], ALU.mult)
                    ins.then_inc(att_ready, 1)
                else:
                    dve.wait_ge(den_ready, i * NU + u + 1)
                    nc.vector.reciprocal(rden[:, :], m.slot[slots.index(("den", u, 0)) % 2][:, 0:QB]).then_inc(den_used, 1)
                    dve.wait_ge(den_used, i * NU + u + 1)
                    dve.wait_ge(av_done, i * TILES + (u + 1) * NT)
                    nc.vector.tensor_tensor(att[:, :], m.bank[u % 2][:, :], rden[:, :], ALU.mult).then_inc(att_ready, 1)

            def residual(i, u):
                dve.wait_ge(out_ready, i * NU + u + 1)
                dve.wait_ge(out_used, i * NU + u + 1)
                xs = m.x[:, 4 * u:4 * u + 4, :].rearrange("p t d -> p (t d)")
                nc.vector.scalar_tensor_tensor(xs, m.slot[slots.index(("out", u, 0)) % 2][:, :], m.tg[:, a.gate:a.gate + 1], xs,
                                               ALU.mult, ALU.add).then_inc(out_used, 1)

            def pair(i, last=False):
                project(i + 1, not last, True, i)
                for u in range(NU):
                    s = 0
                    for t in range(NT):
                        if u and t == a.den_after + 1:
                            normalise(i, u - 1)
                        if u and t == a.out_after + 1:
                            residual(i, u - 1)
                        if not last:
                            for _ in range(places[t]):
                                max_step(i + 1, u, s)
                                s += 1
                            if u and t == TURN:
                                shift_of_unit(i + 1, u - 1)
                        if t:
                            add(i, u, t - 1)
                        elif u:
                            add(i, u - 1, NT - 1)
                    if not last:
                        max_of_unit(i + 1, u)
                add(i, NU - 1, NT - 1)
                normalise(i, NU - 1)
                if not last:
                    shift_of_unit(i + 1, NU - 1)
                residual(i, NU - 1)

            k0 = kn_hi
            project(0, True, False, 0)
            for u in range(NU):
                for s in range(MS):
                    max_step(0, u, s)
                max_of_unit(0, u)
                shift_of_unit(0, u)
            with dve.Fori(0, NPAIR - 1) as i:
                pair(i)
            pair(NPAIR - 1, last=True)

        @block.tensor
        def _(pe):
            def project(it, kq, values):
                g0 = groups_before(it)
                n = 0
                pe.wait_ge(w_split, it + 1)
                if kq:
                    for j in range(NKQ):
                        key = j < NK
                        c0, w, tokens = a.kchunks[j] if key else ((j - NK) * QB, QB, True)
                        src = (m.xh, m.xl) if tokens else (m.ch, m.cl)
                        c1 = c0 if tokens else c0 - NL * P
                        wait(pe, proj_read, g0 + n - 3 if n >= 4 else 0)
                        what = 1 if key else 0
                        steps = [(w_hi, 0), (w_hi, 1), (w_lo, 0)]
                        for q, (wt, half) in enumerate(steps):
                            for c in range(DC):
                                ins = nc.tensor.matmul(bank_of(n)[:, 0:w], weights(wt, what, c), src[half][:, c, c1:c1 + w],
                                                       start=(q == 0 and c == 0), stop=(q == 2 and c == DC - 1))
                        ins.then_inc(proj_done, 1)
                        n += 1
                if values:
                    for tiles in a.vgroups:
                        wait(pe, proj_read, g0 + n - 3 if n >= 4 else 0)
                        for z, t in enumerate(tiles):
                            src = (m.xh, m.xl) if t < NL else (m.ch, m.cl)
                            c1 = (t if t < NL else t - NL) * P
                            for q, (wt, half) in enumerate([(w_hi, 0), (w_hi, 1), (w_lo, 0)]):
                                for c in range(DC):
                                    ins = nc.tensor.matmul(bank_of(n)[:, z * P:(z + 1) * P], src[half][:, c, c1:c1 + P], weights(wt, 2, c),
                                                           start=(q == 0 and c == 0), stop=(q == 2 and c == DC - 1))
                        ins.then_inc(proj_done, 1)
                        n += 1
                return n

            max_before = [None]

            def max_step(it, u, s):
                c, jp = s // (QB // P), s % (QB // P)
                first, w, masked = a.mchunks[c]
                if u == 0 and s == 0:
                    pe.wait_ge(next_ready, it + 1)
                wait(pe, *wide_free(it, u, s))
                src = (kmask if masked else kn_hi)[:, first:first + w]
                for z in range(2):
                    b = u * (QB // HB) + 2 * jp + z
                    ins = nc.tensor.matmul(m.wide[:, z * 512:z * 512 + w], qdiag[:, b, :, :].rearrange("p h q -> p (h q)"), src,
                                           start=True, stop=True)
                ins.then_inc(max_ready, 1)
                max_before[0] = (max_used, u * MS + s + 1)

            def wide_free(it, u, s):
                held = max_before[0]
                if held is None:
                    return shift_ready, it * NU
                sem_, n = held
                return sem_, it * (NU * MS if sem_ is max_used else NU) + n

            def turn(it, u):
                pe.wait_ge(neg_ready, it * NU + u + 1)
                wait(pe, *wide_free(it, u, 0))
                nc.tensor.transpose(m.wide[0:8, 0:P], neg_max[:, :], m.ident[:, :]).then_inc(neg_turned, 1)
                max_before[0] = (shift_ready, u + 1)

            def free_slot(i, k, groups):
                if k >= 2:
                    pe.wait_ge(*consumed(k - 2, i))
                elif k == 0:
                    pe.wait_ge(proj_read, groups)

            def scores(i, u, t, k, groups):
                if t == 0:
                    pe.wait_ge(q_laid[u], (i + 1) * 16 * 8)
                for n, (lo, _) in enumerate(a.kparts):
                    if u == 0 and t == lo:
                        pe.wait_ge(k_laid[n], (i + 1) * 16 * 6)
                free_slot(i, k, groups)
                for h in range(2):
                    for n in range(n_pass):
                        ins = nc.tensor.matmul(m.slot[k % 2][:, h * QB:(h + 1) * QB], k_op[h][n][:, t * P:(t + 1) * P],
                                               q_op[h][n][:, u * QB:(u + 1) * QB], start=(n == 0), stop=(n == n_pass - 1))
                ins.then_inc(scores_ready, 1)

            def values(i, u, t, groups):
                k = u * NT + t
                if t == 0 and u >= 2:
                    pe.wait_ge(att_ready, i * NU + u - 1)
                if k == 0:
                    if a.biased:
                        pe.wait_ge(y_used, groups)
                pe.wait_ge(probs_ready, i * TILES + k + 1)
                for h in range(2):
                    ins = nc.tensor.matmul(m.bank[u % 2][h * HB:(h + 1) * HB, :], val[:, t, h * HB:(h + 1) * HB],
                                           prob[:, k % RP, h * QB:(h + 1) * QB], start=(t == 0), stop=(t == NT - 1))
                ins.then_inc(av_done, 1)

            def sums(i, u, k):
                free_slot(i, k, 0)
                pe.wait_ge(added_v, summed(a.dve_tiles, i, u + 1, 0))
                pe.wait_ge(added_p, summed(a.pool_tiles, i, u + 1, 0))
                for h in range(2):
                    for n, acc in enumerate((acc_v, acc_p)):
                        ins = nc.tensor.matmul(m.slot[k % 2][h * HB:(h + 1) * HB, 0:QB], ones[:, :], acc[:, u % 2, h * QB:(h + 1) * QB],
                                               start=(n == 0), stop=(n == 1))
                ins.then_inc(den_ready, 1)

            def outputs(i, u, k):
                free_slot(i, k, 0)
                if u == 0:
                    pe.wait_ge(wo_loaded, i * 16 + 16)
                pe.wait_ge(att_ready, i * NU + u + 1)
                for j in range(QB // P):
                    ins = nc.tensor.matmul(m.slot[k % 2][:, j * D:(j + 1) * D], att[:, j * P:(j + 1) * P], wo[:, :], start=True, stop=True)
                ins.then_inc(out_ready, 1)

            def pair(i, last=False):
                max_before[0] = None
                pe.wait_ge(out_used, i * NU + 1)
                project(i + 1, not last, True)
                groups = groups_before(i + 1) + (0 if last else NKQ) + NV
                k = 0
                for u in range(NU):
                    s = 0
                    for t in range(NT):
                        scores(i, u, t, k, groups)
                        k += 1
                        if not last and places[t]:
                            max_step(i + 1, u, s)
                            s += 1
                        if t:
                            values(i, u, t - 1, groups)
                        elif u:
                            values(i, u - 1, NT - 1, groups)
                        for _ in range(places[t] - 1 if not last else 0):
                            max_step(i + 1, u, s)
                            s += 1
                        if u and t == a.den_after and n_den:
                            sums(i, u - 1, k)
                            k += 1
                        if u and t == a.out_after:
                            outputs(i, u - 1, k)
                            k += 1
                        if u and t == TURN and not last:
                            turn(i + 1, u - 1)
                values(i, NU - 1, NT - 1, groups)
                if n_den:
                    sums(i, NU - 1, k)
                    k += 1
                if not last:
                    turn(i + 1, NU - 1)
                outputs(i, NU - 1, k)

            project(0, True, False)
            for u in range(NU):
                for s in range(MS):
                    max_step(0, u, s)
                turn(0, u)
            with pe.Fori(0, NPAIR - 1) as i:
                pair(i)
            pair(NPAIR - 1, last=True)


def stage_experts(nc, m, gate, rw_in, rb_in, w1_in, b1_in, w2_in, b2_in):
    NB = TOK // QB
    STEPS = NB * NE
    with Semaphores(nc, "moe") as sem, ExitStack() as ctx:
        def sb(name, shape, dt=FP32):
            return ctx.enter_context(nc.sbuf_tensor(f"moe_{name}", shape, dt))

        rw, rw_h, rw_l = sb("rw", [P, DC, NE]), sb("rw_hi", [P, DC, NE], FP16), sb("rw_lo", [P, DC, NE], FP16)
        w1, w1_h, w1_l = sb("w1", [P, DC, NE, EF]), sb("w1_hi", [P, DC, NE, EF], FP16), sb("w1_lo", [P, DC, NE, EF], FP16)
        w2, w2_h, w2_l = sb("w2", [P, NE, D]), sb("w2_hi", [P, NE, D], FP16), sb("w2_lo", [P, NE, D], FP16)
        b1 = sb("b1", [P, NE])
        b2, b2_h, b2_l = sb("b2", [P, D]), sb("b2_hi", [P, D], FP16), sb("b2_lo", [P, D], FP16)
        rb = sb("rb", [P, NE])
        lg, top = sb("logits", [P, NX, NE]), sb("top", [P, NX, 8])
        best, total, pair_sum = sb("best", [P, NX]), sb("total", [P, NX]), sb("pair_sum", [P, NX])
        left = sb("left", [P, NX, NE])
        wt = sb("weights", [P, NX, P])
        wt_h, wt_l = sb("wt_hi", [P, TOK], FP16), sb("wt_lo", [P, TOK], FP16)
        pick = sb("pick", [P, NE, P], FP16)
        h = sb("hidden", [P, 2, QB])
        y, y_h, y_l = sb("y", [P, 2, QB]), sb("y_hi", [P, 2, QB], FP16), sb("y_lo", [P, 2, QB], FP16)
        tgs = sb("gate_scaled", [P, 1])
        loaded, zeroed, w_hi_done, w_ready = sem("loaded"), sem("zeroed"), sem("w_hi_done"), sem("w_ready")
        routed, exp_done, dvec = sem("routed"), sem("exp_done"), sem("dve_chain")
        wt_turned, wt_read, wt_ready = sem("wt_turned"), sem("wt_read"), sem("wt_ready")
        shifted = sem("logits_shifted")
        weights_done = sem("weights_done")
        h_ready, h_done, spread_ready = sem("h_ready"), sem("h_done"), sem("spread_ready")
        y_done, yh_done, yl_done = sem("y_done"), sem("yh_done"), sem("yl_done")
        step_used, out_used = sem("step_used"), sem("out_used")
        block = ctx.enter_context(nc.Block())
        hbank = lambda n: m.slot[0][:, (n % 2) * 512:(n % 2) * 512 + 512]
        sbank = lambda n: m.slot[1][:, (n % 2) * 512:(n % 2) * 512 + 512]
        obank = lambda b, z: m.wide[:, z * 512:z * 512 + 512] if b % 2 == 0 else m.bank[z][:, :]
        splits = [(rw, rw_h, rw_l, WSCALE), (b2, b2_h, b2_l, WSCALE), (w1, w1_h, w1_l, WSCALE), (w2, w2_h, w2_l, WSCALE)]

        def flat(t):
            return t[:] if len(t.shape) == 2 else t[:].rearrange("p a b -> p (a b)") if len(t.shape) == 3 else t[:].rearrange("p a b c -> p (a b c)")

        @block.sync
        def _(sp):
            sp.wait_ge(zeroed, 1)
            sp.dma_start(rw[:, :, :], rw_in.rearrange("(c p) e -> p c e", p=P)).then_inc(loaded, 16)
            sp.dma_start(b2[0:NE, :], b2_in).then_inc(loaded, 16)
            sp.dma_start(b1[:, :], b1_in).then_inc(loaded, 16)
            sp.dma_start(rb[:, :], rb_in[0:1, :].broadcast_to([P, NE])).then_inc(loaded, 16)
            for c in range(DC):
                sp.dma_start(w1[:, c, :, :], w1_in[:, c * P:(c + 1) * P, :].rearrange("e p f -> p e f")).then_inc(loaded, 16)
            sp.dma_start(w2[:, :, :], w2_in.rearrange("e f d -> f e d")).then_inc(loaded, 16)

        @block.gpsimd
        def _(pool):
            for n, (w, hi, lo, _) in enumerate(splits):
                pool.wait_ge(w_hi_done, 2 * n + 2)
                nc.gpsimd.tensor_tensor(flat(lo), flat(w), flat(hi), ALU.subtract).then_inc(w_ready, 1)

        @block.scalar
        def _(act):
            act.wait_ge(loaded, 16 * 7)
            for n, (w, hi, lo, s) in enumerate(splits):
                nc.scalar.activation(flat(w), flat(w), ACT.Copy, scale=s).then_inc(w_hi_done, 1)
                act.wait_ge(w_hi_done, 2 * n + 1)
                nc.scalar.activation(flat(hi), flat(w), ACT.Copy).then_inc(w_hi_done, 1)
            act.wait_ge(shifted, 1)
            nc.scalar.activation(flat(lg), flat(lg), ACT.Exp).then_inc(exp_done, 1)
            for g in range(NB):
                act.wait_ge(wt_turned, g + 1)
                nc.scalar.activation(wt_h[:, g * QB:(g + 1) * QB], sbank(g), ACT.Copy).then_inc(wt_read, 1)
            for n in range(STEPS):
                e = n % NE
                act.wait_ge(h_ready, n + 1)
                if n >= 2:
                    act.wait_ge(y_done, n - 1)
                nc.scalar.activation(h[:, n % 2, :], hbank(n), ACT.Gelu, bias=b1[:, e:e + 1], scale=1.0 / WSCALE).then_inc(h_done, 1)
                act.wait_ge(y_done, n + 1)
                if n >= 2:
                    act.wait_ge(step_used, n - 1)
                nc.scalar.activation(y_h[:, n % 2, :], y[:, n % 2, :], ACT.Copy).then_inc(yh_done, 1)

        @block.vector
        def _(dve):
            chain = [0]

            def link(ins):
                chain[0] += 1
                ins.then_inc(dvec, 1)
                dve.wait_ge(dvec, chain[0])

            nc.vector.memset(b2[:, :], 0.0).then_inc(zeroed, 1)
            nc.vector.memset(wt[:, :, :], 0.0)
            for e in range(NE):
                nc.vector.tensor_copy(pick[:, e, :], m.ident[:, e:e + 1].broadcast_to([P, P]))
            link(nc.vector.tensor_scalar(tgs[:, :], m.tg[:, gate:gate + 1], 1.0 / WSCALE, None, ALU.mult))
            dve.wait_ge(loaded, 16 * 7)
            dve.wait_ge(routed, 1)
            logits = hbank(0)[:, 0:NX * NE].rearrange("p (t e) -> p t e", e=NE)
            rbb = rb[:, :].rearrange("p (o e) -> p o e", o=1).broadcast_to([P, NX, NE])
            link(nc.vector.scalar_tensor_tensor(lg[:, :, :], logits, 1.0 / WSCALE, rbb, ALU.mult, ALU.add))
            link(nc.vector.reduce_max(best[:, :], lg[:, :, :], AX.X))
            col = lambda t: t[:, :].rearrange("p (t o) -> p t o", o=1).broadcast_to([P, NX, NE])
            nc.vector.tensor_tensor(lg[:, :, :], lg[:, :, :], col(best), ALU.subtract).then_inc(shifted, 1)
            dve.wait_ge(exp_done, 1)
            link(nc.vector.reduce_sum(total[:, :], lg[:, :, :], AX.X))
            link(nc.vector.reciprocal(total[:, :], total[:, :]))
            link(nc.vector.tensor_tensor(lg[:, :, :], lg[:, :, :], col(total), ALU.mult))
            for t in range(NX):
                ins = nc.vector.max(top[:, t, :], lg[:, t, :])
            link(ins)
            link(nc.vector.tensor_tensor(pair_sum[:, :], top[:, :, 0], top[:, :, 1], ALU.add))
            link(nc.vector.reciprocal(pair_sum[:, :], pair_sum[:, :]))
            link(nc.vector.memset(top[:, :, 2:8], -1.0))
            for t in range(NX):
                ins = nc.vector.match_replace(left[:, t, :], top[:, t, :], lg[:, t, :], -2.0)
            link(ins)
            link(nc.vector.tensor_scalar(left[:, :, :], left[:, :, :], -1.5, None, ALU.is_lt))
            link(nc.vector.tensor_tensor(left[:, :, :], left[:, :, :], lg[:, :, :], ALU.mult))
            nc.vector.tensor_tensor(wt[:, :, 0:NE], left[:, :, :], col(pair_sum), ALU.mult).then_inc(weights_done, 1)
            for g in range(NB):
                dve.wait_ge(wt_read, g + 1)
                nc.vector.tensor_tensor(wt_l[:, g * QB:(g + 1) * QB], sbank(g), wt_h[:, g * QB:(g + 1) * QB],
                                        ALU.subtract).then_inc(wt_ready, 1)

            def residual(b):
                dve.wait_ge(step_used, (b + 1) * NE)
                for z in range(2):
                    xs = m.x[:, 4 * b + 2 * z:4 * b + 2 * z + 2, :].rearrange("p t d -> p (t d)")
                    ins = nc.vector.scalar_tensor_tensor(xs, obank(b, z), tgs[:, 0:1], xs, ALU.mult, ALU.add)
                ins.then_inc(out_used, 1)

            for n in range(STEPS):
                b, e = divmod(n, NE)
                dve.wait_ge(h_done, n + 1)
                dve.wait_ge(spread_ready, n + 1)
                nc.vector.tensor_tensor(y[:, n % 2, :], sbank(n), h[:, n % 2, :], ALU.mult).then_inc(y_done, 1)
                dve.wait_ge(yh_done, n + 1)
                nc.vector.tensor_tensor(y_l[:, n % 2, :], y[:, n % 2, :], y_h[:, n % 2, :], ALU.subtract).then_inc(yl_done, 1)
                if b and e == 1:
                    residual(b - 1)
            residual(NB - 1)

        @block.tensor
        def _(pe):
            pe.wait_ge(w_ready, 1)
            for t in range(NX):
                q = 0
                for wv, half in ((rw_h, m.xh), (rw_h, m.xl), (rw_l, m.xh)):
                    for c in range(DC):
                        ins = nc.tensor.matmul(hbank(0)[:, t * NE:(t + 1) * NE], half[:, c, t * P:(t + 1) * P], wv[:, c, :],
                                               start=(q == 0), stop=(q == 5))
                        q += 1
            ins.then_inc(routed, 1)

            def first(n):
                b, e = divmod(n, NE)
                if n >= 2:
                    pe.wait_ge(h_done, n - 1)
                elif n == 0:
                    pe.wait_ge(shifted, 1)
                    pe.wait_ge(w_ready, len(splits))
                q = 0
                for wv, half in ((w1_h, m.xh), (w1_h, m.xl), (w1_l, m.xh)):
                    for c in range(DC):
                        ins = nc.tensor.matmul(hbank(n), wv[:, c, e, :], half[:, c, b * QB:(b + 1) * QB], start=(q == 0), stop=(q == 5))
                        q += 1
                ins.then_inc(h_ready, 1)

            def spread(n):
                b, e = divmod(n, NE)
                if n >= 2:
                    pe.wait_ge(y_done, n - 1)
                for q, half in enumerate((wt_h, wt_l)):
                    ins = nc.tensor.matmul(sbank(n), pick[:, e, :], half[:, b * QB:(b + 1) * QB], start=(q == 0), stop=(q == 1))
                ins.then_inc(spread_ready, 1)

            def second(n):
                b, e = divmod(n, NE)
                if e == 0:
                    if b >= 2:
                        pe.wait_ge(out_used, b - 1)
                    for j in range(4):
                        for q, (half, bv) in enumerate(((wt_h, b2_h), (wt_h, b2_l), (wt_l, b2_h))):
                            nc.tensor.matmul(obank(b, j // 2)[:, (j % 2) * D:(j % 2 + 1) * D],
                                             half[:, b * QB + j * P:b * QB + (j + 1) * P], bv[:, :],
                                             start=(q == 0 and j % 2 == 0), stop=False, skip_group_check=True)
                pe.wait_ge(yl_done, n + 1)
                for j in range(4):
                    for q, (half, wv) in enumerate(((y_h, w2_h), (y_h, w2_l), (y_l, w2_h))):
                        ins = nc.tensor.matmul(obank(b, j // 2)[:, (j % 2) * D:(j % 2 + 1) * D],
                                               half[:, n % 2, j * P:(j + 1) * P], wv[:, e, :],
                                               start=False, stop=(e == NE - 1 and q == 2), skip_group_check=True)
                ins.then_inc(step_used, 1)

            first(0)
            first(1)
            pe.wait_ge(weights_done, 1)
            for g in range(NB):
                if g >= 2:
                    pe.wait_ge(wt_ready, g - 1)
                for j in range(4):
                    ins = nc.tensor.transpose(sbank(g)[:, j * P:(j + 1) * P], wt[:, 4 * g + j, :], m.ident[:, :])
                ins.then_inc(wt_turned, 1)
            pe.wait_ge(wt_ready, NB)
            spread(0)
            for n in range(STEPS):
                if n + 1 < STEPS:
                    if n >= 1:
                        first(n + 1)
                    spread(n + 1)
                second(n)


def stage_quantised(nc, m, xn, gate, wg_in, wu_in, wd_in):
    KF = FF // P
    with Semaphores(nc, "ffn") as sem, ExitStack() as ctx:
        def sb(name, shape, dt=FP32):
            return ctx.enter_context(nc.sbuf_tensor(f"ffn_{name}", shape, dt))

        wf = [sb(f"w{n}", [P, 2048]) for n in range(3)]
        wq = [sb(f"wq{n}", [P, 2048], BF16) for n in range(3)]
        ones = sb("ones", [P, P])
        wsum, wmean, wscale = sb("wsum", [P, 3]), sb("wmean", [P, 3]), sb("wscale", [P, 3])
        amax, ascale, adq = sb("amax", [P, NX]), sb("ascale", [P, NX]), sb("adq", [P, NX])
        gs, us = sb("gate_scale", [P, NX]), sb("up_scale", [P, NX])
        xi = sb("xi", [P, 2, D])
        xt = sb("xt", [P, 2, DC, P], BF16)
        sg = sb("silu", [P, 2, FF])
        hh = sb("h", [P, 2, FF])
        hmax, hscale, hdq = sb("hmax", [P, 2]), sb("hscale", [P, 2]), sb("hdq", [P, 2])
        ht = sb("ht", [P, 2, KF, P], BF16)
        w_loaded, dvec, wsum_done, wmean_done, wq_done = sem("w_loaded"), sem("dve_chain"), sem("wsum_done"), sem("wmean_done"), sem("wq_done")
        xi_ready, xt_turned, xt_ready = sem("xi_ready"), sem("xt_turned"), sem("xt_ready")
        gate_ready, up_ready, silu_done, h_done = sem("gate_ready"), sem("up_ready"), sem("silu_done"), sem("h_done")
        hi_ready, h_turned, ht_ready, down_ready, x_done = sem("hi_ready"), sem("h_turned"), sem("ht_ready"), sem("down_ready"), sem("x_done")
        scales_ready = sem("scales_ready")
        block = ctx.enter_context(nc.Block())

        @block.sync
        def _(sp):
            for n, w in enumerate((wg_in, wu_in)):
                sp.dma_start(wf[n][:, :].rearrange("p (c f) -> p c f", c=DC), w.rearrange("(c p) f -> p c f", p=P)).then_inc(w_loaded, 16)
            sp.dma_start(wf[2][:, :].rearrange("p (k d) -> p k d", k=KF), wd_in.rearrange("(k p) d -> p k d", p=P)).then_inc(w_loaded, 16)

        @block.vector
        def _(dve):
            chain = [0]

            def link(ins):
                chain[0] += 1
                ins.then_inc(dvec, 1)
                dve.wait_ge(dvec, chain[0])

            nc.vector.memset(ones[:, :], 1.0)
            dve.wait_ge(w_loaded, 48)
            for n in range(3):
                ins = nc.vector.tensor_reduce(wsum[:, n:n + 1], wf[n][:, :], AX.X, ALU.add, apply_absolute_value=True)
            ins.then_inc(wsum_done, 1)
            for t in range(NX):
                ins = nc.vector.tensor_reduce(amax[:, t:t + 1], xn[:, t, :], AX.X, ALU.max, apply_absolute_value=True)
            link(ins)
            link(nc.vector.tensor_scalar(amax[:, :], amax[:, :], 1e-5, None, ALU.max))
            link(nc.vector.reciprocal(ascale[:, :], amax[:, :]))
            nc.vector.tensor_scalar(ascale[:, :], ascale[:, :], 127.0, None, ALU.mult)
            link(nc.vector.tensor_scalar(adq[:, :], amax[:, :], 1.0 / 127.0, None, ALU.mult))
            dve.wait_ge(wmean_done, 1)
            link(nc.vector.tensor_scalar(wmean[:, :], m.bank[0][:, 0:3], 1.0 / (FF * D), 1e-5, ALU.mult, ALU.max))
            link(nc.vector.reciprocal(wscale[:, :], wmean[:, :]))
            nc.vector.tensor_scalar(gs[:, :], adq[:, :], wmean[:, 0:1], None, ALU.mult)
            nc.vector.tensor_scalar(us[:, :], adq[:, :], wmean[:, 1:2], None, ALU.mult).then_inc(scales_ready, 1)
            for n in range(3):
                link(nc.vector.tensor_scalar(wf[n][:, :], wf[n][:, :], wscale[:, n:n + 1], ROUND, ALU.mult, ALU.add))
                link(nc.vector.tensor_scalar(wf[n][:, :], wf[n][:, :], ROUND, 1.0, ALU.subtract, ALU.min))
                nc.vector.tensor_scalar(wq[n][:, :], wf[n][:, :], -1.0, None, ALU.max).then_inc(wq_done, 1)

            def quantise_x(t):
                link(nc.vector.tensor_scalar(xi[:, t % 2, :], xn[:, t, :], ascale[:, t:t + 1], ROUND, ALU.mult, ALU.add))
                nc.vector.tensor_scalar(xi[:, t % 2, :], xi[:, t % 2, :], ROUND, 127.0, ALU.subtract, ALU.min).then_inc(xi_ready, 1)

            def take_x(t):
                dve.wait_ge(xt_turned, t + 1)
                nc.vector.tensor_scalar(xt[:, t % 2, :, :].rearrange("p c q -> p (c q)"), m.bank[0][:, 0:D], -128.0, None, ALU.max).then_inc(xt_ready, 1)

            def residual(t):
                dve.wait_ge(down_ready, t + 1)
                nc.vector.scalar_tensor_tensor(m.x[:, t, :], m.bank[1][:, 0:D], hdq[:, t % 2:t % 2 + 1], m.x[:, t, :], ALU.mult, ALU.add).then_inc(x_done, 1)

            quantise_x(0)
            take_x(0)
            for t in range(NX):
                if t + 1 < NX:
                    quantise_x(t + 1)
                    take_x(t + 1)
                dve.wait_ge(up_ready, t + 1)
                dve.wait_ge(silu_done, t + 1)
                nc.vector.scalar_tensor_tensor(hh[:, t % 2, :], m.slot[1][:, :], us[:, t:t + 1], sg[:, t % 2, :],
                                               ALU.mult, ALU.mult).then_inc(h_done, 1)
                dve.wait_ge(h_done, t + 1)
                if t:
                    residual(t - 1)
                mx = hmax[:, t % 2:t % 2 + 1]
                link(nc.vector.tensor_reduce(mx, hh[:, t % 2, :], AX.X, ALU.max, apply_absolute_value=True))
                link(nc.vector.tensor_scalar(mx, mx, 1e-5, None, ALU.max))
                link(nc.vector.reciprocal(hscale[:, t % 2:t % 2 + 1], mx))
                link(nc.vector.tensor_scalar(hscale[:, t % 2:t % 2 + 1], hscale[:, t % 2:t % 2 + 1], 127.0, None, ALU.mult))
                link(nc.vector.tensor_scalar(hdq[:, t % 2:t % 2 + 1], mx, 1.0 / 127.0, wmean[:, 2:3], ALU.mult, ALU.mult))
                link(nc.vector.tensor_scalar(hdq[:, t % 2:t % 2 + 1], hdq[:, t % 2:t % 2 + 1], m.tg[:, gate:gate + 1], None, ALU.mult))
                link(nc.vector.tensor_scalar(hh[:, t % 2, :], hh[:, t % 2, :], hscale[:, t % 2:t % 2 + 1], ROUND, ALU.mult, ALU.add))
                nc.vector.tensor_scalar(hh[:, t % 2, :], hh[:, t % 2, :], ROUND, 127.0, ALU.subtract, ALU.min).then_inc(hi_ready, 1)
            residual(NX - 1)

        def take_h(t, act):
            act.wait_ge(h_turned, t + 1)
            if t >= 2:
                act.wait_ge(down_ready, t - 1)
            nc.scalar.activation(ht[:, t % 2, :, :].rearrange("p k q -> p (k q)"), m.wide[:, :], ACT.Copy).then_inc(ht_ready, 1)

        @block.scalar
        def _(act):
            act.wait_ge(scales_ready, 1)
            for t in range(NX):
                act.wait_ge(gate_ready, t + 1)
                if t >= 2:
                    act.wait_ge(h_done, t - 1)
                nc.scalar.activation(sg[:, t % 2, :], m.slot[0][:, :], ACT.Silu, scale=gs[:, t:t + 1]).then_inc(silu_done, 1)
                if t:
                    take_h(t - 1, act)
            take_h(NX - 1, act)

        @block.tensor
        def _(pe):
            pe.wait_ge(wsum_done, 1)
            nc.tensor.matmul(m.bank[0][:, 0:3], ones[:, :], wsum[:, :], start=True, stop=True).then_inc(wmean_done, 1)

            def turn_x(t):
                pe.wait_ge(xi_ready, t + 1)
                pe.wait_ge(scales_ready, 1) if t == 0 else pe.wait_ge(xt_ready, t)
                for c in range(DC):
                    ins = nc.tensor.transpose(m.bank[0][:, c * P:(c + 1) * P], xi[:, t % 2, c * P:(c + 1) * P], m.ident[:, :])
                ins.then_inc(xt_turned, 1)

            def gate_up(t):
                pe.wait_ge(xt_ready, t + 1)
                for n, (slot, used, ready) in enumerate(((m.slot[0], silu_done, gate_ready), (m.slot[1], h_done, up_ready))):
                    if t == 0:
                        pe.wait_ge(wq_done, n + 1)
                    else:
                        pe.wait_ge(used, t)
                    for z in range(2):
                        for c in range(DC):
                            ins = nc.tensor.matmul(slot[:, z * 512:(z + 1) * 512], xt[:, t % 2, c, :],
                                                   wq[n][:, c * FF + z * 512:c * FF + (z + 1) * 512], start=(c == 0), stop=(c == DC - 1))
                    ins.then_inc(ready, 1)

            def turn_h(t):
                pe.wait_ge(hi_ready, t + 1)
                if t:
                    pe.wait_ge(ht_ready, t)
                for k in range(KF):
                    ins = nc.tensor.transpose(m.wide[:, k * P:(k + 1) * P], hh[:, t % 2, k * P:(k + 1) * P], m.ident[:, :])
                ins.then_inc(h_turned, 1)

            def down(t):
                pe.wait_ge(ht_ready, t + 1)
                if t == 0:
                    pe.wait_ge(wq_done, 3)
                else:
                    pe.wait_ge(x_done, t)
                for k in range(KF):
                    ins = nc.tensor.matmul(m.bank[1][:, 0:D], ht[:, t % 2, k, :], wq[2][:, k * D:(k + 1) * D], start=(k == 0), stop=(k == KF - 1))
                ins.then_inc(down_ready, 1)

            turn_x(0)
            gate_up(0)
            for t in range(NX):
                if t + 1 < NX:
                    turn_x(t + 1)
                    gate_up(t + 1)
                turn_h(t)
                down(t)


def stage_context(nc, m, ctxt_in):
    with Semaphores(nc, "context") as sem, ExitStack() as ctx:
        c32 = ctx.enter_context(nc.sbuf_tensor("ctx_t", [P, DC, CTXP], FP32))
        loaded = sem("ctxt_loaded")
        padded = sem("ctxt_padded")
        hi_done = sem("ctxt_hi")
        block = ctx.enter_context(nc.Block())

        @block.sync
        def _(sp):
            sp.dma_start(c32[:, :, 0:CTX], ctxt_in.rearrange("(c p) t -> p c t", p=P)).then_inc(loaded, 16)

        @block.gpsimd
        def _(pool):
            nc.gpsimd.memset(c32[:, :, CTX:CTXP], 0.0).then_inc(padded, 1)

        @block.vector
        def _(dve):
            dve.wait_ge(loaded, 16)
            dve.wait_ge(padded, 1)
            for c in range(DC):
                nc.vector.tensor_copy(m.ch[:, c, :], c32[:, c, :]).then_inc(hi_done, 1)
            for c in range(DC):
                dve.wait_ge(hi_done, c + 1)
                nc.vector.tensor_tensor(m.cl[:, c, :], c32[:, c, :], m.ch[:, c, :], ALU.subtract)


def stage_store(nc, m, out):
    with Semaphores(nc, "store") as sem, ExitStack() as ctx:
        stored = sem("stored")
        block = ctx.enter_context(nc.Block())

        @block.sync
        def _(sp):
            sp.dma_start(out.rearrange("(t p) d -> p t d", p=P), m.x[:, :, :]).then_inc(stored, 16)
            sp.wait_ge(stored, 16)


def flamingo_kernel(nc, t, out, stages=4):
    with ExitStack() as ctx:
        m = allocate(nc, ctx)
        stage_setup(nc, m, t["x"], t["gates"])
        if stages >= 1:
            with nc.sbuf_tensor("ctx_rows", [P, NCT, D], FP32) as rows:
                stage_norm(nc, m, "nc0", rows, NCT, m.ch, m.cl, affine=t["gb1"], load=t["ctx"])
            stage_norm(nc, m, "nx0", m.x, NX, m.xh, m.xl, norms=2, affine=t["gb2"])
            stage_attention(nc, m, Attention("a0", True, 64, 0.125, False, 0), t["w0"], t["wo0"], (t["mask_row"], t["mask_cols"]))
        if stages >= 2:
            stage_norm(nc, m, "nx1", m.x, NX, m.xh, m.xl)
            stage_experts(nc, m, 2, t["rw"], t["rb"], t["w1"], t["eb1"], t["w2"], t["eb2"])
        if stages >= 3:
            stage_norm(nc, m, "nx2", m.x, NX, m.xh, m.xl)
            stage_context(nc, m, t["ctxt"])
            stage_attention(nc, m, Attention("a1", False, 16, 0.25, True, 1), t["w1a"], t["wo1"], (t["all_row"], t["all_cols"]),
                            t["bv"], t["bo"])
        if stages >= 4:
            with nc.sbuf_tensor("xn_rows", [P, NX, D], FP32) as rows:
                stage_norm(nc, m, "nx3", m.x, NX, rows=rows)
                stage_quantised(nc, m, rows, 3, t["wg"], t["wu"], t["wd"])
        stage_store(nc, m, out)


def lay_out(x, ctx_1024, mask_BxS2_bk0, g_xattn, g_ffn, L0_xattn_g1, L0_xattn_b1, L0_xattn_g2, L0_xattn_b2, L0_xattn_Wq,
            L0_xattn_Wkv, L0_xattn_Wout, L0_ffn_router_w, L0_ffn_router_b, L0_ffn_W1, L0_ffn_b1, L0_ffn_W2, L0_ffn_b2,
            L1_xattn_Wq, L1_xattn_bq, L1_xattn_Wk, L1_xattn_bk, L1_xattn_Wv, L1_xattn_bv, L1_xattn_Wo, L1_xattn_bo,
            L1_ffn_w_gate, L1_ffn_w_up, L1_ffn_w_down):
    import numpy as np

    def iterations(wq, wk, wv, *biases):
        def blocks(w):
            return w.reshape(DC, P, NPAIR, P).transpose(2, 1, 0, 3)
        out = np.zeros((NPAIR + 1, P, 3, DC, P), wq.dtype)
        out[:NPAIR, :, 0] = blocks(wq)
        out[:NPAIR, :, 1] = blocks(wk)
        out[1:, :, 2] = blocks(wv)
        out = out.reshape(NPAIR + 1, P, 3 * DC * P)
        if biases:
            own = np.zeros((NPAIR + 1, P, 2), wq.dtype)
            for n, b in enumerate(biases):
                own[:NPAIR, :, n] = b.reshape(NPAIR, P)
            out = np.concatenate([out, own], axis=2)
        return out

    def pad_heads(a):
        out = np.zeros((*a.shape[:-1], 16, HB), a.dtype)
        out[..., :16] = a.reshape(*a.shape[:-1], 16, 16)
        return out.reshape(*a.shape[:-1], 16 * HB)

    def columns(*rows):
        return np.stack([r.reshape(-1, P).T for r in rows], axis=1)

    def pad_mask(mask):
        row = np.zeros((1, CTXP), bool)
        row[:, :CTX] = mask
        return row, row.reshape(NCT, P).T

    mask_row, mask_cols = pad_mask(mask_BxS2_bk0)
    all_row, all_cols = pad_mask(np.ones((1, CTX), bool))
    inner = L0_xattn_Wq.shape[1]
    return {
        "x": x[0], "ctx": ctx_1024[0], "ctxt": ctx_1024[0].T, "mask_row": mask_row, "mask_cols": mask_cols,
        "all_row": all_row, "all_cols": all_cols,
        "gates": np.stack([g_xattn[0], g_xattn[1], g_ffn[0], g_ffn[1]])[None],
        "gb1": columns(L0_xattn_g1, L0_xattn_b1), "gb2": columns(L0_xattn_g2, L0_xattn_b2),
        "w0": iterations(L0_xattn_Wq, L0_xattn_Wkv[:, :inner], L0_xattn_Wkv[:, inner:]),
        "wo0": L0_xattn_Wout.reshape(NPAIR, P, D),
        "rw": L0_ffn_router_w, "rb": L0_ffn_router_b[None], "w1": L0_ffn_W1, "eb1": L0_ffn_b1.T, "w2": L0_ffn_W2, "eb2": L0_ffn_b2,
        "w1a": iterations(pad_heads(L1_xattn_Wq.T), pad_heads(L1_xattn_Wk.T), pad_heads(L1_xattn_Wv.T),
                          pad_heads(L1_xattn_bq), pad_heads(L1_xattn_bk)),
        "wo1": pad_heads(L1_xattn_Wo).T.reshape(NPAIR, P, D),
        "bv": pad_heads(L1_xattn_bv)[None], "bo": L1_xattn_bo[None],
        "wg": L1_ffn_w_gate.T, "wu": L1_ffn_w_up.T, "wd": L1_ffn_w_down.T,
    }


def kernel(**inputs):
    import numpy as np
    import concourse.bacc as bacc
    from concourse.bass_utils import run_bass_kernel_spmd

    arrays = {f"in_{k}": np.ascontiguousarray(v) for k, v in lay_out(**{k: np.asarray(v) for k, v in inputs.items()}).items()}
    nc = bacc.Bacc("TRN2", target_bir_lowering=False, num_devices=1)
    t = {k[3:]: nc.dram_tensor(k, v.shape, mybir.dt.from_np(v.dtype), kind="ExternalInput").ap() for k, v in arrays.items()}
    out = nc.dram_tensor("out_x", (TOK, D), FP32, kind="ExternalOutput").ap()
    flamingo_kernel(nc, t, out)
    result = run_bass_kernel_spmd(nc, [arrays], core_ids=[0])
    return result.results[0]["out_x"].reshape(1, TOK, D)
```

```python
import concourse.bass as bass
from concourse import mybir
from contextlib import ExitStack

FP32 = mybir.dt.float32
FP16 = mybir.dt.float16
BF16 = mybir.dt.bfloat16
ALU = mybir.AluOpType
ACT = mybir.ActivationFunctionType
AX = mybir.AxisListType

P = 128
D = 256
DC = D // P
TOK = 2048
NX = TOK // P
CTX = 1601
NCT = -(-CTX // P)
CTXP = NCT * P
CTX_LAST = CTX - (NCT - 1) * P
QB = 512
NU = TOK // QB
HALF = P // 2
EPS = 1e-5
WSCALE = 16.0
MASKED = -1e30
RY = 3
NE, EF = 8, 128
FF = 1024
ROUND = 1.5 * 2.0 ** 23


def wait(eng, sem, value):
    if not isinstance(value, int) or value > 0:
        eng.wait_ge(sem, value)


def split_even(n, parts):
    return [(j + 1) * n // parts - j * n // parts for j in range(parts)]


class Semaphores:

    def __init__(self, nc, tag):
        self.nc, self.tag, self.all = nc, tag, []

    def __call__(self, name):
        self.all.append(self.nc.alloc_semaphore(f"{self.tag}_{name}"))
        return self.all[-1]

    def __enter__(self):
        return self

    def __exit__(self, kind, *rest):
        if kind is None:
            self.nc.clear_and_free_semaphores(self.all)
            self.nc.all_engine_barrier()


class Memory:
    pass


def allocate(nc, ctx):
    m = Memory()

    def sb(name, shape, dt=FP32):
        return ctx.enter_context(nc.sbuf_tensor(name, shape, dt))

    m.x = sb("x_res", [P, NX, D])
    m.xh = sb("xt_hi", [P, DC, TOK], FP16)
    m.xl = sb("xt_lo", [P, DC, TOK], FP16)
    m.ch = sb("ct_hi", [P, DC, CTXP], FP16)
    m.cl = sb("ct_lo", [P, DC, CTXP], FP16)
    m.ident = sb("ident", [P, P])
    m.tg = sb("tanh_gates", [P, 4])
    m.slot = [ctx.enter_context(nc.psum_tensor(f"slot{n}", [P, 1024], FP32)) for n in range(2)]
    m.bank = [ctx.enter_context(nc.psum_tensor(f"bank{n}", [P, 512], FP32)) for n in range(2)]
    m.wide = ctx.enter_context(nc.psum_tensor("wide", [P, 1024], FP32))
    return m


def stage_setup(nc, m, x_in, gates_in):
    with Semaphores(nc, "setup") as sem, ExitStack() as ctx:
        gates = ctx.enter_context(nc.sbuf_tensor("gates_raw", [P, 4], FP32))
        x_in_sem = sem("x_loaded")
        gates_sem = sem("gates_loaded")
        zeroed = sem("identity_zeroed")
        block = ctx.enter_context(nc.Block())

        @block.sync
        def _(sp):
            sp.dma_start(gates[:, :], gates_in[0:1, :].broadcast_to([P, 4])).then_inc(gates_sem, 16)
            sp.dma_start(m.x[:, :, :], x_in.rearrange("(t p) d -> p t d", p=P)).then_inc(x_in_sem, 16)
            sp.wait_ge(x_in_sem, 16)

        @block.gpsimd
        def _(pool):
            nc.gpsimd.memset(m.ident[:, :], 0.0).then_inc(zeroed, 1)
            pool.wait_ge(zeroed, 1)
            nc.gpsimd.affine_select(out=m.ident[:, :], in_=m.ident[:, :], compare_op=ALU.not_equal, fill=1.0,
                                    base=0, pattern=[[-1, P]], channel_multiplier=1)

        @block.scalar
        def _(act):
            act.wait_ge(gates_sem, 16)
            nc.scalar.activation(m.tg[:, :], gates[:, :], ACT.Tanh)


def stage_norm(nc, m, tag, src, nt, hi=None, lo=None, norms=1, affine=None, load=None, rows=None):
    groups = [list(range(a, min(a + 4, nt))) for a in range(0, nt, 4)] if rows is None else []
    with Semaphores(nc, tag) as sem, ExitStack() as ctx:
        def sb(name, shape, dt=FP32):
            return ctx.enter_context(nc.sbuf_tensor(f"{tag}_{name}", shape, dt))

        stats = sb("stats", [P, nt, 6])
        mv = sb("mv", [P, nt, 2])
        std = sb("std", [P, nt])
        rstd = sb("rstd", [P, nt])
        eps = sb("eps", [P, 1])
        xn = sb("xn", [P, nt, D]) if rows is None else rows
        y = sb("y", [P, 2, 512])
        gb = sb("gb", [P, 2, DC])
        loaded, gb_loaded = sem("loaded"), sem("gb_loaded")
        padded, eps_set, stats_done = sem("padded"), sem("eps_set"), sem("stats_done")
        aggregated, std_done, rstd_done, normed = sem("aggregated"), sem("std_done"), sem("rstd_done"), sem("normed")
        turned, y_ready, hi_done, lo_done = sem("turned"), sem("y_ready"), sem("hi_done"), sem("lo_done")
        block = ctx.enter_context(nc.Block())
        n_load = 0
        if load is not None:
            n_load = 1 + (CTX_LAST < P)

        @block.sync
        def _(sp):
            if load is not None:
                full = (nt - 1) * P
                sp.dma_start(src[:, 0:nt - 1, :], load[0:full, :].rearrange("(t p) d -> p t d", p=P)).then_inc(loaded, 16)
                sp.wait_ge(padded, 1)
                sp.dma_start(src[0:CTX_LAST, nt - 1, :], load[full:full + CTX_LAST, :]).then_inc(loaded, 16)
            if affine is not None:
                sp.dma_start(gb[:, :, :], affine).then_inc(gb_loaded, 16)

        @block.vector
        def _(dve):
            nc.vector.memset(eps[:, :], EPS).then_inc(eps_set, 1)
            if load is not None:
                nc.vector.memset(src[:, nt - 1, :], 0.0).then_inc(padded, 1)
                dve.wait_ge(loaded, 16 * n_load)
            for r in range(norms):
                a = src if r == 0 else xn
                if r:
                    dve.wait_ge(normed, nt * r)
                for t in range(nt):
                    nc.vector.bn_stats(stats[:, t, :], a[:, t, :]).then_inc(stats_done, 1)
                for t in range(nt):
                    dve.wait_ge(stats_done, r * nt + t + 1)
                    nc.vector.bn_aggr(mv[:, t, :], stats[:, t, :]).then_inc(aggregated, 1)
                dve.wait_ge(std_done, r + 1)
                nc.vector.reciprocal(rstd[:, :], std[:, :]).then_inc(rstd_done, 1)
                dve.wait_ge(rstd_done, r + 1)
                dve.wait_ge(aggregated, (r + 1) * nt)
                for t in range(nt):
                    nc.vector.tensor_scalar(xn[:, t, :], a[:, t, :], mv[:, t, 0:1], rstd[:, t:t + 1],
                                            ALU.subtract, ALU.mult).then_inc(normed, 1)
            for g, tiles in enumerate(groups):
                w = len(tiles) * P
                for c in range(DC):
                    n = g * DC + c
                    dve.wait_ge(hi_done, n + 1)
                    nc.vector.tensor_tensor(lo[:, c, g * 512:g * 512 + w], y[:, n % 2, 0:w],
                                            hi[:, c, g * 512:g * 512 + w], ALU.subtract).then_inc(lo_done, 1)

        @block.scalar
        def _(act):
            act.wait_ge(eps_set, 1)
            for r in range(norms):
                act.wait_ge(aggregated, (r + 1) * nt)
                nc.scalar.activation(std[:, :], mv[:, :, 1], ACT.Sqrt, bias=eps[:, 0:1]).then_inc(std_done, 1)
            if affine is not None:
                act.wait_ge(gb_loaded, 16)
            for g, tiles in enumerate(groups):
                w = len(tiles) * P
                for c in range(DC):
                    n = g * DC + c
                    act.wait_ge(turned, n + 1)
                    if n >= 2:
                        act.wait_ge(lo_done, n - 1)
                    if affine is None:
                        nc.scalar.activation(y[:, n % 2, 0:w], m.slot[n % 2][:, 0:w], ACT.Copy).then_inc(y_ready, 1)
                    else:
                        nc.scalar.activation(y[:, n % 2, 0:w], m.slot[n % 2][:, 0:w], ACT.Identity,
                                             bias=gb[:, 1, c:c + 1], scale=gb[:, 0, c:c + 1]).then_inc(y_ready, 1)
                    act.wait_ge(y_ready, n + 1)
                    nc.scalar.activation(hi[:, c, g * 512:g * 512 + w], y[:, n % 2, 0:w], ACT.Copy).then_inc(hi_done, 1)

        @block.tensor
        def _(pe):
            for g, tiles in enumerate(groups):
                pe.wait_ge(normed, (norms - 1) * nt + tiles[-1] + 1)
                for c in range(DC):
                    n = g * DC + c
                    if n >= 2:
                        pe.wait_ge(y_ready, n - 1)
                    for j, t in enumerate(tiles):
                        last = nc.tensor.transpose(m.slot[n % 2][:, j * P:(j + 1) * P], xn[:, t, c * P:(c + 1) * P],
                                                   m.ident[:, :])
                    last.then_inc(turned, 1)


class Attention:

    def __init__(self, name, latents, head, heads, q_scale, biased, gate):
        self.name = name
        self.latents = latents
        self.head = head
        self.heads = heads
        self.pitch = P // heads
        self.groups = 16 // heads
        self.stacked = head < HALF
        self.q_scale = q_scale
        self.biased = biased
        self.gate = gate
        self.ring = 8 if self.stacked else 5
        self.nl = NX if latents else 0
        self.nt = self.nl + NCT
        self.keys = self.nt * P
        self.kchunks = [(a, 512, True) for a in range(0, self.nl * P, 512)]
        self.kchunks += [(self.nl * P + a, min(512, CTXP - a), False) for a in range(0, CTXP, 512)]
        self.vgroups = [list(range(a, min(a + 4, self.nt))) for a in range(0, self.nt, 4)]
        self.qblock = P // heads
        self.nblock = QB // self.qblock
        self.mchunks = [(a, 512, False) for a in range(0, self.nl * P, 512)]
        self.mchunks += [(a, CTXP // 4, True) for a in range(0, CTXP, CTXP // 4)]
        self.msteps = len(self.mchunks) * self.nblock
        n = 4 if latents else 2
        self.kparts = [(j * self.nt // n, (j + 1) * self.nt // n) for j in range(n)]
        self.pool_tiles = [t for t in range(self.nt) if t * 17 // 29 != (t + 1) * 17 // 29] if not self.stacked else []
        self.dve_tiles = [t for t in range(self.nt) if t not in self.pool_tiles] if not self.stacked else []
        self.raw_after, self.den_after, self.turn_after, self.out_after = (2, 5, 8, 12) if self.stacked else (0, 2, 4, 6)


def stage_attention(nc, m, a, w_in, wo_in, mask_in, bv_in=None, bo_in=None):
    NT, NL, KEYS = a.nt, a.nl, a.keys
    NK, NV = len(a.kchunks), len(a.vgroups)
    NKQ = NK + NU
    MS = a.msteps
    G, PITCH, QW, NB, RP = a.heads, a.pitch, a.qblock, a.nblock, a.ring
    PAIRS = G // 2
    NS = NT * PAIRS
    STEPS, TILES = NU * NS, NU * NT
    n_pass = 1 if a.stacked else 2
    with Semaphores(nc, a.name) as sem, ExitStack() as ctx:
        def sb(name, shape, dt=FP32):
            return ctx.enter_context(nc.sbuf_tensor(f"{a.name}_{name}", shape, dt))

        nb = 2 if a.biased else 0
        w_st = sb("w_staged", [P, 3 * DC * P + nb])
        w_hi, w_lo = sb("w_hi", [P, 3 * DC * P], FP16), sb("w_lo", [P, 3 * DC * P], FP16)
        w16 = sb("w_scaled", [P, 3 * DC * P])
        wscale = sb("w_scale", [P, 1])

        def weights(half, what, c):
            at = (what * DC + c) * P
            return half[:, at:at + P]

        wo = sb("wo", [P, D])
        y = sb("y", [P, RY, 512])
        kn_hi, kn_lo = sb("kn_hi", [P, KEYS], FP16), sb("kn_lo", [P, KEYS], FP16)
        qn_hi, qn_lo = sb("qn_hi", [P, TOK], FP16), sb("qn_lo", [P, TOK], FP16)
        kmask = sb("k_masked", [P, CTXP], FP16)
        qdiag = sb("q_diag", [P, TOK // QW, G, QW], FP16)
        part_max = sb("part_max", [P, NB, len(a.mchunks)])
        neg_max = sb("neg_max", [P, NB])
        shift = sb("shift", [NB, G, QB], FP16)
        diag = sb("diag", [NB, NB, QW])
        k_op = [[sb(f"k_op{h}{n}", [P, KEYS], FP16) for n in range(n_pass)] for h in range(G)]
        q_op = [[sb(f"q_op{h}{n}", [P, TOK], FP16) for n in range(n_pass)] for h in range(G)]
        val = sb("val", [P, NT, P])
        prob = sb("prob", [P, RP, 2 * QB])
        if not a.stacked:
            acc_v, acc_p = sb("acc_v", [P, 2, 2 * QB]), sb("acc_p", [P, 2, 2 * QB])
            ones = sb("ones", [P, HALF])
        else:
            raw = sb("raw", [P, QB])
            spread = sb("spread", [P, P])
        rden = sb("rden", [P, QB])
        att = sb("att", [P, QB])
        valid_u8 = sb("valid_u8", [P, CTXP], mybir.dt.uint8)
        valid = sb("valid", [P, CTXP], FP16)
        mcol_u8 = sb("mcol_u8", [P, NCT], mybir.dt.uint8)
        mbias = sb("mask_bias", [P, NT])
        if a.biased:
            qk_bias, bscale = sb("qk_bias", [P, 2]), sb("bias_scale", [P, 2])
            bv = sb("bv", [P, a.groups, P])
            bo = sb("bo", [P, D])
            bos = sb("bo_gated", [P, D])

        w_loaded, w_split, wo_loaded = sem("w_loaded"), sem("w_split"), sem("wo_loaded")
        split16, wscale_set = sem("w_scaled"), sem("wscale_set")
        mask_loaded, bias_loaded = sem("mask_loaded"), sem("bias_loaded")
        zeros_set, prep = sem("zeros_set"), sem("prep")
        proj_done, proj_read = sem("proj_done"), sem("proj_read")
        y_used, y_hi = sem("y_used"), sem("y_hi")
        next_ready, kmask_part = sem("next_ready"), sem("kmask_part")
        k_laid = [sem(f"k_laid{c}") for c in range(len(a.kparts))]
        q_laid = [sem(f"q_laid{u}") for u in range(NU)]
        scores_ready, probs_ready, av_done = sem("scores_ready"), sem("probs_ready"), sem("av_done")
        added_v, added_p = sem("added_v"), sem("added_p")
        raw_ready = sem("raw_ready")
        den_ready, den_used = sem("den_ready"), sem("den_used")
        att_ready, out_ready, out_used = sem("att_ready"), sem("out_ready"), sem("out_used")
        max_ready, max_used = sem("max_ready"), sem("max_used")
        neg_ready, neg_turned, shift_ready = sem("neg_ready"), sem("neg_turned"), sem("shift_ready")
        block = ctx.enter_context(nc.Block())


        def summed(tiles, i, u, n):
            return (i * NU + u) * (len(tiles) - 1) + n

        wide = [m.wide[:, n * 512:(n + 1) * 512] for n in range(2)]
        slots = []
        for u in range(NU):
            for t in range(NS):
                slots.append(("scores", u, t))
                if u and t == a.den_after:
                    slots.append(("den", u - 1, 0))
                if u and t == a.out_after:
                    slots.append(("out", u - 1, 0))
        slots.append(("den", NU - 1, 0))
        slots.append(("out", NU - 1, 0))
        places = split_even(MS, NS)

        def bank_of(n):
            return m.slot[(n // 2) % 2][:, (n % 2) * 512:(n % 2) * 512 + 512]

        def consumed(k, i):
            kind, u, t = slots[k]
            if kind == "scores":
                return probs_ready, i * STEPS + u * NS + t + 1
            if kind == "den":
                return den_used, i * NU + u + 1
            return out_used, i * NU + u + 2

        def groups_before(it):
            return it * NKQ + (it - 1) * NV if not isinstance(it, int) or it else 0

        def y_before(it):
            return groups_before(it) if a.biased else it * NKQ

        @block.sync
        def _(sp):
            sp.dma_start(w_st[:, :], w_in[0, :, :]).then_inc(w_loaded, 16)
            sp.dma_start(valid_u8[:, :], mask_in[0][0:1, :].broadcast_to([P, CTXP])).then_inc(mask_loaded, 16)
            sp.dma_start(mcol_u8[:, :], mask_in[1]).then_inc(mask_loaded, 16)
            if a.biased:
                sp.dma_start(bv[:, :, :].rearrange("p n c -> p (n c)"), bv_in[0:1, :].broadcast_to([P, a.groups * P])).then_inc(bias_loaded, 16)
                sp.dma_start(bo[:, :], bo_in[0:1, :].broadcast_to([P, D])).then_inc(bias_loaded, 16)
            sp.wait_ge(zeros_set, 1)

            def lay_q(u, i, it):
                sp.wait_ge(shift_ready, u + 1 if it is None else it * NU + u + 1)
                c = slice(u * QB, (u + 1) * QB)
                for h in range(G):
                    r = slice(h * PITCH, h * PITCH + a.head)
                    if a.stacked:
                        parts = [(q_op[h][0][0:a.head, c], qn_hi[r, c]),
                                 (q_op[h][0][a.head:2 * a.head, c], qn_lo[r, c]),
                                 (q_op[h][0][2 * a.head:3 * a.head, c], qn_hi[r, c]),
                                 (q_op[h][0][HALF:HALF + NB, c], shift[:, h, :])]
                    else:
                        parts = [(q_op[h][0][0:HALF, c], qn_hi[r, c]), (q_op[h][0][HALF:P, c], qn_lo[r, c]),
                                 (q_op[h][1][0:HALF, c], qn_hi[r, c]), (q_op[h][1][HALF:HALF + NB, c], shift[:, h, :])]
                    for dst, src in parts:
                        sp.dma_start(dst, src).then_inc(q_laid[u], 16)

            def lay_k(n, i, it):
                lo, hi = a.kparts[n]
                wait(sp, scores_ready, i * STEPS + (NU - 1) * NS + hi * PAIRS if it is not None else 0)
                c = slice(lo * P, hi * P)
                for h in range(G):
                    r = slice(h * PITCH, h * PITCH + a.head)
                    if a.stacked:
                        parts = [(k_op[h][0][0:a.head, c], kn_hi[r, c]),
                                 (k_op[h][0][a.head:2 * a.head, c], kn_hi[r, c]),
                                 (k_op[h][0][2 * a.head:3 * a.head, c], kn_lo[r, c])]
                    else:
                        parts = [(k_op[h][0][0:HALF, c], kn_hi[r, c]), (k_op[h][0][HALF:P, c], kn_hi[r, c]),
                                 (k_op[h][1][0:HALF, c], kn_lo[r, c])]
                    for dst, src in parts:
                        sp.dma_start(dst, src).then_inc(k_laid[n], 16)

            def pair(i, first=False, last=False):
                it = None if first else i + 1
                if not first:
                    sp.wait_ge(proj_done, groups_before(i + 1) + 1)
                    sp.wait_ge(zeros_set, 1)
                    sp.dma_start(wo[:, :], wo_in[i, :, :]).then_inc(wo_loaded, 16)
                if last:
                    return
                sp.wait_ge(w_split, 1 if first else i + 2)
                sp.wait_ge(zeros_set, 1)
                sp.dma_start(w_st[:, :], w_in[1 if first else i + 2, :, :]).then_inc(w_loaded, 16)
                sp.wait_ge(next_ready, 1 if first else i + 2)
                if first:
                    for n in range(len(a.kparts)):
                        lay_k(n, 0, None)
                    for u in range(NU):
                        lay_q(u, 0, None)
                else:
                    for u in range(NU - 1):
                        lay_q(u, i, it)
                    for n in range(len(a.kparts)):
                        lay_k(n, i, it)
                    lay_q(NU - 1, i, it)

            pair(0, first=True)
            with sp.Fori(0, a.groups - 1) as i:
                pair(i)
            pair(a.groups - 1, last=True)

        @block.gpsimd
        def _(pool):
            def split(n):
                scale = wscale[:, 0:1].broadcast_to([P, 3 * DC * P])
                pool.wait_ge(w_loaded, n * 16 + 16)
                nc.gpsimd.tensor_tensor(w_hi[:, :], w_st[:, 0:3 * DC * P], scale, ALU.mult)
                if a.biased:
                    nc.gpsimd.tensor_tensor(qk_bias[:, :], w_st[:, 3 * DC * P:], bscale[:, :], ALU.mult)
                nc.gpsimd.tensor_tensor(w16[:, :], w_st[:, 0:3 * DC * P], scale, ALU.mult).then_inc(split16, 1)
                pool.wait_ge(split16, n + 1)
                nc.gpsimd.tensor_tensor(w_lo[:, :], w16[:, :], w_hi[:, :], ALU.subtract).then_inc(w_split, 1)

            def pair(i, last=False):
                for u in range(NU):
                    if u == 0 and not last:
                        pool.wait_ge(proj_read, groups_before(i + 2))
                        split(i + 2)
                    for n, t in enumerate(a.pool_tiles[1:]):
                        k = u * NT + t
                        if n == 0 and u >= 2:
                            pool.wait_ge(den_ready, i * NU + u - 1)
                        pool.wait_ge(probs_ready, i * STEPS + k + 1)
                        if n == 0:
                            before = prob[:, (u * NT + a.pool_tiles[0]) % RP, :]
                        else:
                            before = acc_p[:, u % 2, :]
                            pool.wait_ge(added_p, summed(a.pool_tiles, i, u, n))
                        nc.gpsimd.tensor_tensor(acc_p[:, u % 2, :], before, prob[:, k % RP, :], ALU.add).then_inc(added_p, 1)

            nc.gpsimd.memset(wscale[:, :], WSCALE)
            if a.biased:
                nc.gpsimd.memset(bscale[:, 1:2], 1.0)
                nc.gpsimd.memset(bscale[:, 0:1], a.q_scale)
            nc.gpsimd.memset(w16[:, 0:1], 0.0).then_inc(wscale_set, 1)
            pool.wait_ge(wscale_set, 1)
            split(0)
            pool.wait_ge(proj_read, NKQ)
            split(1)
            with pool.Fori(0, a.groups - 1) as i:
                pair(i)
            if a.pool_tiles:
                pair(a.groups - 1, last=True)

        @block.scalar
        def _(act):
            def project(it, kq, values):
                g0, y0 = groups_before(it), y_before(it)
                n = 0
                if kq:
                    for j in range(NKQ):
                        w = a.kchunks[j][1] if j < NK else QB
                        act.wait_ge(proj_done, g0 + n + 1)
                        wait(act, y_used, y0 + n - RY + 1)
                        src = bank_of(n)[:, 0:w]
                        scale = (1.0 if j < NK else a.q_scale) / WSCALE
                        if a.biased:
                            b = qk_bias[:, 1:2] if j < NK else qk_bias[:, 0:1]
                            nc.scalar.activation(y[:, n % RY, 0:w], src, ACT.Identity, bias=b, scale=scale).then_inc(proj_read, 1)
                        else:
                            nc.scalar.activation(y[:, n % RY, 0:w], src, ACT.Copy, scale=scale).then_inc(proj_read, 1)
                        n += 1
                if values:
                    for tiles in a.vgroups:
                        w = len(tiles) * P
                        act.wait_ge(proj_done, g0 + n + 1)
                        src = bank_of(n)[:, 0:w]
                        if a.biased:
                            wait(act, y_used, y0 + n - RY + 1)
                            nc.scalar.activation(y[:, n % RY, 0:w], src, ACT.Copy, scale=1.0 / WSCALE).then_inc(proj_read, 1)
                        else:
                            dst = val[:, tiles[0]:tiles[-1] + 1, :].rearrange("p t c -> p (t c)")
                            nc.scalar.activation(dst, src, ACT.Copy, scale=1.0 / WSCALE).then_inc(proj_read, 1)
                        n += 1

            def pair(i, last=False):
                project(i + 1, not last, True)
                for u in range(NU):
                    for t in range(NS):
                        k = u * NS + t
                        act.wait_ge(scores_ready, i * STEPS + k + 1)
                        if k >= RP:
                            o = (k - RP) // PAIRS
                            act.wait_ge(av_done, i * TILES + o + 1)
                            for tiles, added in ((a.pool_tiles, added_p), (a.dve_tiles, added_v)):
                                if o % NT in tiles:
                                    act.wait_ge(added, summed(tiles, i, o // NT, max(tiles.index(o % NT), 1)))
                        slot = slots.index(("scores", u, t))
                        nc.scalar.activation(prob[:, k % RP, :], m.slot[slot % 2][:, :], ACT.Exp,
                                             bias=mbias[:, t // PAIRS:t // PAIRS + 1]).then_inc(probs_ready, 1)

            act.wait_ge(prep, 1)
            project(0, True, False)
            with act.Fori(0, a.groups - 1) as i:
                pair(i)
            pair(a.groups - 1, last=True)

        @block.vector
        def _(dve):
            chain = [0]
            link_sem = sem("dve_chain")

            def link(ins):
                chain[0] += 1
                ins.then_inc(link_sem, 1)
                dve.wait_ge(link_sem, chain[0])

            nc.vector.memset(mbias[:, :], 0.0)
            nc.vector.memset(qdiag[:, :, :, :], 0.0)
            nc.vector.memset(att[:, :], 0.0)
            if not a.stacked:
                nc.vector.memset(ones[:, :], 1.0)
            if a.stacked:
                row = m.ident[:, :].rearrange("p (g c) -> p g c", c=PITCH)[:, :, PITCH // 2:PITCH // 2 + 1]
                nc.vector.tensor_copy(spread[:, :].rearrange("p (g c) -> p g c", c=PITCH), row.broadcast_to([P, G, PITCH]))
            for h in range(G):
                for op, v in ((k_op, 1.0), (q_op, 0.0)):
                    t = op[h][-1]
                    lo = 0 if a.stacked else HALF
                    link(nc.vector.memset(t[lo:P, :], 0.0))
                    link(nc.vector.memset(t[HALF:HALF + NB, :], v))
            nc.vector.memset(rden[:, :], 0.0).then_inc(zeros_set, 1)
            link(nc.vector.tensor_copy(diag[:, :, :], m.ident[0:NB, 0:NB].rearrange("p (j o) -> p j o", o=1).broadcast_to([NB, NB, QW])))
            dve.wait_ge(mask_loaded, 32)
            nc.vector.tensor_copy(valid[:, :], valid_u8[:, :])
            link(nc.vector.tensor_scalar(mbias[:, NL:NT], mcol_u8[:, :], -1.0, -MASKED, ALU.add, ALU.mult))
            if a.biased:
                dve.wait_ge(bias_loaded, 32)
                ones_cols = bv[:, :, :].rearrange("p n (h c) -> p (n h) c", c=PITCH)[:, :, PITCH // 2:]
                link(nc.vector.memset(ones_cols, 1.0))
                link(nc.vector.tensor_scalar(bos[:, :], bo[:, :], m.tg[:, a.gate:a.gate + 1], None, ALU.mult))
                for t in range(NX):
                    ins = nc.vector.tensor_tensor(m.x[:, t, :], m.x[:, t, :], bos[:, :], ALU.add)
                link(ins)
            nc.vector.memset(rden[:, :], 0.0).then_inc(prep, 1)
            nc.vector.memset(att[:, :], 0.0).then_inc(out_used, 1)

            def project(it, kq, values, pair_v):
                g0, y0 = groups_before(it), y_before(it)
                n = 0
                if kq:
                    for c in range(len(a.kparts)):
                        wait(dve, k_laid[c], it * 16 * 3 * G)
                    for u in range(NU):
                        wait(dve, q_laid[u], it * 16 * 4 * G)
                    for j in range(NKQ):
                        key = j < NK
                        c0, w = a.kchunks[j][:2] if key else ((j - NK) * QB, QB)
                        hi, lo = (kn_hi, kn_lo) if key else (qn_hi, qn_lo)
                        dve.wait_ge(proj_read, g0 + n + 1)
                        nc.vector.tensor_copy(hi[:, c0:c0 + w], y[:, n % RY, 0:w]).then_inc(y_hi, 1)
                        dve.wait_ge(y_hi, it * NKQ + j + 1)
                        nc.vector.tensor_tensor(lo[:, c0:c0 + w], y[:, n % RY, 0:w], hi[:, c0:c0 + w], ALU.subtract).then_inc(y_used, 1)
                        if key and not a.kchunks[j][2]:
                            b0 = c0 - NL * P
                            km = kmask[:, b0:b0 + w]
                            nc.vector.scalar_tensor_tensor(km, hi[:, c0:c0 + w], k0[:, 0:1], valid[:, b0:b0 + w],
                                                           ALU.subtract, ALU.mult).then_inc(kmask_part, 1)
                            dve.wait_ge(kmask_part, it * (NK - NL // 4) + (j - NL // 4) + 1)
                            nc.vector.tensor_scalar(km, km, k0[:, 0:1], None, ALU.add)
                        if not key:
                            for h in range(G):
                                r = slice(h * PITCH, (h + 1) * PITCH)
                                b = c0 // QW
                                ins = nc.vector.tensor_copy(qdiag[r, b:b + NB, h, :],
                                                            hi[r, c0:c0 + w].rearrange("p (b q) -> p b q", q=QW))
                        n += 1
                    ins.then_inc(next_ready, 1)
                if values and a.biased:
                    for tiles in a.vgroups:
                        w = len(tiles)
                        dve.wait_ge(proj_read, g0 + n + 1)
                        row = bv[:, pair_v:pair_v + 1, :] if isinstance(pair_v, int) else bv[:, bass.ds(pair_v, 1), :]
                        nc.vector.tensor_tensor(val[:, tiles[0]:tiles[-1] + 1, :],
                                                y[:, n % RY, 0:w * P].rearrange("p (t c) -> p t c", c=P),
                                                row.broadcast_to([P, w, P]), ALU.add).then_inc(y_used, 1)
                        n += 1

            def max_step(it, u, s):
                c, j = s // NB, s % NB
                w = a.mchunks[c][1]
                if s == 0:
                    wait(dve, neg_ready, it * NU + u)
                dve.wait_ge(max_ready, it * NU * MS + u * MS + s + 1)
                nc.vector.reduce_max(part_max[:, j:j + 1, c], wide[s % 2][:, 0:w], AX.X).then_inc(max_used, 1)

            def max_of_unit(it, u):
                dve.wait_ge(max_used, it * NU * MS + (u + 1) * MS)
                nc.vector.tensor_reduce(neg_max[:, :], part_max[:, :, :], AX.X, ALU.max, negate=True).then_inc(neg_ready, 1)

            def shift_of_unit(it, u):
                dve.wait_ge(neg_turned, it * NU + u + 1)
                if u:
                    dve.wait_ge(q_laid[u - 1], (it + 1) * 16 * 4 * G)
                rows = wide[0][0:NB, 0:P].rearrange("j (h o q) -> j h o q", h=G, o=1).broadcast_to([NB, G, NB, QW])
                for h in range(G):
                    ins = nc.vector.tensor_tensor(shift[:, h, :].rearrange("j (k q) -> j k q", q=QW), rows[:, h], diag[:, :, :], ALU.mult)
                ins.then_inc(shift_ready, 1)

            def add(i, u, t):
                if t not in a.dve_tiles[1:]:
                    return
                n, k = a.dve_tiles.index(t) - 1, u * NT + t
                if n == 0 and u >= 2:
                    dve.wait_ge(den_ready, i * NU + u - 1)
                dve.wait_ge(probs_ready, i * STEPS + k + 1)
                if n == 0:
                    before = prob[:, (u * NT + a.dve_tiles[0]) % RP, :]
                else:
                    before = acc_v[:, u % 2, :]
                    dve.wait_ge(added_v, summed(a.dve_tiles, i, u, n))
                nc.vector.tensor_tensor(acc_v[:, u % 2, :], before, prob[:, k % RP, :], ALU.add).then_inc(added_v, 1)

            def take_raw(i, u):
                dve.wait_ge(av_done, i * TILES + (u + 1) * NT)
                nc.vector.tensor_copy(raw[:, :], m.bank[u % 2][:, :]).then_inc(raw_ready, 1)

            def normalise(i, u):
                dve.wait_ge(den_ready, i * NU + u + 1)
                nc.vector.reciprocal(rden[:, :], m.slot[slots.index(("den", u, 0)) % 2][:, 0:QB]).then_inc(den_used, 1)
                dve.wait_ge(den_used, i * NU + u + 1)
                if not a.stacked:
                    dve.wait_ge(av_done, i * TILES + (u + 1) * NT)
                sums = raw if a.stacked else m.bank[u % 2]
                nc.vector.tensor_tensor(att[:, :], sums[:, :], rden[:, :], ALU.mult).then_inc(att_ready, 1)

            def residual(i, u):
                dve.wait_ge(out_ready, i * NU + u + 1)
                dve.wait_ge(out_used, i * NU + u + 1)
                xs = m.x[:, 4 * u:4 * u + 4, :].rearrange("p t d -> p (t d)")
                nc.vector.scalar_tensor_tensor(xs, m.slot[slots.index(("out", u, 0)) % 2][:, :], m.tg[:, a.gate:a.gate + 1], xs,
                                               ALU.mult, ALU.add).then_inc(out_used, 1)

            def pair(i, last=False):
                project(i + 1, not last, True, i)
                for u in range(NU):
                    s = 0
                    for t in range(NS):
                        if u and t == a.raw_after and a.stacked:
                            take_raw(i, u - 1)
                        if u and t == a.den_after + 1:
                            normalise(i, u - 1)
                        if u and t == a.out_after + 1:
                            residual(i, u - 1)
                        if not last:
                            for _ in range(places[t]):
                                max_step(i + 1, u, s)
                                s += 1
                            if u and t == a.turn_after:
                                shift_of_unit(i + 1, u - 1)
                        if a.stacked:
                            continue
                        if t:
                            add(i, u, t - 1)
                        elif u:
                            add(i, u - 1, NT - 1)
                    if not last:
                        max_of_unit(i + 1, u)
                if a.stacked:
                    take_raw(i, NU - 1)
                else:
                    add(i, NU - 1, NT - 1)
                normalise(i, NU - 1)
                if not last:
                    shift_of_unit(i + 1, NU - 1)
                residual(i, NU - 1)

            k0 = kn_hi
            project(0, True, False, 0)
            for u in range(NU):
                for s in range(MS):
                    max_step(0, u, s)
                max_of_unit(0, u)
                shift_of_unit(0, u)
            with dve.Fori(0, a.groups - 1) as i:
                pair(i)
            pair(a.groups - 1, last=True)

        @block.tensor
        def _(pe):
            def project(it, kq, values):
                g0 = groups_before(it)
                n = 0
                pe.wait_ge(w_split, it + 1)
                if kq:
                    for j in range(NKQ):
                        key = j < NK
                        c0, w, tokens = a.kchunks[j] if key else ((j - NK) * QB, QB, True)
                        src = (m.xh, m.xl) if tokens else (m.ch, m.cl)
                        c1 = c0 if tokens else c0 - NL * P
                        wait(pe, proj_read, g0 + n - 3 if n >= 4 else 0)
                        what = 1 if key else 0
                        steps = [(w_hi, 0), (w_hi, 1), (w_lo, 0)]
                        for q, (wt, half) in enumerate(steps):
                            for c in range(DC):
                                ins = nc.tensor.matmul(bank_of(n)[:, 0:w], weights(wt, what, c), src[half][:, c, c1:c1 + w],
                                                       start=(q == 0 and c == 0), stop=(q == 2 and c == DC - 1))
                        ins.then_inc(proj_done, 1)
                        n += 1
                if values:
                    for tiles in a.vgroups:
                        wait(pe, proj_read, g0 + n - 3 if n >= 4 else 0)
                        for z, t in enumerate(tiles):
                            src = (m.xh, m.xl) if t < NL else (m.ch, m.cl)
                            c1 = (t if t < NL else t - NL) * P
                            for q, (wt, half) in enumerate([(w_hi, 0), (w_hi, 1), (w_lo, 0)]):
                                for c in range(DC):
                                    ins = nc.tensor.matmul(bank_of(n)[:, z * P:(z + 1) * P], src[half][:, c, c1:c1 + P], weights(wt, 2, c),
                                                           start=(q == 0 and c == 0), stop=(q == 2 and c == DC - 1))
                        ins.then_inc(proj_done, 1)
                        n += 1
                return n

            max_before = [None, None]

            def max_step(it, u, s):
                c, j = s // NB, s % NB
                first, w, masked = a.mchunks[c]
                if u == 0 and s == 0:
                    pe.wait_ge(next_ready, it + 1)
                wait(pe, *wide_free(it, s % 2))
                src = (kmask if masked else kn_hi)[:, first:first + w]
                nc.tensor.matmul(wide[s % 2][:, 0:w], qdiag[:, u * NB + j, :, :].rearrange("p h q -> p (h q)"), src,
                                 start=True, stop=True).then_inc(max_ready, 1)
                max_before[s % 2] = (max_used, u * MS + s + 1)

            def wide_free(it, bank):
                held = max_before[bank]
                if held is None:
                    return shift_ready, it * NU
                sem_, n = held
                return sem_, it * (NU * MS if sem_ is max_used else NU) + n

            def turn(it, u):
                pe.wait_ge(neg_ready, it * NU + u + 1)
                wait(pe, *wide_free(it, 0))
                nc.tensor.transpose(wide[0][0:NB, 0:P], neg_max[:, :], m.ident[:, :]).then_inc(neg_turned, 1)
                max_before[0] = (shift_ready, u + 1)

            def free_slot(i, k, groups):
                if k >= 2:
                    pe.wait_ge(*consumed(k - 2, i))
                elif k == 0:
                    pe.wait_ge(proj_read, groups)

            def scores(i, u, s, k, groups):
                t, first_head = s // PAIRS, s % PAIRS * 2
                if s == 0:
                    pe.wait_ge(q_laid[u], (i + 1) * 16 * 4 * G)
                for n, (lo, _) in enumerate(a.kparts):
                    if u == 0 and s == lo * PAIRS:
                        pe.wait_ge(k_laid[n], (i + 1) * 16 * 3 * G)
                free_slot(i, k, groups)
                for z in range(2):
                    h = first_head + z
                    for n in range(n_pass):
                        ins = nc.tensor.matmul(m.slot[k % 2][:, z * QB:(z + 1) * QB], k_op[h][n][:, t * P:(t + 1) * P],
                                               q_op[h][n][:, u * QB:(u + 1) * QB], start=(n == 0), stop=(n == n_pass - 1))
                ins.then_inc(scores_ready, 1)

            def values(i, u, t, groups):
                k = (u * NT + t) * PAIRS
                if t == 0 and u >= 2:
                    pe.wait_ge(att_ready, i * NU + u - 1)
                if k == 0:
                    if a.biased:
                        pe.wait_ge(y_used, groups)
                pe.wait_ge(probs_ready, i * STEPS + k + PAIRS)
                for h in range(G):
                    r = slice(h * PITCH, (h + 1) * PITCH)
                    ins = nc.tensor.matmul(m.bank[u % 2][r, :], val[:, t, r], prob[:, (k + h // 2) % RP, h % 2 * QB:(h % 2 + 1) * QB],
                                           start=(t == 0), stop=(t == NT - 1), tile_position=(0, h * PITCH))
                ins.then_inc(av_done, 1)

            def sums(i, u, k):
                free_slot(i, k, 0)
                if a.stacked:
                    pe.wait_ge(raw_ready, i * NU + u + 1)
                    nc.tensor.matmul(m.slot[k % 2][:, 0:QB], spread[:, :], raw[:, :], start=True, stop=True).then_inc(den_ready, 1)
                    return
                pe.wait_ge(added_v, summed(a.dve_tiles, i, u + 1, 0))
                pe.wait_ge(added_p, summed(a.pool_tiles, i, u + 1, 0))
                for h in range(2):
                    for n, acc in enumerate((acc_v, acc_p)):
                        ins = nc.tensor.matmul(m.slot[k % 2][h * HALF:(h + 1) * HALF, 0:QB], ones[:, :], acc[:, u % 2, h * QB:(h + 1) * QB],
                                               start=(n == 0), stop=(n == 1))
                ins.then_inc(den_ready, 1)

            def outputs(i, u, k):
                free_slot(i, k, 0)
                if u == 0:
                    pe.wait_ge(wo_loaded, i * 16 + 16)
                pe.wait_ge(att_ready, i * NU + u + 1)
                for j in range(QB // P):
                    ins = nc.tensor.matmul(m.slot[k % 2][:, j * D:(j + 1) * D], att[:, j * P:(j + 1) * P], wo[:, :], start=True, stop=True)
                ins.then_inc(out_ready, 1)

            def pair(i, last=False):
                max_before[:] = [None, None]
                pe.wait_ge(out_used, i * NU + 1)
                project(i + 1, not last, True)
                groups = groups_before(i + 1) + (0 if last else NKQ) + NV
                k = 0
                for u in range(NU):
                    s = 0
                    for t in range(NS):
                        scores(i, u, t, k, groups)
                        k += 1
                        if not last and places[t]:
                            max_step(i + 1, u, s)
                            s += 1
                        if t % PAIRS == PAIRS - 1:
                            if t >= PAIRS:
                                values(i, u, t // PAIRS - 1, groups)
                            elif u:
                                values(i, u - 1, NT - 1, groups)
                        for _ in range(places[t] - 1 if not last else 0):
                            max_step(i + 1, u, s)
                            s += 1
                        if u and t == a.den_after:
                            sums(i, u - 1, k)
                            k += 1
                        if u and t == a.out_after:
                            outputs(i, u - 1, k)
                            k += 1
                        if u and t == a.turn_after and not last:
                            turn(i + 1, u - 1)
                values(i, NU - 1, NT - 1, groups)
                sums(i, NU - 1, k)
                k += 1
                if not last:
                    turn(i + 1, NU - 1)
                outputs(i, NU - 1, k)

            project(0, True, False)
            for u in range(NU):
                for s in range(MS):
                    max_step(0, u, s)
                turn(0, u)
            with pe.Fori(0, a.groups - 1) as i:
                pair(i)
            pair(a.groups - 1, last=True)


def stage_experts(nc, m, gate, rw_in, rb_in, w1_in, b1_in, w2_in, b2_in):
    NB = TOK // QB
    STEPS = NB * NE
    with Semaphores(nc, "moe") as sem, ExitStack() as ctx:
        def sb(name, shape, dt=FP32):
            return ctx.enter_context(nc.sbuf_tensor(f"moe_{name}", shape, dt))

        rw, rw_h, rw_l = sb("rw", [P, DC, NE]), sb("rw_hi", [P, DC, NE], FP16), sb("rw_lo", [P, DC, NE], FP16)
        w1, w1_h, w1_l = sb("w1", [P, DC, NE, EF]), sb("w1_hi", [P, DC, NE, EF], FP16), sb("w1_lo", [P, DC, NE, EF], FP16)
        w2, w2_h, w2_l = sb("w2", [P, NE, D]), sb("w2_hi", [P, NE, D], FP16), sb("w2_lo", [P, NE, D], FP16)
        b1 = sb("b1", [P, NE])
        b2, b2_h, b2_l = sb("b2", [P, D]), sb("b2_hi", [P, D], FP16), sb("b2_lo", [P, D], FP16)
        rb = sb("rb", [P, NE])
        lg, top = sb("logits", [P, NX, NE]), sb("top", [P, NX, 8])
        best, total, pair_sum = sb("best", [P, NX]), sb("total", [P, NX]), sb("pair_sum", [P, NX])
        left = sb("left", [P, NX, NE])
        wt = sb("weights", [P, NX, P])
        wt_h, wt_l = sb("wt_hi", [P, TOK], FP16), sb("wt_lo", [P, TOK], FP16)
        pick = sb("pick", [P, NE, P], FP16)
        h = sb("hidden", [P, 2, QB])
        y, y_h, y_l = sb("y", [P, 2, QB]), sb("y_hi", [P, 2, QB], FP16), sb("y_lo", [P, 2, QB], FP16)
        tgs = sb("gate_scaled", [P, 1])
        loaded, zeroed, w_hi_done, w_ready = sem("loaded"), sem("zeroed"), sem("w_hi_done"), sem("w_ready")
        routed, exp_done, dvec = sem("routed"), sem("exp_done"), sem("dve_chain")
        wt_turned, wt_read, wt_ready = sem("wt_turned"), sem("wt_read"), sem("wt_ready")
        shifted = sem("logits_shifted")
        weights_done = sem("weights_done")
        h_ready, h_done, spread_ready = sem("h_ready"), sem("h_done"), sem("spread_ready")
        y_done, yh_done, yl_done = sem("y_done"), sem("yh_done"), sem("yl_done")
        step_used, out_used = sem("step_used"), sem("out_used")
        block = ctx.enter_context(nc.Block())
        hbank = lambda n: m.slot[0][:, (n % 2) * 512:(n % 2) * 512 + 512]
        sbank = lambda n: m.slot[1][:, (n % 2) * 512:(n % 2) * 512 + 512]
        obank = lambda b, z: m.wide[:, z * 512:z * 512 + 512] if b % 2 == 0 else m.bank[z][:, :]
        splits = [(rw, rw_h, rw_l, WSCALE), (b2, b2_h, b2_l, WSCALE), (w1, w1_h, w1_l, WSCALE), (w2, w2_h, w2_l, WSCALE)]

        def flat(t):
            return t[:] if len(t.shape) == 2 else t[:].rearrange("p a b -> p (a b)") if len(t.shape) == 3 else t[:].rearrange("p a b c -> p (a b c)")

        @block.sync
        def _(sp):
            sp.wait_ge(zeroed, 1)
            sp.dma_start(rw[:, :, :], rw_in.rearrange("(c p) e -> p c e", p=P)).then_inc(loaded, 16)
            sp.dma_start(b2[0:NE, :], b2_in).then_inc(loaded, 16)
            sp.dma_start(b1[:, :], b1_in).then_inc(loaded, 16)
            sp.dma_start(rb[:, :], rb_in[0:1, :].broadcast_to([P, NE])).then_inc(loaded, 16)
            for c in range(DC):
                sp.dma_start(w1[:, c, :, :], w1_in[:, c * P:(c + 1) * P, :].rearrange("e p f -> p e f")).then_inc(loaded, 16)
            sp.dma_start(w2[:, :, :], w2_in.rearrange("e f d -> f e d")).then_inc(loaded, 16)

        @block.gpsimd
        def _(pool):
            for n, (w, hi, lo, _) in enumerate(splits):
                pool.wait_ge(w_hi_done, 2 * n + 2)
                nc.gpsimd.tensor_tensor(flat(lo), flat(w), flat(hi), ALU.subtract).then_inc(w_ready, 1)

        @block.scalar
        def _(act):
            act.wait_ge(loaded, 16 * 7)
            for n, (w, hi, lo, s) in enumerate(splits):
                nc.scalar.activation(flat(w), flat(w), ACT.Copy, scale=s).then_inc(w_hi_done, 1)
                act.wait_ge(w_hi_done, 2 * n + 1)
                nc.scalar.activation(flat(hi), flat(w), ACT.Copy).then_inc(w_hi_done, 1)
            act.wait_ge(shifted, 1)
            nc.scalar.activation(flat(lg), flat(lg), ACT.Exp).then_inc(exp_done, 1)
            for g in range(NB):
                act.wait_ge(wt_turned, g + 1)
                nc.scalar.activation(wt_h[:, g * QB:(g + 1) * QB], sbank(g), ACT.Copy).then_inc(wt_read, 1)
            for n in range(STEPS):
                e = n % NE
                act.wait_ge(h_ready, n + 1)
                if n >= 2:
                    act.wait_ge(y_done, n - 1)
                nc.scalar.activation(h[:, n % 2, :], hbank(n), ACT.Gelu, bias=b1[:, e:e + 1], scale=1.0 / WSCALE).then_inc(h_done, 1)
                act.wait_ge(y_done, n + 1)
                if n >= 2:
                    act.wait_ge(step_used, n - 1)
                nc.scalar.activation(y_h[:, n % 2, :], y[:, n % 2, :], ACT.Copy).then_inc(yh_done, 1)

        @block.vector
        def _(dve):
            chain = [0]

            def link(ins):
                chain[0] += 1
                ins.then_inc(dvec, 1)
                dve.wait_ge(dvec, chain[0])

            nc.vector.memset(b2[:, :], 0.0).then_inc(zeroed, 1)
            nc.vector.memset(wt[:, :, :], 0.0)
            for e in range(NE):
                nc.vector.tensor_copy(pick[:, e, :], m.ident[:, e:e + 1].broadcast_to([P, P]))
            link(nc.vector.tensor_scalar(tgs[:, :], m.tg[:, gate:gate + 1], 1.0 / WSCALE, None, ALU.mult))
            dve.wait_ge(loaded, 16 * 7)
            dve.wait_ge(routed, 1)
            logits = hbank(0)[:, 0:NX * NE].rearrange("p (t e) -> p t e", e=NE)
            rbb = rb[:, :].rearrange("p (o e) -> p o e", o=1).broadcast_to([P, NX, NE])
            link(nc.vector.scalar_tensor_tensor(lg[:, :, :], logits, 1.0 / WSCALE, rbb, ALU.mult, ALU.add))
            link(nc.vector.reduce_max(best[:, :], lg[:, :, :], AX.X))
            col = lambda t: t[:, :].rearrange("p (t o) -> p t o", o=1).broadcast_to([P, NX, NE])
            nc.vector.tensor_tensor(lg[:, :, :], lg[:, :, :], col(best), ALU.subtract).then_inc(shifted, 1)
            dve.wait_ge(exp_done, 1)
            link(nc.vector.reduce_sum(total[:, :], lg[:, :, :], AX.X))
            link(nc.vector.reciprocal(total[:, :], total[:, :]))
            link(nc.vector.tensor_tensor(lg[:, :, :], lg[:, :, :], col(total), ALU.mult))
            for t in range(NX):
                ins = nc.vector.max(top[:, t, :], lg[:, t, :])
            link(ins)
            link(nc.vector.tensor_tensor(pair_sum[:, :], top[:, :, 0], top[:, :, 1], ALU.add))
            link(nc.vector.reciprocal(pair_sum[:, :], pair_sum[:, :]))
            link(nc.vector.memset(top[:, :, 2:8], -1.0))
            for t in range(NX):
                ins = nc.vector.match_replace(left[:, t, :], top[:, t, :], lg[:, t, :], -2.0)
            link(ins)
            link(nc.vector.tensor_scalar(left[:, :, :], left[:, :, :], -1.5, None, ALU.is_lt))
            link(nc.vector.tensor_tensor(left[:, :, :], left[:, :, :], lg[:, :, :], ALU.mult))
            nc.vector.tensor_tensor(wt[:, :, 0:NE], left[:, :, :], col(pair_sum), ALU.mult).then_inc(weights_done, 1)
            for g in range(NB):
                dve.wait_ge(wt_read, g + 1)
                nc.vector.tensor_tensor(wt_l[:, g * QB:(g + 1) * QB], sbank(g), wt_h[:, g * QB:(g + 1) * QB],
                                        ALU.subtract).then_inc(wt_ready, 1)

            def residual(b):
                dve.wait_ge(step_used, (b + 1) * NE)
                for z in range(2):
                    xs = m.x[:, 4 * b + 2 * z:4 * b + 2 * z + 2, :].rearrange("p t d -> p (t d)")
                    ins = nc.vector.scalar_tensor_tensor(xs, obank(b, z), tgs[:, 0:1], xs, ALU.mult, ALU.add)
                ins.then_inc(out_used, 1)

            for n in range(STEPS):
                b, e = divmod(n, NE)
                dve.wait_ge(h_done, n + 1)
                dve.wait_ge(spread_ready, n + 1)
                nc.vector.tensor_tensor(y[:, n % 2, :], sbank(n), h[:, n % 2, :], ALU.mult).then_inc(y_done, 1)
                dve.wait_ge(yh_done, n + 1)
                nc.vector.tensor_tensor(y_l[:, n % 2, :], y[:, n % 2, :], y_h[:, n % 2, :], ALU.subtract).then_inc(yl_done, 1)
                if b and e == 1:
                    residual(b - 1)
            residual(NB - 1)

        @block.tensor
        def _(pe):
            pe.wait_ge(w_ready, 1)
            for t in range(NX):
                q = 0
                for wv, half in ((rw_h, m.xh), (rw_h, m.xl), (rw_l, m.xh)):
                    for c in range(DC):
                        ins = nc.tensor.matmul(hbank(0)[:, t * NE:(t + 1) * NE], half[:, c, t * P:(t + 1) * P], wv[:, c, :],
                                               start=(q == 0), stop=(q == 5))
                        q += 1
            ins.then_inc(routed, 1)

            def first(n):
                b, e = divmod(n, NE)
                if n >= 2:
                    pe.wait_ge(h_done, n - 1)
                elif n == 0:
                    pe.wait_ge(shifted, 1)
                    pe.wait_ge(w_ready, len(splits))
                q = 0
                for wv, half in ((w1_h, m.xh), (w1_h, m.xl), (w1_l, m.xh)):
                    for c in range(DC):
                        ins = nc.tensor.matmul(hbank(n), wv[:, c, e, :], half[:, c, b * QB:(b + 1) * QB], start=(q == 0), stop=(q == 5))
                        q += 1
                ins.then_inc(h_ready, 1)

            def spread(n):
                b, e = divmod(n, NE)
                if n >= 2:
                    pe.wait_ge(y_done, n - 1)
                for q, half in enumerate((wt_h, wt_l)):
                    ins = nc.tensor.matmul(sbank(n), pick[:, e, :], half[:, b * QB:(b + 1) * QB], start=(q == 0), stop=(q == 1))
                ins.then_inc(spread_ready, 1)

            def second(n):
                b, e = divmod(n, NE)
                if e == 0:
                    if b >= 2:
                        pe.wait_ge(out_used, b - 1)
                    for j in range(4):
                        for q, (half, bv) in enumerate(((wt_h, b2_h), (wt_h, b2_l), (wt_l, b2_h))):
                            nc.tensor.matmul(obank(b, j // 2)[:, (j % 2) * D:(j % 2 + 1) * D],
                                             half[:, b * QB + j * P:b * QB + (j + 1) * P], bv[:, :],
                                             start=(q == 0 and j % 2 == 0), stop=False, skip_group_check=True)
                pe.wait_ge(yl_done, n + 1)
                for j in range(4):
                    for q, (half, wv) in enumerate(((y_h, w2_h), (y_h, w2_l), (y_l, w2_h))):
                        ins = nc.tensor.matmul(obank(b, j // 2)[:, (j % 2) * D:(j % 2 + 1) * D],
                                               half[:, n % 2, j * P:(j + 1) * P], wv[:, e, :],
                                               start=False, stop=(e == NE - 1 and q == 2), skip_group_check=True)
                ins.then_inc(step_used, 1)

            first(0)
            first(1)
            pe.wait_ge(weights_done, 1)
            for g in range(NB):
                if g >= 2:
                    pe.wait_ge(wt_ready, g - 1)
                for j in range(4):
                    ins = nc.tensor.transpose(sbank(g)[:, j * P:(j + 1) * P], wt[:, 4 * g + j, :], m.ident[:, :])
                ins.then_inc(wt_turned, 1)
            pe.wait_ge(wt_ready, NB)
            spread(0)
            for n in range(STEPS):
                if n + 1 < STEPS:
                    if n >= 1:
                        first(n + 1)
                    spread(n + 1)
                second(n)


def stage_quantised(nc, m, xn, gate, wg_in, wu_in, wd_in):
    KF = FF // P
    with Semaphores(nc, "ffn") as sem, ExitStack() as ctx:
        def sb(name, shape, dt=FP32):
            return ctx.enter_context(nc.sbuf_tensor(f"ffn_{name}", shape, dt))

        wf = [sb(f"w{n}", [P, 2048]) for n in range(3)]
        wq = [sb(f"wq{n}", [P, 2048], BF16) for n in range(3)]
        ones = sb("ones", [P, P])
        wsum, wmean, wscale = sb("wsum", [P, 3]), sb("wmean", [P, 3]), sb("wscale", [P, 3])
        amax, ascale, adq = sb("amax", [P, NX]), sb("ascale", [P, NX]), sb("adq", [P, NX])
        gs, us = sb("gate_scale", [P, NX]), sb("up_scale", [P, NX])
        xi = sb("xi", [P, 2, D])
        xt = sb("xt", [P, 2, DC, P], BF16)
        sg = sb("silu", [P, 2, FF])
        hh = sb("h", [P, 2, FF])
        hmax, hscale, hdq = sb("hmax", [P, 2]), sb("hscale", [P, 2]), sb("hdq", [P, 2])
        ht = sb("ht", [P, 2, KF, P], BF16)
        w_loaded, dvec, wsum_done, wmean_done, wq_done = sem("w_loaded"), sem("dve_chain"), sem("wsum_done"), sem("wmean_done"), sem("wq_done")
        xi_ready, xt_turned, xt_ready = sem("xi_ready"), sem("xt_turned"), sem("xt_ready")
        gate_ready, up_ready, silu_done, h_done = sem("gate_ready"), sem("up_ready"), sem("silu_done"), sem("h_done")
        hi_ready, h_turned, ht_ready, down_ready, x_done = sem("hi_ready"), sem("h_turned"), sem("ht_ready"), sem("down_ready"), sem("x_done")
        scales_ready = sem("scales_ready")
        block = ctx.enter_context(nc.Block())

        @block.sync
        def _(sp):
            for n, w in enumerate((wg_in, wu_in)):
                sp.dma_start(wf[n][:, :].rearrange("p (c f) -> p c f", c=DC), w.rearrange("(c p) f -> p c f", p=P)).then_inc(w_loaded, 16)
            sp.dma_start(wf[2][:, :].rearrange("p (k d) -> p k d", k=KF), wd_in.rearrange("(k p) d -> p k d", p=P)).then_inc(w_loaded, 16)

        @block.vector
        def _(dve):
            chain = [0]

            def link(ins):
                chain[0] += 1
                ins.then_inc(dvec, 1)
                dve.wait_ge(dvec, chain[0])

            nc.vector.memset(ones[:, :], 1.0)
            dve.wait_ge(w_loaded, 48)
            for n in range(3):
                ins = nc.vector.tensor_reduce(wsum[:, n:n + 1], wf[n][:, :], AX.X, ALU.add, apply_absolute_value=True)
            ins.then_inc(wsum_done, 1)
            for t in range(NX):
                ins = nc.vector.tensor_reduce(amax[:, t:t + 1], xn[:, t, :], AX.X, ALU.max, apply_absolute_value=True)
            link(ins)
            link(nc.vector.tensor_scalar(amax[:, :], amax[:, :], 1e-5, None, ALU.max))
            link(nc.vector.reciprocal(ascale[:, :], amax[:, :]))
            nc.vector.tensor_scalar(ascale[:, :], ascale[:, :], 127.0, None, ALU.mult)
            link(nc.vector.tensor_scalar(adq[:, :], amax[:, :], 1.0 / 127.0, None, ALU.mult))
            dve.wait_ge(wmean_done, 1)
            link(nc.vector.tensor_scalar(wmean[:, :], m.bank[0][:, 0:3], 1.0 / (FF * D), 1e-5, ALU.mult, ALU.max))
            link(nc.vector.reciprocal(wscale[:, :], wmean[:, :]))
            nc.vector.tensor_scalar(gs[:, :], adq[:, :], wmean[:, 0:1], None, ALU.mult)
            nc.vector.tensor_scalar(us[:, :], adq[:, :], wmean[:, 1:2], None, ALU.mult).then_inc(scales_ready, 1)
            for n in range(3):
                link(nc.vector.tensor_scalar(wf[n][:, :], wf[n][:, :], wscale[:, n:n + 1], ROUND, ALU.mult, ALU.add))
                link(nc.vector.tensor_scalar(wf[n][:, :], wf[n][:, :], ROUND, 1.0, ALU.subtract, ALU.min))
                nc.vector.tensor_scalar(wq[n][:, :], wf[n][:, :], -1.0, None, ALU.max).then_inc(wq_done, 1)

            def quantise_x(t):
                link(nc.vector.tensor_scalar(xi[:, t % 2, :], xn[:, t, :], ascale[:, t:t + 1], ROUND, ALU.mult, ALU.add))
                nc.vector.tensor_scalar(xi[:, t % 2, :], xi[:, t % 2, :], ROUND, 127.0, ALU.subtract, ALU.min).then_inc(xi_ready, 1)

            def take_x(t):
                dve.wait_ge(xt_turned, t + 1)
                nc.vector.tensor_scalar(xt[:, t % 2, :, :].rearrange("p c q -> p (c q)"), m.bank[0][:, 0:D], -128.0, None, ALU.max).then_inc(xt_ready, 1)

            def residual(t):
                dve.wait_ge(down_ready, t + 1)
                nc.vector.scalar_tensor_tensor(m.x[:, t, :], m.bank[1][:, 0:D], hdq[:, t % 2:t % 2 + 1], m.x[:, t, :], ALU.mult, ALU.add).then_inc(x_done, 1)

            quantise_x(0)
            take_x(0)
            for t in range(NX):
                if t + 1 < NX:
                    quantise_x(t + 1)
                    take_x(t + 1)
                dve.wait_ge(up_ready, t + 1)
                dve.wait_ge(silu_done, t + 1)
                nc.vector.scalar_tensor_tensor(hh[:, t % 2, :], m.slot[1][:, :], us[:, t:t + 1], sg[:, t % 2, :],
                                               ALU.mult, ALU.mult).then_inc(h_done, 1)
                dve.wait_ge(h_done, t + 1)
                if t:
                    residual(t - 1)
                mx = hmax[:, t % 2:t % 2 + 1]
                link(nc.vector.tensor_reduce(mx, hh[:, t % 2, :], AX.X, ALU.max, apply_absolute_value=True))
                link(nc.vector.tensor_scalar(mx, mx, 1e-5, None, ALU.max))
                link(nc.vector.reciprocal(hscale[:, t % 2:t % 2 + 1], mx))
                link(nc.vector.tensor_scalar(hscale[:, t % 2:t % 2 + 1], hscale[:, t % 2:t % 2 + 1], 127.0, None, ALU.mult))
                link(nc.vector.tensor_scalar(hdq[:, t % 2:t % 2 + 1], mx, 1.0 / 127.0, wmean[:, 2:3], ALU.mult, ALU.mult))
                link(nc.vector.tensor_scalar(hdq[:, t % 2:t % 2 + 1], hdq[:, t % 2:t % 2 + 1], m.tg[:, gate:gate + 1], None, ALU.mult))
                link(nc.vector.tensor_scalar(hh[:, t % 2, :], hh[:, t % 2, :], hscale[:, t % 2:t % 2 + 1], ROUND, ALU.mult, ALU.add))
                nc.vector.tensor_scalar(hh[:, t % 2, :], hh[:, t % 2, :], ROUND, 127.0, ALU.subtract, ALU.min).then_inc(hi_ready, 1)
            residual(NX - 1)

        def take_h(t, act):
            act.wait_ge(h_turned, t + 1)
            if t >= 2:
                act.wait_ge(down_ready, t - 1)
            nc.scalar.activation(ht[:, t % 2, :, :].rearrange("p k q -> p (k q)"), m.wide[:, :], ACT.Copy).then_inc(ht_ready, 1)

        @block.scalar
        def _(act):
            act.wait_ge(scales_ready, 1)
            for t in range(NX):
                act.wait_ge(gate_ready, t + 1)
                if t >= 2:
                    act.wait_ge(h_done, t - 1)
                nc.scalar.activation(sg[:, t % 2, :], m.slot[0][:, :], ACT.Silu, scale=gs[:, t:t + 1]).then_inc(silu_done, 1)
                if t:
                    take_h(t - 1, act)
            take_h(NX - 1, act)

        @block.tensor
        def _(pe):
            pe.wait_ge(wsum_done, 1)
            nc.tensor.matmul(m.bank[0][:, 0:3], ones[:, :], wsum[:, :], start=True, stop=True).then_inc(wmean_done, 1)

            def turn_x(t):
                pe.wait_ge(xi_ready, t + 1)
                pe.wait_ge(scales_ready, 1) if t == 0 else pe.wait_ge(xt_ready, t)
                for c in range(DC):
                    ins = nc.tensor.transpose(m.bank[0][:, c * P:(c + 1) * P], xi[:, t % 2, c * P:(c + 1) * P], m.ident[:, :])
                ins.then_inc(xt_turned, 1)

            def gate_up(t):
                pe.wait_ge(xt_ready, t + 1)
                for n, (slot, used, ready) in enumerate(((m.slot[0], silu_done, gate_ready), (m.slot[1], h_done, up_ready))):
                    if t == 0:
                        pe.wait_ge(wq_done, n + 1)
                    else:
                        pe.wait_ge(used, t)
                    for z in range(2):
                        for c in range(DC):
                            ins = nc.tensor.matmul(slot[:, z * 512:(z + 1) * 512], xt[:, t % 2, c, :],
                                                   wq[n][:, c * FF + z * 512:c * FF + (z + 1) * 512], start=(c == 0), stop=(c == DC - 1))
                    ins.then_inc(ready, 1)

            def turn_h(t):
                pe.wait_ge(hi_ready, t + 1)
                if t:
                    pe.wait_ge(ht_ready, t)
                for k in range(KF):
                    ins = nc.tensor.transpose(m.wide[:, k * P:(k + 1) * P], hh[:, t % 2, k * P:(k + 1) * P], m.ident[:, :])
                ins.then_inc(h_turned, 1)

            def down(t):
                pe.wait_ge(ht_ready, t + 1)
                if t == 0:
                    pe.wait_ge(wq_done, 3)
                else:
                    pe.wait_ge(x_done, t)
                for k in range(KF):
                    ins = nc.tensor.matmul(m.bank[1][:, 0:D], ht[:, t % 2, k, :], wq[2][:, k * D:(k + 1) * D], start=(k == 0), stop=(k == KF - 1))
                ins.then_inc(down_ready, 1)

            turn_x(0)
            gate_up(0)
            for t in range(NX):
                if t + 1 < NX:
                    turn_x(t + 1)
                    gate_up(t + 1)
                turn_h(t)
                down(t)


def stage_context(nc, m, ctxt_in):
    with Semaphores(nc, "context") as sem, ExitStack() as ctx:
        c32 = ctx.enter_context(nc.sbuf_tensor("ctx_t", [P, DC, CTXP], FP32))
        loaded = sem("ctxt_loaded")
        padded = sem("ctxt_padded")
        hi_done = sem("ctxt_hi")
        block = ctx.enter_context(nc.Block())

        @block.sync
        def _(sp):
            sp.dma_start(c32[:, :, 0:CTX], ctxt_in.rearrange("(c p) t -> p c t", p=P)).then_inc(loaded, 16)

        @block.gpsimd
        def _(pool):
            nc.gpsimd.memset(c32[:, :, CTX:CTXP], 0.0).then_inc(padded, 1)

        @block.vector
        def _(dve):
            dve.wait_ge(loaded, 16)
            dve.wait_ge(padded, 1)
            for c in range(DC):
                nc.vector.tensor_copy(m.ch[:, c, :], c32[:, c, :]).then_inc(hi_done, 1)
            for c in range(DC):
                dve.wait_ge(hi_done, c + 1)
                nc.vector.tensor_tensor(m.cl[:, c, :], c32[:, c, :], m.ch[:, c, :], ALU.subtract)


def stage_store(nc, m, out):
    with Semaphores(nc, "store") as sem, ExitStack() as ctx:
        stored = sem("stored")
        block = ctx.enter_context(nc.Block())

        @block.sync
        def _(sp):
            sp.dma_start(out.rearrange("(t p) d -> p t d", p=P), m.x[:, :, :]).then_inc(stored, 16)
            sp.wait_ge(stored, 16)


def flamingo_kernel(nc, t, out, stages=4):
    with ExitStack() as ctx:
        m = allocate(nc, ctx)
        stage_setup(nc, m, t["x"], t["gates"])
        if stages >= 1:
            with nc.sbuf_tensor("ctx_rows", [P, NCT, D], FP32) as rows:
                stage_norm(nc, m, "nc0", rows, NCT, m.ch, m.cl, affine=t["gb1"], load=t["ctx"])
            stage_norm(nc, m, "nx0", m.x, NX, m.xh, m.xl, norms=2, affine=t["gb2"])
            stage_attention(nc, m, Attention("a0", True, 64, 2, 0.125, False, 0), t["w0"], t["wo0"], (t["mask_row"], t["mask_cols"]))
        if stages >= 2:
            stage_norm(nc, m, "nx1", m.x, NX, m.xh, m.xl)
            stage_experts(nc, m, 2, t["rw"], t["rb"], t["w1"], t["eb1"], t["w2"], t["eb2"])
        if stages >= 3:
            stage_norm(nc, m, "nx2", m.x, NX, m.xh, m.xl)
            stage_context(nc, m, t["ctxt"])
            stage_attention(nc, m, Attention("a1", False, 16, 4, 0.25, True, 1), t["w1a"], t["wo1"], (t["all_row"], t["all_cols"]),
                            t["bv"], t["bo"])
        if stages >= 4:
            with nc.sbuf_tensor("xn_rows", [P, NX, D], FP32) as rows:
                stage_norm(nc, m, "nx3", m.x, NX, rows=rows)
                stage_quantised(nc, m, rows, 3, t["wg"], t["wu"], t["wd"])
        stage_store(nc, m, out)


def lay_out(x, ctx_1024, mask_BxS2_bk0, g_xattn, g_ffn, L0_xattn_g1, L0_xattn_b1, L0_xattn_g2, L0_xattn_b2, L0_xattn_Wq,
            L0_xattn_Wkv, L0_xattn_Wout, L0_ffn_router_w, L0_ffn_router_b, L0_ffn_W1, L0_ffn_b1, L0_ffn_W2, L0_ffn_b2,
            L1_xattn_Wq, L1_xattn_bq, L1_xattn_Wk, L1_xattn_bk, L1_xattn_Wv, L1_xattn_bv, L1_xattn_Wo, L1_xattn_bo,
            L1_ffn_w_gate, L1_ffn_w_up, L1_ffn_w_down):
    import numpy as np

    def iterations(wq, wk, wv, *biases):
        n = wq.shape[1] // P

        def blocks(w):
            return w.reshape(DC, P, n, P).transpose(2, 1, 0, 3)
        out = np.zeros((n + 1, P, 3, DC, P), wq.dtype)
        out[:n, :, 0] = blocks(wq)
        out[:n, :, 1] = blocks(wk)
        out[1:, :, 2] = blocks(wv)
        out = out.reshape(n + 1, P, 3 * DC * P)
        if biases:
            own = np.zeros((n + 1, P, 2), wq.dtype)
            for j, b in enumerate(biases):
                own[:n, :, j] = b.reshape(n, P)
            out = np.concatenate([out, own], axis=2)
        return out

    def pad_heads(a):
        out = np.zeros((*a.shape[:-1], 16, 32), a.dtype)
        out[..., :16] = a.reshape(*a.shape[:-1], 16, 16)
        return out.reshape(*a.shape[:-1], 16 * 32)

    def columns(*rows):
        return np.stack([r.reshape(-1, P).T for r in rows], axis=1)

    def pad_mask(mask):
        row = np.zeros((1, CTXP), bool)
        row[:, :CTX] = mask
        return row, row.reshape(NCT, P).T

    mask_row, mask_cols = pad_mask(mask_BxS2_bk0)
    all_row, all_cols = pad_mask(np.ones((1, CTX), bool))
    inner = L0_xattn_Wq.shape[1]
    return {
        "x": x[0], "ctx": ctx_1024[0], "ctxt": ctx_1024[0].T, "mask_row": mask_row, "mask_cols": mask_cols,
        "all_row": all_row, "all_cols": all_cols,
        "gates": np.stack([g_xattn[0], g_xattn[1], g_ffn[0], g_ffn[1]])[None],
        "gb1": columns(L0_xattn_g1, L0_xattn_b1), "gb2": columns(L0_xattn_g2, L0_xattn_b2),
        "w0": iterations(L0_xattn_Wq, L0_xattn_Wkv[:, :inner], L0_xattn_Wkv[:, inner:]),
        "wo0": L0_xattn_Wout.reshape(-1, P, D),
        "rw": L0_ffn_router_w, "rb": L0_ffn_router_b[None], "w1": L0_ffn_W1, "eb1": L0_ffn_b1.T, "w2": L0_ffn_W2, "eb2": L0_ffn_b2,
        "w1a": iterations(pad_heads(L1_xattn_Wq.T), pad_heads(L1_xattn_Wk.T), pad_heads(L1_xattn_Wv.T),
                          pad_heads(L1_xattn_bq), pad_heads(L1_xattn_bk)),
        "wo1": pad_heads(L1_xattn_Wo).T.reshape(-1, P, D),
        "bv": pad_heads(L1_xattn_bv)[None], "bo": L1_xattn_bo[None],
        "wg": L1_ffn_w_gate.T, "wu": L1_ffn_w_up.T, "wd": L1_ffn_w_down.T,
    }


def kernel(**inputs):
    import numpy as np
    import concourse.bacc as bacc
    from concourse.bass_utils import run_bass_kernel_spmd

    arrays = {f"in_{k}": np.ascontiguousarray(v) for k, v in lay_out(**{k: np.asarray(v) for k, v in inputs.items()}).items()}
    nc = bacc.Bacc("TRN2", target_bir_lowering=False, num_devices=1)
    t = {k[3:]: nc.dram_tensor(k, v.shape, mybir.dt.from_np(v.dtype), kind="ExternalInput").ap() for k, v in arrays.items()}
    out = nc.dram_tensor("out_x", (TOK, D), FP32, kind="ExternalOutput").ap()
    flamingo_kernel(nc, t, out)
    result = run_bass_kernel_spmd(nc, [arrays], core_ids=[0])
    return result.results[0]["out_x"].reshape(1, TOK, D)
```

```python
import concourse.bass as bass
from concourse import mybir
from contextlib import ExitStack

FP32 = mybir.dt.float32
FP16 = mybir.dt.float16
BF16 = mybir.dt.bfloat16
ALU = mybir.AluOpType
ACT = mybir.ActivationFunctionType
AX = mybir.AxisListType

P = 128
D = 256
DC = D // P
TOK = 2048
NX = TOK // P
CTX = 1601
NCT = -(-CTX // P)
CTXP = NCT * P
CTX_LAST = CTX - (NCT - 1) * P
QB = 512
NU = TOK // QB
HALF = P // 2
EPS = 1e-5
WSCALE = 16.0
MASKED = -1e30
RY = 3
AHEAD = 2
NEXT_AT = NU - AHEAD
LATE = 4
NE, EF = 8, 128
FF = 1024
ROUND = 1.5 * 2.0 ** 23


def wait(eng, sem, value):
    if not isinstance(value, int) or value > 0:
        eng.wait_ge(sem, value)


def split_even(n, parts):
    return [(j + 1) * n // parts - j * n // parts for j in range(parts)]


class Semaphores:

    def __init__(self, nc, tag):
        self.nc, self.tag, self.all = nc, tag, []

    def __call__(self, name):
        self.all.append(self.nc.alloc_semaphore(f"{self.tag}_{name}"))
        return self.all[-1]

    def __enter__(self):
        return self

    def __exit__(self, kind, *rest):
        if kind is None:
            self.nc.clear_and_free_semaphores(self.all)
            self.nc.all_engine_barrier()


class Memory:
    pass


def allocate(nc, ctx):
    m = Memory()

    def sb(name, shape, dt=FP32):
        return ctx.enter_context(nc.sbuf_tensor(name, shape, dt))

    m.x = sb("x_res", [P, NX, D])
    m.xh = sb("xt_hi", [P, DC, TOK], FP16)
    m.xl = sb("xt_lo", [P, DC, TOK], FP16)
    m.ch = sb("ct_hi", [P, DC, CTXP], FP16)
    m.cl = sb("ct_lo", [P, DC, CTXP], FP16)
    m.ident = sb("ident", [P, P])
    m.tg = sb("tanh_gates", [P, 4])
    m.slot = [ctx.enter_context(nc.psum_tensor(f"slot{n}", [P, 1024], FP32)) for n in range(2)]
    m.bank = [ctx.enter_context(nc.psum_tensor(f"bank{n}", [P, 512], FP32)) for n in range(2)]
    m.wide = ctx.enter_context(nc.psum_tensor("wide", [P, 1024], FP32))
    return m


def stage_setup(nc, m, x_in, gates_in, rows, ctx_in):
    with Semaphores(nc, "setup") as sem, ExitStack() as ctx:
        gates = ctx.enter_context(nc.sbuf_tensor("gates_raw", [P, 4], FP32))
        x_in_sem = sem("x_loaded")
        gates_sem = sem("gates_loaded")
        zeroed = sem("identity_zeroed")
        padded, ctx_loaded = sem("padded"), sem("context_loaded")
        block = ctx.enter_context(nc.Block())

        @block.sync
        def _(sp):
            sp.dma_start(gates[:, :], gates_in[0:1, :].broadcast_to([P, 4])).then_inc(gates_sem, 16)
            sp.dma_start(m.x[:, :, :], x_in.rearrange("(t p) d -> p t d", p=P)).then_inc(x_in_sem, 16)
            full = (NCT - 1) * P
            sp.dma_start(rows[:, 0:NCT - 1, :], ctx_in[0:full, :].rearrange("(t p) d -> p t d", p=P)).then_inc(ctx_loaded, 16)
            sp.wait_ge(padded, 1)
            sp.dma_start(rows[0:CTX_LAST, NCT - 1, :], ctx_in[full:full + CTX_LAST, :]).then_inc(ctx_loaded, 16)
            sp.wait_ge(x_in_sem, 16)
            sp.wait_ge(ctx_loaded, 32)

        @block.gpsimd
        def _(pool):
            nc.gpsimd.memset(rows[:, NCT - 1, :], 0.0).then_inc(padded, 1)
            nc.gpsimd.memset(m.ident[:, :], 0.0).then_inc(zeroed, 1)
            pool.wait_ge(zeroed, 1)
            nc.gpsimd.affine_select(out=m.ident[:, :], in_=m.ident[:, :], compare_op=ALU.not_equal, fill=1.0,
                                    base=0, pattern=[[-1, P]], channel_multiplier=1)

        @block.scalar
        def _(act):
            act.wait_ge(gates_sem, 16)
            nc.scalar.activation(m.tg[:, :], gates[:, :], ACT.Tanh)


def stage_norm(nc, m, tag, src, nt, hi=None, lo=None, norms=1, affine=None, rows=None, ahead_of_use=(), context=None):
    groups = [list(range(a, min(a + 4, nt))) for a in range(0, nt, 4)] if rows is None else []
    with Semaphores(nc, tag) as sem, ExitStack() as ctx:
        def sb(name, shape, dt=FP32):
            return ctx.enter_context(nc.sbuf_tensor(f"{tag}_{name}", shape, dt))

        stats = sb("stats", [P, nt, 6])
        mv = sb("mv", [P, nt, 2])
        std = sb("std", [P, nt])
        rstd = sb("rstd", [P, nt])
        var2 = sb("var2", [P, nt])
        eps = sb("eps", [P, 1])
        xn = sb("xn", [P, nt, D]) if rows is None else rows
        y = sb("y", [P, 2, 512])
        gb = sb("gb", [P, 2, DC])
        gb_loaded = sem("gb_loaded")
        eps_set, stats_done = sem("eps_set"), sem("stats_done")
        var2_done = sem("var2_done")
        aggregated, std_done, rstd_done, normed = sem("aggregated"), sem("std_done"), sem("rstd_done"), sem("normed")
        turned, y_ready, hi_done, lo_done = sem("turned"), sem("y_ready"), sem("hi_done"), sem("lo_done")
        block = ctx.enter_context(nc.Block())

        if context is not None:
            c32 = sb("context", [P, DC, CTXP])
        fetched, c_loaded, c_padded, c_hi = sem("fetched"), sem("context_loaded"), sem("context_padded"), sem("context_hi")

        @block.gpsimd
        def _(pool):
            if context is None:
                return
            nc.gpsimd.memset(c32[:, :, CTX:CTXP], 0.0).then_inc(c_padded, 1)
            pool.wait_ge(c_padded, 1)
            pool.wait_ge(c_loaded, 16)
            for c in range(DC):
                nc.gpsimd.tensor_copy(m.ch[:, c, :], c32[:, c, :]).then_inc(c_hi, 1)
            for c in range(DC):
                pool.wait_ge(c_hi, c + 1)
                nc.gpsimd.tensor_tensor(m.cl[:, c, :], c32[:, c, :], m.ch[:, c, :], ALU.subtract)

        @block.sync
        def _(sp):
            if context is not None:
                sp.dma_start(c32[:, :, 0:CTX], context.rearrange("(c p) t -> p c t", p=P)).then_inc(c_loaded, 16)
            for dst, source in ahead_of_use:
                sp.dma_start(dst, source).then_inc(fetched, 16)
            wait(sp, fetched, 16 * len(ahead_of_use))
            if affine is not None:
                sp.dma_start(gb[:, :, :], affine).then_inc(gb_loaded, 16)

        @block.vector
        def _(dve):
            nc.vector.memset(eps[:, :], EPS).then_inc(eps_set, 1)
            for t in range(nt):
                nc.vector.bn_stats(stats[:, t, :], src[:, t, :]).then_inc(stats_done, 1)
            for t in range(nt):
                dve.wait_ge(stats_done, t + 1)
                nc.vector.bn_aggr(mv[:, t, :], stats[:, t, :]).then_inc(aggregated, 1)
            dve.wait_ge(std_done, 1)
            nc.vector.reciprocal(rstd[:, :], std[:, :]).then_inc(rstd_done, 1)
            dve.wait_ge(rstd_done, 1)
            dve.wait_ge(aggregated, nt)
            if norms == 2:
                nc.vector.tensor_tensor(var2[:, :], mv[:, :, 1], rstd[:, :], ALU.mult).then_inc(rstd_done, 1)
                dve.wait_ge(rstd_done, 2)
                nc.vector.tensor_tensor(var2[:, :], var2[:, :], rstd[:, :], ALU.mult).then_inc(var2_done, 1)
                dve.wait_ge(std_done, 2)
                nc.vector.reciprocal(var2[:, :], std[:, :]).then_inc(rstd_done, 1)
                dve.wait_ge(rstd_done, 3)
                nc.vector.tensor_tensor(rstd[:, :], rstd[:, :], var2[:, :], ALU.mult).then_inc(rstd_done, 1)
                dve.wait_ge(rstd_done, 4)
            for t in range(nt):
                nc.vector.tensor_scalar(xn[:, t, :], src[:, t, :], mv[:, t, 0:1], rstd[:, t:t + 1],
                                        ALU.subtract, ALU.mult).then_inc(normed, 1)
            for g, tiles in enumerate(groups):
                w = len(tiles) * P
                for c in range(DC):
                    n = g * DC + c
                    dve.wait_ge(hi_done, n + 1)
                    whole = m.slot[n % 2] if affine is None else y[:, n % 2, :]
                    nc.vector.tensor_tensor(lo[:, c, g * 512:g * 512 + w], whole[:, 0:w],
                                            hi[:, c, g * 512:g * 512 + w], ALU.subtract).then_inc(lo_done, 1)

        @block.scalar
        def _(act):
            act.wait_ge(eps_set, 1)
            act.wait_ge(aggregated, nt)
            nc.scalar.activation(std[:, :], mv[:, :, 1], ACT.Sqrt, bias=eps[:, 0:1]).then_inc(std_done, 1)
            if norms == 2:
                act.wait_ge(var2_done, 1)
                nc.scalar.activation(std[:, :], var2[:, :], ACT.Sqrt, bias=eps[:, 0:1]).then_inc(std_done, 1)
            if affine is not None:
                act.wait_ge(gb_loaded, 16)
            for g, tiles in enumerate(groups):
                w = len(tiles) * P
                for c in range(DC):
                    n = g * DC + c
                    act.wait_ge(turned, n + 1)
                    if affine is None:
                        nc.scalar.activation(hi[:, c, g * 512:g * 512 + w], m.slot[n % 2][:, 0:w], ACT.Copy).then_inc(hi_done, 1)
                        continue
                    if n >= 2:
                        act.wait_ge(lo_done, n - 1)
                    nc.scalar.activation(y[:, n % 2, 0:w], m.slot[n % 2][:, 0:w], ACT.Identity,
                                         bias=gb[:, 1, c:c + 1], scale=gb[:, 0, c:c + 1]).then_inc(y_ready, 1)
                    act.wait_ge(y_ready, n + 1)
                    nc.scalar.activation(hi[:, c, g * 512:g * 512 + w], y[:, n % 2, 0:w], ACT.Copy).then_inc(hi_done, 1)

        @block.tensor
        def _(pe):
            for g, tiles in enumerate(groups):
                pe.wait_ge(normed, tiles[-1] + 1)
                for c in range(DC):
                    n = g * DC + c
                    if n >= 2:
                        pe.wait_ge(lo_done if affine is None else y_ready, n - 1)
                    for j, t in enumerate(tiles):
                        last = nc.tensor.transpose(m.slot[n % 2][:, j * P:(j + 1) * P], xn[:, t, c * P:(c + 1) * P],
                                                   m.ident[:, :])
                    last.then_inc(turned, 1)


class Attention:

    def __init__(self, name, latents, head, heads, q_scale, biased, gate):
        self.name = name
        self.latents = latents
        self.head = head
        self.heads = heads
        self.pitch = P // heads
        self.groups = 16 // heads
        self.stacked = head < HALF
        self.q_scale = q_scale
        self.biased = biased
        self.gate = gate
        self.ring = 8 if self.stacked else 5
        self.nl = NX if latents else 0
        self.nt = self.nl + NCT
        self.keys = self.nt * P
        self.kchunks = [(a, 512, True) for a in range(0, self.nl * P, 512)]
        self.kchunks += [(self.nl * P + a, min(512, CTXP - a), False) for a in range(0, CTXP, 512)]
        self.vgroups = [list(range(a, min(a + 4, self.nt))) for a in range(0, self.nt, 4)]
        self.qblock = P // heads
        self.nblock = QB // self.qblock
        self.mchunks = [(a, 512, False) for a in range(0, self.nl * P, 512)]
        w = -(-CTX // 8) * 2
        self.mchunks += [(a, w, True) for a in range(0, CTX, w)]
        self.msteps = len(self.mchunks) * self.nblock
        n = 4 if latents else 2
        self.kparts = [(j * self.nt // n, (j + 1) * self.nt // n) for j in range(n)]
        self.pool_tiles = [t for t in range(self.nt) if t * 19 // 29 != (t + 1) * 19 // 29] if not self.stacked else []
        self.dve_tiles = [t for t in range(self.nt) if t not in self.pool_tiles] if not self.stacked else []
        if self.stacked:
            self.raw_at, self.den_after, self.pieces, self.att_at, self.out_after = 3, 4, 4, 9, 12
        else:
            self.raw_at, self.den_after, self.pieces, self.att_at, self.out_after = 2, 4, 2, 8, 12
        self.turn_after, self.res_at = 2, self.out_after + 2
        assert NU == 4 and AHEAD == 2


def stage_attention(nc, m, a, w_in, wo_in, mask_in, bv_in=None, bo_in=None, ahead_of_use=()):
    NT, NL, KEYS = a.nt, a.nl, a.keys
    NK, NV = len(a.kchunks), len(a.vgroups)
    NKQ = NK + NU
    MS = a.msteps
    G, PITCH, QW, NB, RP = a.heads, a.pitch, a.qblock, a.nblock, a.ring
    PAIRS = G // 2
    NS = NT * PAIRS
    STEPS, TILES = NU * NS, NU * NT
    n_pass = 1 if a.stacked else 2
    with Semaphores(nc, a.name) as sem, ExitStack() as ctx:
        def sb(name, shape, dt=FP32):
            return ctx.enter_context(nc.sbuf_tensor(f"{a.name}_{name}", shape, dt))

        nb = 2 if a.biased else 0
        w_st = sb("w_staged", [P, 3 * DC * P + nb])
        w_hi, w_lo = sb("w_hi", [P, 3 * DC * P], FP16), sb("w_lo", [P, 3 * DC * P], FP16)
        w16 = sb("w_scaled", [P, 3 * DC * P])
        wscale = sb("w_scale", [P, 1])

        def weights(half, what, c):
            at = (what * DC + c) * P
            return half[:, at:at + P]

        wo = sb("wo", [P, D])
        y = sb("y", [P, RY, 512])
        kn_hi, kn_lo = sb("kn_hi", [P, KEYS], FP16), sb("kn_lo", [P, KEYS], FP16)
        qn_hi, qn_lo = sb("qn_hi", [P, TOK], FP16), sb("qn_lo", [P, TOK], FP16)
        kmask = sb("k_masked", [P, CTXP], FP16)
        qdiag = sb("q_diag", [P, TOK // QW, G, QW], FP16)
        part_max = sb("part_max", [P, NB, len(a.mchunks)])
        neg_max = sb("neg_max", [P, NB])
        shift = sb("shift", [NB, P], FP16)
        k_op = [[sb(f"k_op{h}{n}", [P, KEYS], FP16) for n in range(n_pass)] for h in range(G)]
        q_op = [[sb(f"q_op{h}{n}", [P, TOK], FP16) for n in range(n_pass)] for h in range(G)]
        val = sb("val", [P, NT, P])
        prob = sb("prob", [P, RP, 2 * QB])
        if not a.stacked:
            acc_v, acc_p = sb("acc_v", [P, 2, 2 * QB]), sb("acc_p", [P, 2, 2 * QB])
            ones = sb("ones", [P, HALF])
        else:
            spread = sb("spread", [P, P])
        rden = sb("rden", [P, QB])
        att = sb("att", [P, QB])
        gated = sb("gated", [P, 2 * QB])
        valid_u8 = sb("valid_u8", [P, CTXP], mybir.dt.uint8)
        valid = sb("valid", [P, CTXP], FP16)
        mcol_u8 = sb("mcol_u8", [P, NCT], mybir.dt.uint8)
        mbias = sb("mask_bias", [P, NT])
        if a.biased:
            qk_bias, bscale = sb("qk_bias", [P, 2]), sb("bias_scale", [P, 2])
            bv = sb("bv", [P, a.groups, P])
            bo = sb("bo", [P, D])
            bos = sb("bo_gated", [P, D])

        w_loaded, w_split, wo_loaded = sem("w_loaded"), sem("w_split"), sem("wo_loaded")
        split16, wscale_set = sem("w_scaled"), sem("wscale_set")
        fetched = sem("fetched")
        mask_loaded, bias_loaded = sem("mask_loaded"), sem("bias_loaded")
        zeros_set, diag_zeroed, prep = sem("zeros_set"), sem("diag_zeroed"), sem("prep")
        proj_done, proj_read = sem("proj_done"), sem("proj_read")
        y_used = sem("y_used")
        next_ready, kmask_part = sem("next_ready"), sem("kmask_part")
        k_laid = [sem(f"k_laid{c}") for c in range(len(a.kparts))]
        q_laid = [sem(f"q_laid{u}") for u in range(NU)]
        scores_ready, probs_ready, av_done = sem("scores_ready"), sem("probs_ready"), sem("av_done")
        total_ready = sem("total_ready")
        added_v, added_p = sem("added_v"), sem("added_p")
        raw_ready = sem("raw_ready")
        den_ready, inverted = sem("den_ready"), sem("inverted")
        att_ready, out_ready = sem("att_ready"), sem("out_ready")
        gated_ready, res_added = sem("gated_ready"), sem("res_added")
        max_ready, max_used = sem("max_ready"), sem("max_used")
        neg_ready, neg_turned = sem("neg_ready"), sem("neg_turned")
        shift_ready, shift_laid = sem("shift_ready"), sem("shift_laid")
        block = ctx.enter_context(nc.Block())


        def summed(tiles, i, u, n):
            return (i * NU + u) * (len(tiles) - 1) + n + 1

        def place(i, u):
            return i * NU + u + 1

        wide = [m.wide[:, n * 512:(n + 1) * 512] for n in range(2)]

        def max_bank(u, s):
            n = s % 2 if u is None else banks[u][s]
            return n, (wide[n] if n < 2 else m.bank[(u - 1) % 2][:, :])

        slots = []
        for u in range(NU):
            for t in range(NS):
                slots.append(("scores", u, t))
                if t == a.out_after:
                    slots.append(("out", u, 0))
        room = []
        for u in range(NU):
            rooms = [(t, z) for t in range(LATE * PAIRS if u == NEXT_AT else 0, NS) for z in range(3)
                     if z < 2 or t % PAIRS == PAIRS - 1]
            room.append(dict(zip(rooms, split_even(MS, len(rooms)))))
        banks = [[] for _ in range(NU)]
        for u in range(NU):
            for t, z in sorted(room[u]):
                for _ in range(room[u][t, z]):
                    n = len(banks[u])
                    used = banks[u][-1] if n else 1
                    banks[u].append((used + 1) % (3 if t > a.den_after + a.pieces else 2) if used < 2 else 0)
        places = [[sum(r.get((t, z), 0) for z in range(3)) for t in range(NS)] for r in room]

        def bank_of(n):
            return m.slot[(n // 2) % 2][:, (n % 2) * 512:(n % 2) * 512 + 512]

        def consumed(k, i):
            kind, u, t = slots[k]
            if kind == "scores":
                return probs_ready, i * STEPS + u * NS + t + 1
            return gated_ready, place(i, u)

        def ahead(i, u):
            return i * NU + u + AHEAD

        def groups_before(it):
            return it * NKQ + (it - 1) * NV if not isinstance(it, int) or it else 0

        def y_before(it):
            return groups_before(it) if a.biased else it * NKQ

        @block.sync
        def _(sp):
            sp.dma_start(w_st[:, :], w_in[0, :, :]).then_inc(w_loaded, 16)
            sp.dma_start(valid_u8[:, :], mask_in[0][0:1, :].broadcast_to([P, CTXP])).then_inc(mask_loaded, 16)
            sp.dma_start(mcol_u8[:, :], mask_in[1]).then_inc(mask_loaded, 16)
            for dst, src in ahead_of_use:
                sp.dma_start(dst, src).then_inc(fetched, 16)
            if a.biased:
                sp.dma_start(bv[:, :, :].rearrange("p n c -> p (n c)"), bv_in[0:1, :].broadcast_to([P, a.groups * P])).then_inc(bias_loaded, 16)
                sp.dma_start(bo[:, :], bo_in[0:1, :].broadcast_to([P, D])).then_inc(bias_loaded, 16)
            sp.wait_ge(zeros_set, 1)

            def lay_q(u, i):
                wait(sp, scores_ready, i * STEPS + (u + 1) * NS if i is not None else 0)
                c = slice(u * QB, (u + 1) * QB)
                for h in range(G):
                    r = slice(h * PITCH, h * PITCH + a.head)
                    if a.stacked:
                        parts = [(q_op[h][0][0:a.head, c], qn_hi[r, c]),
                                 (q_op[h][0][a.head:2 * a.head, c], qn_lo[r, c]),
                                 (q_op[h][0][2 * a.head:3 * a.head, c], qn_hi[r, c])]
                    else:
                        parts = [(q_op[h][0][0:HALF, c], qn_hi[r, c]), (q_op[h][0][HALF:P, c], qn_lo[r, c]),
                                 (q_op[h][1][0:HALF, c], qn_hi[r, c])]
                    for dst, src in parts:
                        sp.dma_start(dst, src).then_inc(q_laid[u], 16)

            def lay_shift(i, u):
                sp.wait_ge(shift_ready, i * NU + u + 1)
                for h in range(G):
                    dst = q_op[h][-1][HALF:HALF + 1, u * QB:(u + 1) * QB].rearrange("o (j q) -> o j q", q=QW)
                    sp.dma_start(dst, shift[:, h * QW:(h + 1) * QW]).then_inc(shift_laid, 16)

            def lay_k(n, i):
                lo, hi = a.kparts[n]
                wait(sp, scores_ready, i * STEPS + (NU - 1) * NS + hi * PAIRS if i is not None else 0)
                c = slice(lo * P, hi * P)
                for h in range(G):
                    r = slice(h * PITCH, h * PITCH + a.head)
                    if a.stacked:
                        parts = [(k_op[h][0][0:a.head, c], kn_hi[r, c]),
                                 (k_op[h][0][a.head:2 * a.head, c], kn_hi[r, c]),
                                 (k_op[h][0][2 * a.head:3 * a.head, c], kn_lo[r, c])]
                    else:
                        parts = [(k_op[h][0][0:HALF, c], kn_hi[r, c]), (k_op[h][0][HALF:P, c], kn_hi[r, c]),
                                 (k_op[h][1][0:HALF, c], kn_lo[r, c])]
                    for dst, src in parts:
                        sp.dma_start(dst, src).then_inc(k_laid[n], 16)

            def group(i, last=False):
                if not last:
                    sp.wait_ge(w_split, i + 2)
                    sp.wait_ge(zeros_set, 1)
                    sp.dma_start(w_st[:, :], w_in[i + 2, :, :]).then_inc(w_loaded, 16)
                lay_shift(i, 1)
                sp.wait_ge(out_ready, place(i, 0))
                sp.wait_ge(zeros_set, 1)
                sp.dma_start(wo[:, :], wo_in[i, :, :]).then_inc(wo_loaded, 16)
                lay_shift(i, 2)
                if last:
                    lay_shift(i, 3)
                    return
                sp.wait_ge(next_ready, i + 2)
                lay_q(0, i)
                lay_q(1, i)
                lay_shift(i, 3)
                lay_q(2, i)
                lay_k(0, i)
                lay_shift(i + 1, 0)
                for n in range(1, len(a.kparts)):
                    lay_k(n, i)
                lay_q(3, i)

            sp.wait_ge(w_split, 1)
            sp.dma_start(w_st[:, :], w_in[1, :, :]).then_inc(w_loaded, 16)
            sp.wait_ge(next_ready, 1)
            for n in range(len(a.kparts)):
                lay_k(n, None)
            for u in range(NU):
                lay_q(u, None)
            lay_shift(0, 0)
            with sp.Fori(0, a.groups - 1) as i:
                group(i)
            group(a.groups - 1, last=True)
            wait(sp, fetched, 16 * len(ahead_of_use))

        @block.gpsimd
        def _(pool):
            def split(n):
                scale = wscale[:, 0:1].broadcast_to([P, 3 * DC * P])
                pool.wait_ge(w_loaded, n * 16 + 16)
                nc.gpsimd.tensor_tensor(w_hi[:, :], w_st[:, 0:3 * DC * P], scale, ALU.mult)
                if a.biased:
                    nc.gpsimd.tensor_tensor(qk_bias[:, :], w_st[:, 3 * DC * P:], bscale[:, :], ALU.mult)
                nc.gpsimd.tensor_tensor(w16[:, :], w_st[:, 0:3 * DC * P], scale, ALU.mult).then_inc(split16, 1)
                pool.wait_ge(split16, n + 1)
                nc.gpsimd.tensor_tensor(w_lo[:, :], w16[:, :], w_hi[:, :], ALU.subtract).then_inc(w_split, 1)

            def divide(i, u):
                pool.wait_ge(raw_ready, place(i, u))
                pool.wait_ge(inverted, place(i, u))
                nc.gpsimd.tensor_tensor(att[:, :], att[:, :], rden[:, :], ALU.mult).then_inc(att_ready, 1)

            def residual(i, u):
                pool.wait_ge(gated_ready, place(i, u))
                pool.wait_ge(res_added, place(i, u))
                o = (u - 1) % NU
                xs = m.x[:, 4 * o:4 * o + 4, :].rearrange("p t d -> p (t d)")
                nc.gpsimd.tensor_tensor(xs, gated[:, :], xs, ALU.add).then_inc(res_added, 1)

            def add_up(i, u):
                pool.wait_ge(added_v, summed(a.dve_tiles, i, u, 0))
                pool.wait_ge(added_p, summed(a.pool_tiles, i, u, 0))
                acc = acc_p[:, (u - 1) % 2, :]
                nc.gpsimd.tensor_tensor(acc, acc, acc_v[:, (u - 1) % 2, :], ALU.add).then_inc(total_ready, 1)

            def add(i, u, t):
                n, k = a.pool_tiles.index(t) - 1, u * NT + t
                if n < 0:
                    return
                if n == 0 and u:
                    pool.wait_ge(den_ready, place(i, u - 1))
                pool.wait_ge(probs_ready, i * STEPS + k + 1)
                if n == 0:
                    before = prob[:, (u * NT + a.pool_tiles[0]) % RP, :]
                else:
                    before = acc_p[:, u % 2, :]
                    pool.wait_ge(added_p, summed(a.pool_tiles, i, u, n))
                nc.gpsimd.tensor_tensor(acc_p[:, u % 2, :], before, prob[:, k % RP, :], ALU.add).then_inc(added_p, 1)

            def group(i, last=False):
                for u in range(NU):
                    for t in range(NS):
                        if u == NU - 1 and t == 0 and not last:
                            pool.wait_ge(proj_read, groups_before(i + 2))
                            split(i + 2)
                        if t == 1 and not a.stacked:
                            add_up(i, u)
                        if t == a.att_at:
                            divide(i, u)
                        if t == a.res_at:
                            residual(i, u)
                        if t in a.pool_tiles:
                            add(i, u, t)

            nc.gpsimd.memset(wscale[:, :], WSCALE)
            if a.biased:
                nc.gpsimd.memset(bscale[:, 1:2], 1.0)
                nc.gpsimd.memset(bscale[:, 0:1], a.q_scale)
            nc.gpsimd.memset(w16[:, 0:1], 0.0).then_inc(wscale_set, 1)
            pool.wait_ge(wscale_set, 1)
            split(0)
            nc.gpsimd.memset(qdiag[:, :, :, :], 0.0).then_inc(diag_zeroed, 1)
            pool.wait_ge(diag_zeroed, 1)
            for h in range(G):
                lo = 0 if a.stacked else HALF
                nc.gpsimd.memset(k_op[h][-1][lo:P, :], 1.0)
                ins = nc.gpsimd.memset(q_op[h][-1][lo:P, :], 0.0)
            ins.then_inc(zeros_set, 1)
            pool.wait_ge(zeros_set, 1)
            pool.wait_ge(proj_read, NKQ)
            split(1)
            pool.wait_ge(prep, 1)
            if a.biased:
                for t in range(NX):
                    nc.gpsimd.tensor_tensor(m.x[:, t, :], m.x[:, t, :], bos[:, :], ALU.add)
            nc.gpsimd.memset(gated[:, 0:1], 0.0).then_inc(res_added, 1)
            with pool.Fori(0, a.groups - 1) as i:
                group(i)
            group(a.groups - 1, last=True)
            if not a.stacked:
                add_up(a.groups, 0)
            divide(a.groups, 0)
            residual(a.groups, 0)

        @block.scalar
        def _(act):
            def project_values(it):
                g0, y0 = groups_before(it), y_before(it)
                for n, tiles in enumerate(a.vgroups):
                    w = len(tiles) * P
                    act.wait_ge(proj_done, g0 + n + 1)
                    src = bank_of(n)[:, 0:w]
                    if a.biased:
                        act.wait_ge(y_used, y0 + n - RY + 1)
                        nc.scalar.activation(y[:, n % RY, 0:w], src, ACT.Copy, scale=1.0 / WSCALE).then_inc(proj_read, 1)
                    else:
                        dst = val[:, tiles[0]:tiles[-1] + 1, :].rearrange("p t c -> p (t c)")
                        nc.scalar.activation(dst, src, ACT.Copy, scale=1.0 / WSCALE).then_inc(proj_read, 1)

            def project_next(it, n0):
                g0, y0, yn = groups_before(it), y_before(it), n0 if a.biased else 0
                for c in range(len(a.kparts)):
                    wait(act, k_laid[c], it * 16 * 3 * G)
                for j in range(NKQ):
                    n, b = n0 + j, (yn + j) % RY
                    c0, w = a.kchunks[j][:2] if j < NK else ((j - NK) * QB, QB)
                    hi = (kn_hi if j < NK else qn_hi)[:, c0:c0 + w]
                    if j >= NK:
                        wait(act, q_laid[j - NK], it * 16 * 3 * G)
                    act.wait_ge(proj_done, g0 + n + 1)
                    wait(act, y_used, y0 + yn + j - RY + 1)
                    src = bank_of(n)[:, 0:w]
                    scale = (1.0 if j < NK else a.q_scale) / WSCALE
                    if a.biased:
                        bias = qk_bias[:, 1:2] if j < NK else qk_bias[:, 0:1]
                        nc.scalar.activation(y[:, b, 0:w], src, ACT.Identity, bias=bias, scale=scale)
                        nc.scalar.activation(hi, src, ACT.Identity, bias=bias, scale=scale).then_inc(proj_read, 1)
                    else:
                        nc.scalar.activation(y[:, b, 0:w], src, ACT.Copy, scale=scale)
                        nc.scalar.activation(hi, src, ACT.Copy, scale=scale).then_inc(proj_read, 1)

            def take_raw(i, u):
                act.wait_ge(av_done, (i * NU + u) * NT + 1)
                nc.scalar.activation(att[:, :], m.bank[(u - 1) % 2][:, :], ACT.Copy).then_inc(raw_ready, 1)

            def gate_outputs(i, u, slot):
                act.wait_ge(out_ready, place(i, u))
                nc.scalar.activation(gated[:, :], m.slot[slot][:, :], ACT.Copy, scale=m.tg[:, a.gate:a.gate + 1]).then_inc(gated_ready, 1)

            def group(i, last=False):
                project_values(i + 1)
                if not a.stacked:
                    act.wait_ge(added_p, summed(a.pool_tiles, i, 0, 0))
                    act.wait_ge(added_v, summed(a.dve_tiles, i, 0, 0))
                for u in range(NU):
                    if u == NEXT_AT and not last:
                        project_next(i + 1, NV)
                    for t in range(NS):
                        k = u * NS + t
                        if t == a.raw_at:
                            take_raw(i, u)
                        if t == a.out_after + 1:
                            gate_outputs(i, u, slots.index(("out", u, 0)) % 2)
                        act.wait_ge(scores_ready, i * STEPS + k + 1)
                        if k >= RP:
                            o = (k - RP) // PAIRS
                            act.wait_ge(av_done, i * TILES + o + 2)
                            for tiles, added in ((a.pool_tiles, added_p), (a.dve_tiles, added_v)):
                                if o % NT in tiles:
                                    act.wait_ge(added, summed(tiles, i, o // NT, max(tiles.index(o % NT), 1)))
                        slot = slots.index(("scores", u, t))
                        nc.scalar.activation(prob[:, k % RP, :], m.slot[slot % 2][:, :], ACT.Exp,
                                             bias=mbias[:, t // PAIRS:t // PAIRS + 1]).then_inc(probs_ready, 1)

            act.wait_ge(w_split, 1)
            project_next(0, 0)
            act.wait_ge(prep, 1)
            with act.Fori(0, a.groups - 1) as i:
                group(i)
            group(a.groups - 1, last=True)
            take_raw(a.groups, 0)
            gate_outputs(a.groups, 0, 0)

        @block.vector
        def _(dve):
            chain = [0]
            link_sem = sem("dve_chain")

            def link(ins):
                chain[0] += 1
                ins.then_inc(link_sem, 1)
                dve.wait_ge(link_sem, chain[0])

            link(nc.vector.memset(mbias[:, :], 0.0))
            nc.vector.memset(wo[:, :], 0.0)
            nc.vector.memset(m.bank[1][:, :], 1.0)
            if not a.stacked:
                nc.vector.memset(ones[:, :], 1.0)
                nc.vector.memset(acc_v[:, 1, :], 1.0)
                nc.vector.memset(acc_p[:, 1, :], 1.0)
            if a.stacked:
                row = m.ident[:, :].rearrange("p (g c) -> p g c", c=PITCH)[:, :, PITCH // 2:PITCH // 2 + 1]
                nc.vector.tensor_copy(spread[:, :].rearrange("p (g c) -> p g c", c=PITCH), row.broadcast_to([P, G, PITCH]))
            dve.wait_ge(mask_loaded, 32)
            nc.vector.tensor_copy(valid[:, :], valid_u8[:, :])
            link(nc.vector.tensor_scalar(mbias[:, NL:NT], mcol_u8[:, :], -1.0, -MASKED, ALU.add, ALU.mult))
            if a.biased:
                dve.wait_ge(bias_loaded, 32)
                ones_cols = bv[:, :, :].rearrange("p n (h c) -> p (n h) c", c=PITCH)[:, :, PITCH // 2:]
                link(nc.vector.memset(ones_cols, 1.0))
                link(nc.vector.tensor_scalar(bos[:, :], bo[:, :], m.tg[:, a.gate:a.gate + 1], None, ALU.mult))
            nc.vector.memset(rden[:, 0:1], 0.0).then_inc(prep, 1)
            nc.vector.memset(rden[:, 1:2], 0.0).then_inc(av_done, 1)
            nc.vector.memset(rden[:, 2:3], 0.0).then_inc(added_p, 1)
            nc.vector.memset(rden[:, 3:4], 0.0).then_inc(added_v, 1)

            def project_values(it, group):
                g0 = groups_before(it)
                for n, tiles in enumerate(a.vgroups if a.biased else []):
                    w = len(tiles)
                    dve.wait_ge(proj_read, g0 + n + 1)
                    row = bv[:, group:group + 1, :] if isinstance(group, int) else bv[:, bass.ds(group, 1), :]
                    nc.vector.tensor_tensor(val[:, tiles[0]:tiles[-1] + 1, :],
                                            y[:, n % RY, 0:w * P].rearrange("p (t c) -> p t c", c=P),
                                            row.broadcast_to([P, w, P]), ALU.add).then_inc(y_used, 1)

            def project_next(it, n0):
                g0, yn = groups_before(it), n0 if a.biased else 0
                for j in range(NKQ):
                    key = j < NK
                    c0, w = a.kchunks[j][:2] if key else ((j - NK) * QB, QB)
                    hi, lo = (kn_hi, kn_lo) if key else (qn_hi, qn_lo)
                    own = y[:, (yn + j) % RY, 0:w]
                    dve.wait_ge(proj_read, g0 + n0 + j + 1)
                    nc.vector.tensor_tensor(lo[:, c0:c0 + w], own, hi[:, c0:c0 + w], ALU.subtract).then_inc(y_used, 1)
                    if key and not a.kchunks[j][2]:
                        b0 = c0 - NL * P
                        km = kmask[:, b0:b0 + w]
                        nc.vector.scalar_tensor_tensor(km, hi[:, c0:c0 + w], k0, valid[:, b0:b0 + w],
                                                       ALU.subtract, ALU.mult).then_inc(kmask_part, 1)
                        dve.wait_ge(kmask_part, it * (NK - NL // 4) + (j - NL // 4) + 1)
                        nc.vector.tensor_scalar(km, km, k0, None, ALU.add)
                    if not key:
                        for h in range(G):
                            r = slice(h * PITCH, (h + 1) * PITCH)
                            b = c0 // QW
                            ins = nc.vector.tensor_copy(qdiag[r, b:b + NB, h, :],
                                                        hi[r, c0:c0 + w].rearrange("p (b q) -> p b q", q=QW))
                ins.then_inc(next_ready, 1)

            def max_step(unit, s, u):
                c, j = s // NB, s % NB
                w = a.mchunks[c][1]
                if s == 0:
                    wait(dve, neg_ready, unit)
                dve.wait_ge(max_ready, unit * MS + s + 1)
                nc.vector.reduce_max(part_max[:, j:j + 1, c], max_bank(u, s)[1][:, 0:w], AX.X).then_inc(max_used, 1)

            def max_of_unit(unit):
                dve.wait_ge(max_used, unit * MS + MS)
                nc.vector.tensor_reduce(neg_max[:, :], part_max[:, :, :], AX.X, ALU.max, negate=True).then_inc(neg_ready, 1)

            def shift_of_unit(unit):
                dve.wait_ge(neg_turned, unit + 1)
                wait(dve, shift_laid, unit * 16 * G)
                nc.vector.tensor_copy(shift[:, :], wide[0][0:NB, 0:P]).then_inc(shift_ready, 1)

            def add(i, u, t):
                if t not in a.dve_tiles[1:]:
                    return
                n, k = a.dve_tiles.index(t) - 1, u * NT + t
                if n == 0 and u:
                    dve.wait_ge(den_ready, place(i, u - 1))
                dve.wait_ge(probs_ready, i * STEPS + k + 1)
                if n == 0:
                    before = prob[:, (u * NT + a.dve_tiles[0]) % RP, :]
                else:
                    before = acc_v[:, u % 2, :]
                    dve.wait_ge(added_v, summed(a.dve_tiles, i, u, n))
                nc.vector.tensor_tensor(acc_v[:, u % 2, :], before, prob[:, k % RP, :], ALU.add).then_inc(added_v, 1)

            def invert(i, u, piece):
                if piece == 0:
                    dve.wait_ge(den_ready, place(i, u))
                c = slice(piece * QB // a.pieces, (piece + 1) * QB // a.pieces)
                ins = nc.vector.reciprocal(rden[:, c], m.bank[(u - 1) % 2][:, c])
                if piece == a.pieces - 1:
                    ins.then_inc(inverted, 1)

            def group(i, last=False):
                project_values(i + 1, i)
                for u in range(NU):
                    finding = not last or u < AHEAD
                    if u == NEXT_AT and not last:
                        project_next(i + 1, NV)
                    s = 0
                    for t in range(NS):
                        if 0 <= t - a.den_after - 1 < a.pieces:
                            invert(i, u, t - a.den_after - 1)
                        if t == a.turn_after + 1 and (not last or u < AHEAD + 1):
                            shift_of_unit(ahead(i, u) - 1)
                        for _ in range(places[u][t] if finding else 0):
                            max_step(ahead(i, u), s, u)
                            s += 1
                        if not a.stacked:
                            if t:
                                add(i, u, t - 1)
                            elif u:
                                add(i, u - 1, NT - 1)
                    if finding:
                        max_of_unit(ahead(i, u))
                if not a.stacked:
                    add(i, NU - 1, NT - 1)

            k0 = kn_hi[:, 0:1]
            dve.wait_ge(diag_zeroed, 1)
            project_next(0, 0)
            for u in range(AHEAD):
                for s in range(MS):
                    max_step(u, s, None)
                max_of_unit(u)
                if u < AHEAD - 1:
                    shift_of_unit(u)
            with dve.Fori(0, a.groups - 1) as i:
                group(i)
            group(a.groups - 1, last=True)
            for piece in range(a.pieces):
                invert(a.groups, 0, piece)

        @block.tensor
        def _(pe):
            def project_values(it):
                g0 = groups_before(it)
                pe.wait_ge(w_split, it + 1)
                for n, tiles in enumerate(a.vgroups):
                    wait(pe, proj_read, g0 + n - 3 if n >= 4 else 0)
                    for z, t in enumerate(tiles):
                        src = (m.xh, m.xl) if t < NL else (m.ch, m.cl)
                        c1 = (t if t < NL else t - NL) * P
                        for q, (wt, half) in enumerate([(w_hi, 0), (w_hi, 1), (w_lo, 0)]):
                            for c in range(DC):
                                ins = nc.tensor.matmul(bank_of(n)[:, z * P:(z + 1) * P], src[half][:, c, c1:c1 + P], weights(wt, 2, c),
                                                       start=(q == 0 and c == 0), stop=(q == 2 and c == DC - 1))
                    ins.then_inc(proj_done, 1)

            def project_next(it, n0):
                g0 = groups_before(it)
                wait(pe, w_split, 1 if n0 == 0 else 0)
                for j in range(NKQ):
                    n, key = n0 + j, j < NK
                    c0, w, tokens = a.kchunks[j] if key else ((j - NK) * QB, QB, True)
                    src = (m.xh, m.xl) if tokens else (m.ch, m.cl)
                    c1 = c0 if tokens else c0 - NL * P
                    wait(pe, proj_read, g0 + n - 3 if n >= 4 else 0)
                    for q, (wt, half) in enumerate([(w_hi, 0), (w_hi, 1), (w_lo, 0)]):
                        for c in range(DC):
                            ins = nc.tensor.matmul(bank_of(n)[:, 0:w], weights(wt, 1 if key else 0, c), src[half][:, c, c1:c1 + w],
                                                   start=(q == 0 and c == 0), stop=(q == 2 and c == DC - 1))
                    ins.then_inc(proj_done, 1)

            max_before = [None] * 3

            def max_step(unit, s, block, beside):
                c, j = s // NB, s % NB
                first, w, masked = a.mchunks[c]
                n, bank = max_bank(beside, s)
                wide_free(unit, n)
                src = (kmask if masked else kn_hi)[:, first:first + w]
                nc.tensor.matmul(bank[:, 0:w], qdiag[:, block * NB + j, :, :].rearrange("p h q -> p (h q)"), src,
                                 start=True, stop=True).then_inc(max_ready, 1)
                max_before[n] = (max_used, s + 1)

            def wide_free(unit, bank):
                if max_before[bank] is None and bank == 2:
                    pe.wait_ge(inverted, unit - AHEAD + 1)
                elif max_before[bank] is None:
                    wait(pe, max_used, unit * MS)
                elif max_before[bank][0] is max_used:
                    pe.wait_ge(max_used, unit * MS + max_before[bank][1])
                else:
                    pe.wait_ge(shift_ready, unit)

            def turn(unit):
                pe.wait_ge(neg_ready, unit)
                wide_free(unit, 0)
                nc.tensor.transpose(wide[0][0:NB, 0:P], neg_max[:, :], m.ident[:, :]).then_inc(neg_turned, 1)
                max_before[0] = (shift_ready, None)

            def free_slot(i, k, groups):
                if k >= 2:
                    pe.wait_ge(*consumed(k - 2, i))
                if k == 0 or k == slots.index(("scores", NEXT_AT, 0)):
                    pe.wait_ge(proj_read, groups)

            def scores(i, u, s, k, groups, beside):
                t, first_head = s // PAIRS, s % PAIRS * 2
                if s == 0:
                    pe.wait_ge(q_laid[u], (i + 1) * 16 * 3 * G)
                    pe.wait_ge(shift_laid, (i * NU + u + 1) * 16 * G)
                for n, (lo, _) in enumerate(a.kparts):
                    if u == 0 and s == lo * PAIRS:
                        pe.wait_ge(k_laid[n], (i + 1) * 16 * 3 * G)
                free_slot(i, k, groups)
                for z in range(2):
                    h = first_head + z
                    for n in range(n_pass):
                        ins = nc.tensor.matmul(m.slot[k % 2][:, z * QB:(z + 1) * QB], k_op[h][n][:, t * P:(t + 1) * P],
                                               q_op[h][n][:, u * QB:(u + 1) * QB], start=(n == 0), stop=(n == n_pass - 1))
                    if z:
                        ins.then_inc(scores_ready, 1)
                    beside(z)

            def values(i, u, t, groups):
                k = (u * NT + t) * PAIRS
                if t == 0 and (not isinstance(i, int) or u <= AHEAD):
                    pe.wait_ge(max_used, ahead(i, u) * MS)
                if k == 0:
                    if a.biased:
                        pe.wait_ge(y_used, groups)
                pe.wait_ge(probs_ready, i * STEPS + k + PAIRS)
                for h in range(G):
                    r = slice(h * PITCH, (h + 1) * PITCH)
                    ins = nc.tensor.matmul(m.bank[u % 2][r, :], val[:, t, r], prob[:, (k + h // 2) % RP, h % 2 * QB:(h % 2 + 1) * QB],
                                           start=(t == 0), stop=(t == NT - 1), tile_position=(0, h * PITCH))
                ins.then_inc(av_done, 1)

            def sums(i, u):
                pe.wait_ge(raw_ready, place(i, u))
                if a.stacked:
                    nc.tensor.matmul(m.bank[(u - 1) % 2][:, :], spread[:, :], att[:, :], start=True, stop=True).then_inc(den_ready, 1)
                    return
                pe.wait_ge(total_ready, place(i, u))
                for h in range(2):
                    ins = nc.tensor.matmul(m.bank[(u - 1) % 2][h * HALF:(h + 1) * HALF, :], ones[:, :],
                                           acc_p[:, (u - 1) % 2, h * QB:(h + 1) * QB], start=True, stop=True)
                ins.then_inc(den_ready, 1)

            def outputs(i, u, slot):
                if u == 1:
                    pe.wait_ge(wo_loaded, i * 16 + 16)
                pe.wait_ge(att_ready, place(i, u))
                for j in range(QB // P):
                    ins = nc.tensor.matmul(m.slot[slot][:, j * D:(j + 1) * D], att[:, j * P:(j + 1) * P], wo[:, :], start=True, stop=True)
                ins.then_inc(out_ready, 1)

            def group(i, last=False):
                project_values(i + 1)
                groups = groups_before(i + 1) + NV
                k = 0
                for u in range(NU):
                    if u == NEXT_AT and not last:
                        values(i, u - 1, NT - 1, groups)
                        project_next(i + 1, NV)
                        groups = groups_before(i + 1) + NV + NKQ
                    step = [0]
                    max_before[:] = [None] * 3
                    finding = not last or u < AHEAD
                    for t in range(NS):
                        if u == NEXT_AT and not last and t == LATE * PAIRS:
                            pe.wait_ge(next_ready, i + 2)

                        def beside(z):
                            for _ in range(room[u].get((t, z), 0) if finding else 0):
                                max_step(ahead(i, u), step[0], (u + AHEAD) % NU, u)
                                step[0] += 1

                        scores(i, u, t, k, groups, beside)
                        k += 1
                        if t % PAIRS == PAIRS - 1:
                            if t >= PAIRS:
                                values(i, u, t // PAIRS - 1, groups)
                            elif u and (u != NEXT_AT or last):
                                values(i, u - 1, NT - 1, groups)
                            beside(2)
                        if t == a.den_after:
                            sums(i, u)
                        if t == a.out_after:
                            free_slot(i, k, groups)
                            outputs(i, u, k % 2)
                            k += 1
                        if t == a.turn_after and (not last or u < AHEAD + 1):
                            turn(ahead(i, u))
                values(i, NU - 1, NT - 1, groups)

            project_next(0, 0)
            pe.wait_ge(prep, 1)
            pe.wait_ge(next_ready, 1)
            for u in range(AHEAD):
                max_before[:] = [None] * 3
                if u:
                    turn(u)
                for s in range(MS):
                    max_step(u, s, u, None)
            with pe.Fori(0, a.groups - 1) as i:
                group(i)
            group(a.groups - 1, last=True)
            sums(a.groups, 0)
            outputs(a.groups, 0, 0)


def expert_weights(nc, ctx, rw_in, rb_in, w1_in, b1_in, w2_in, b2_in):
    def sb(name, shape):
        return ctx.enter_context(nc.sbuf_tensor(f"moe_{name}", shape, FP32))
    rw, w1, w2 = sb("rw", [P, DC, NE]), sb("w1", [P, DC, NE, EF]), sb("w2", [P, NE, D])
    b1, b2, rb = sb("b1", [P, NE]), sb("b2", [P, D]), sb("rb", [P, NE])
    fetch = [(rw[:, :, :], rw_in.rearrange("(c p) e -> p c e", p=P)), (b2[:, :], b2_in), (b1[:, :], b1_in),
             (rb[:, :], rb_in[0:1, :].broadcast_to([P, NE])), (w2[:, :, :], w2_in.rearrange("e f d -> f e d"))]
    fetch += [(w1[:, c, :, :], w1_in[:, c * P:(c + 1) * P, :].rearrange("e p f -> p e f")) for c in range(DC)]
    return (rw, w1, w2, b1, b2, rb), fetch


def stage_experts(nc, m, gate, weights):
    NB = TOK // QB
    STEPS = NB * NE
    with Semaphores(nc, "moe") as sem, ExitStack() as ctx:
        def sb(name, shape, dt=FP32):
            return ctx.enter_context(nc.sbuf_tensor(f"moe_{name}", shape, dt))

        rw, w1, w2, b1, b2, rb = weights
        rw_h, rw_l = sb("rw_hi", [P, DC, NE], FP16), sb("rw_lo", [P, DC, NE], FP16)
        w1_h, w1_l = sb("w1_hi", [P, DC, NE, EF], FP16), sb("w1_lo", [P, DC, NE, EF], FP16)
        w2_h, w2_l = sb("w2_hi", [P, NE, D], FP16), sb("w2_lo", [P, NE, D], FP16)
        b2_h, b2_l = sb("b2_hi", [P, D], FP16), sb("b2_lo", [P, D], FP16)
        lg, top = sb("logits", [P, NX, NE]), sb("top", [P, NX, 8])
        best, total, pair_sum = sb("best", [P, NX]), sb("total", [P, NX]), sb("pair_sum", [P, NX])
        left = sb("left", [P, NX, NE])
        wt = sb("weights", [P, NX, P])
        wt_h, wt_l = sb("wt_hi", [P, TOK], FP16), sb("wt_lo", [P, TOK], FP16)
        pick = sb("pick", [P, NE, P], FP16)
        h = sb("hidden", [P, 2, QB])
        y, y_h, y_l = sb("y", [P, 2, QB]), sb("y_hi", [P, 2, QB], FP16), sb("y_lo", [P, 2, QB], FP16)
        tgs = sb("gate_scaled", [P, 1])
        w_hi_done, w_ready = sem("w_hi_done"), sem("w_ready")
        routed, exp_done, dvec = sem("routed"), sem("exp_done"), sem("dve_chain")
        wt_turned, wt_read, wt_ready = sem("wt_turned"), sem("wt_read"), sem("wt_ready")
        shifted = sem("logits_shifted")
        weights_done = sem("weights_done")
        h_ready, h_done, spread_ready = sem("h_ready"), sem("h_done"), sem("spread_ready")
        y_done, yh_done, yl_done = sem("y_done"), sem("yh_done"), sem("yl_done")
        step_used, out_used = sem("step_used"), sem("out_used")
        block = ctx.enter_context(nc.Block())
        hbank = lambda n: m.slot[0][:, (n % 2) * 512:(n % 2) * 512 + 512]
        sbank = lambda n: m.slot[1][:, (n % 2) * 512:(n % 2) * 512 + 512]
        obank = lambda b, z: m.wide[:, z * 512:z * 512 + 512] if b % 2 == 0 else m.bank[z][:, :]
        splits = [(rw, rw_h, rw_l, WSCALE), (b2, b2_h, b2_l, WSCALE), (w1, w1_h, w1_l, WSCALE), (w2, w2_h, w2_l, WSCALE)]

        def flat(t):
            return t[:] if len(t.shape) == 2 else t[:].rearrange("p a b -> p (a b)") if len(t.shape) == 3 else t[:].rearrange("p a b c -> p (a b c)")

        @block.gpsimd
        def _(pool):
            for n, (w, hi, lo, _) in enumerate(splits):
                pool.wait_ge(w_hi_done, 2 * n + 2)
                nc.gpsimd.tensor_tensor(flat(lo), flat(w), flat(hi), ALU.subtract).then_inc(w_ready, 1)

        @block.scalar
        def _(act):
            for n, (w, hi, lo, s) in enumerate(splits):
                nc.scalar.activation(flat(w), flat(w), ACT.Copy, scale=s).then_inc(w_hi_done, 1)
                act.wait_ge(w_hi_done, 2 * n + 1)
                nc.scalar.activation(flat(hi), flat(w), ACT.Copy).then_inc(w_hi_done, 1)
            act.wait_ge(shifted, 1)
            nc.scalar.activation(flat(lg), flat(lg), ACT.Exp).then_inc(exp_done, 1)
            for g in range(NB):
                act.wait_ge(wt_turned, g + 1)
                nc.scalar.activation(wt_h[:, g * QB:(g + 1) * QB], sbank(g), ACT.Copy).then_inc(wt_read, 1)
            for n in range(STEPS):
                e = n % NE
                act.wait_ge(h_ready, n + 1)
                if n >= 2:
                    act.wait_ge(y_done, n - 1)
                nc.scalar.activation(h[:, n % 2, :], hbank(n), ACT.Gelu, bias=b1[:, e:e + 1], scale=1.0 / WSCALE).then_inc(h_done, 1)
                act.wait_ge(y_done, n + 1)
                if n >= 2:
                    act.wait_ge(step_used, n - 1)
                nc.scalar.activation(y_h[:, n % 2, :], y[:, n % 2, :], ACT.Copy).then_inc(yh_done, 1)

        @block.vector
        def _(dve):
            chain = [0]

            def link(ins):
                chain[0] += 1
                ins.then_inc(dvec, 1)
                dve.wait_ge(dvec, chain[0])

            nc.vector.memset(wt[:, :, :], 0.0)
            for e in range(NE):
                nc.vector.tensor_copy(pick[:, e, :], m.ident[:, e:e + 1].broadcast_to([P, P]))
            link(nc.vector.tensor_scalar(tgs[:, :], m.tg[:, gate:gate + 1], 1.0 / WSCALE, None, ALU.mult))
            dve.wait_ge(routed, 1)
            logits = hbank(0)[:, 0:NX * NE].rearrange("p (t e) -> p t e", e=NE)
            rbb = rb[:, :].rearrange("p (o e) -> p o e", o=1).broadcast_to([P, NX, NE])
            link(nc.vector.scalar_tensor_tensor(lg[:, :, :], logits, 1.0 / WSCALE, rbb, ALU.mult, ALU.add))
            link(nc.vector.reduce_max(best[:, :], lg[:, :, :], AX.X))
            col = lambda t: t[:, :].rearrange("p (t o) -> p t o", o=1).broadcast_to([P, NX, NE])
            nc.vector.tensor_tensor(lg[:, :, :], lg[:, :, :], col(best), ALU.subtract).then_inc(shifted, 1)
            dve.wait_ge(exp_done, 1)
            link(nc.vector.reduce_sum(total[:, :], lg[:, :, :], AX.X))
            link(nc.vector.reciprocal(total[:, :], total[:, :]))
            link(nc.vector.tensor_tensor(lg[:, :, :], lg[:, :, :], col(total), ALU.mult))
            for t in range(NX):
                ins = nc.vector.max(top[:, t, :], lg[:, t, :])
            link(ins)
            link(nc.vector.tensor_tensor(pair_sum[:, :], top[:, :, 0], top[:, :, 1], ALU.add))
            link(nc.vector.reciprocal(pair_sum[:, :], pair_sum[:, :]))
            link(nc.vector.memset(top[:, :, 2:8], -1.0))
            for t in range(NX):
                ins = nc.vector.match_replace(left[:, t, :], top[:, t, :], lg[:, t, :], -2.0)
            link(ins)
            link(nc.vector.tensor_scalar(left[:, :, :], left[:, :, :], -1.5, None, ALU.is_lt))
            link(nc.vector.tensor_tensor(left[:, :, :], left[:, :, :], lg[:, :, :], ALU.mult))
            nc.vector.tensor_tensor(wt[:, :, 0:NE], left[:, :, :], col(pair_sum), ALU.mult).then_inc(weights_done, 1)
            for g in range(NB):
                dve.wait_ge(wt_read, g + 1)
                nc.vector.tensor_tensor(wt_l[:, g * QB:(g + 1) * QB], sbank(g), wt_h[:, g * QB:(g + 1) * QB],
                                        ALU.subtract).then_inc(wt_ready, 1)

            def residual(b):
                dve.wait_ge(step_used, (b + 1) * NE)
                for z in range(2):
                    xs = m.x[:, 4 * b + 2 * z:4 * b + 2 * z + 2, :].rearrange("p t d -> p (t d)")
                    ins = nc.vector.scalar_tensor_tensor(xs, obank(b, z), tgs[:, 0:1], xs, ALU.mult, ALU.add)
                ins.then_inc(out_used, 1)

            for n in range(STEPS):
                b, e = divmod(n, NE)
                dve.wait_ge(h_done, n + 1)
                dve.wait_ge(spread_ready, n + 1)
                nc.vector.tensor_tensor(y[:, n % 2, :], sbank(n), h[:, n % 2, :], ALU.mult).then_inc(y_done, 1)
                dve.wait_ge(yh_done, n + 1)
                nc.vector.tensor_tensor(y_l[:, n % 2, :], y[:, n % 2, :], y_h[:, n % 2, :], ALU.subtract).then_inc(yl_done, 1)
                if b and e == 1:
                    residual(b - 1)
            residual(NB - 1)

        @block.tensor
        def _(pe):
            pe.wait_ge(w_ready, 1)
            for t in range(NX):
                q = 0
                for wv, half in ((rw_h, m.xh), (rw_h, m.xl), (rw_l, m.xh)):
                    for c in range(DC):
                        ins = nc.tensor.matmul(hbank(0)[:, t * NE:(t + 1) * NE], half[:, c, t * P:(t + 1) * P], wv[:, c, :],
                                               start=(q == 0), stop=(q == 5))
                        q += 1
            ins.then_inc(routed, 1)

            def first(n):
                b, e = divmod(n, NE)
                if n >= 2:
                    pe.wait_ge(h_done, n - 1)
                elif n == 0:
                    pe.wait_ge(shifted, 1)
                    pe.wait_ge(w_ready, len(splits))
                q = 0
                for wv, half in ((w1_h, m.xh), (w1_h, m.xl), (w1_l, m.xh)):
                    for c in range(DC):
                        ins = nc.tensor.matmul(hbank(n), wv[:, c, e, :], half[:, c, b * QB:(b + 1) * QB], start=(q == 0), stop=(q == 5))
                        q += 1
                ins.then_inc(h_ready, 1)

            def spread(n):
                b, e = divmod(n, NE)
                if n >= 2:
                    pe.wait_ge(y_done, n - 1)
                for q, half in enumerate((wt_h, wt_l)):
                    ins = nc.tensor.matmul(sbank(n), pick[:, e, :], half[:, b * QB:(b + 1) * QB], start=(q == 0), stop=(q == 1))
                ins.then_inc(spread_ready, 1)

            def second(n):
                b, e = divmod(n, NE)
                if e == 0:
                    if b >= 2:
                        pe.wait_ge(out_used, b - 1)
                    for j in range(4):
                        for q, (half, bv) in enumerate(((wt_h, b2_h), (wt_h, b2_l), (wt_l, b2_h))):
                            nc.tensor.matmul(obank(b, j // 2)[:, (j % 2) * D:(j % 2 + 1) * D],
                                             half[:, b * QB + j * P:b * QB + (j + 1) * P], bv[:, :],
                                             start=(q == 0 and j % 2 == 0), stop=False, skip_group_check=True)
                pe.wait_ge(yl_done, n + 1)
                for j in range(4):
                    for q, (half, wv) in enumerate(((y_h, w2_h), (y_h, w2_l), (y_l, w2_h))):
                        ins = nc.tensor.matmul(obank(b, j // 2)[:, (j % 2) * D:(j % 2 + 1) * D],
                                               half[:, n % 2, j * P:(j + 1) * P], wv[:, e, :],
                                               start=False, stop=(e == NE - 1 and q == 2), skip_group_check=True)
                ins.then_inc(step_used, 1)

            first(0)
            first(1)
            pe.wait_ge(weights_done, 1)
            for g in range(NB):
                if g >= 2:
                    pe.wait_ge(wt_ready, g - 1)
                for j in range(4):
                    ins = nc.tensor.transpose(sbank(g)[:, j * P:(j + 1) * P], wt[:, 4 * g + j, :], m.ident[:, :])
                ins.then_inc(wt_turned, 1)
            pe.wait_ge(wt_ready, NB)
            spread(0)
            for n in range(STEPS):
                if n + 1 < STEPS:
                    if n >= 1:
                        first(n + 1)
                    spread(n + 1)
                second(n)


def stage_quantised(nc, m, xn, gate, wf, out):
    KF = FF // P
    with Semaphores(nc, "ffn") as sem, ExitStack() as ctx:
        def sb(name, shape, dt=FP32):
            return ctx.enter_context(nc.sbuf_tensor(f"ffn_{name}", shape, dt))

        wq = [sb(f"wq{n}", [P, 2048], BF16) for n in range(3)]
        ones = sb("ones", [P, P])
        wsum, wmean, wscale = sb("wsum", [P, 3]), sb("wmean", [P, 3]), sb("wscale", [P, 3])
        amax, ascale, adq = sb("amax", [P, NX]), sb("ascale", [P, NX]), sb("adq", [P, NX])
        gain = sb("gain", [P, 1])
        gs, us = sb("gate_scale", [P, NX]), sb("up_scale", [P, NX])
        xi = sb("xi", [P, 2, D])
        xt = sb("xt", [P, 3, DC, P], BF16)
        sg = sb("silu", [P, 2, FF])
        hh = sb("h", [P, 2, FF])
        hmax, hscale, hdq = sb("hmax", [P, 2]), sb("hscale", [P, 2]), sb("hdq", [P, 2])
        ht = sb("ht", [P, 2, KF, P], BF16)
        dvec, wsum_done, wmean_done, wq_done = sem("dve_chain"), sem("wsum_done"), sem("wmean_done"), sem("wq_done")
        xi_part = sem("xi_part")
        xi_ready, xt_turned, xt_ready = sem("xi_ready"), sem("xt_turned"), sem("xt_ready")
        gate_ready, up_ready, silu_done, h_done = sem("gate_ready"), sem("up_ready"), sem("silu_done"), sem("h_done")
        hi_ready, h_turned, ht_ready, down_ready, x_done = sem("hi_ready"), sem("h_turned"), sem("ht_ready"), sem("down_ready"), sem("x_done")
        scales_ready, stored = sem("scales_ready"), sem("stored")
        block = ctx.enter_context(nc.Block())

        @block.sync
        def _(sp):
            for t in range(NX):
                sp.wait_ge(x_done, t + 1)
                sp.dma_start(out[t * P:(t + 1) * P, :], m.x[:, t, :]).then_inc(stored, 16)
            sp.wait_ge(stored, 16 * NX)

        @block.vector
        def _(dve):
            chain = [0]

            def link(ins):
                chain[0] += 1
                ins.then_inc(dvec, 1)
                dve.wait_ge(dvec, chain[0])

            nc.vector.memset(ones[:, :], 1.0)
            for n in range(3):
                ins = nc.vector.tensor_reduce(wsum[:, n:n + 1], wf[n][:, :], AX.X, ALU.add, apply_absolute_value=True)
            ins.then_inc(wsum_done, 1)
            for t in range(NX):
                ins = nc.vector.tensor_reduce(amax[:, t:t + 1], xn[:, t, :], AX.X, ALU.max, apply_absolute_value=True)
            link(ins)
            link(nc.vector.tensor_scalar(amax[:, :], amax[:, :], 1e-5, None, ALU.max))
            link(nc.vector.reciprocal(ascale[:, :], amax[:, :]))
            nc.vector.tensor_scalar(ascale[:, :], ascale[:, :], 127.0, None, ALU.mult)
            link(nc.vector.tensor_scalar(adq[:, :], amax[:, :], 1.0 / 127.0, None, ALU.mult))
            dve.wait_ge(wmean_done, 1)
            link(nc.vector.tensor_scalar(wmean[:, :], m.bank[0][:, 0:3], 1.0 / (FF * D), 1e-5, ALU.mult, ALU.max))
            link(nc.vector.reciprocal(wscale[:, :], wmean[:, :]))
            nc.vector.tensor_scalar(gs[:, :], adq[:, :], wmean[:, 0:1], None, ALU.mult)
            nc.vector.tensor_scalar(gain[:, :], wmean[:, 2:3], m.tg[:, gate:gate + 1], None, ALU.mult)
            nc.vector.tensor_scalar(us[:, :], adq[:, :], wmean[:, 1:2], None, ALU.mult).then_inc(scales_ready, 1)
            for n in range(3):
                link(nc.vector.tensor_scalar(wf[n][:, :], wf[n][:, :], wscale[:, n:n + 1], ROUND, ALU.mult, ALU.add))
                link(nc.vector.tensor_scalar(wf[n][:, :], wf[n][:, :], ROUND, 1.0, ALU.subtract, ALU.min))
                nc.vector.tensor_scalar(wq[n][:, :], wf[n][:, :], -1.0, None, ALU.max).then_inc(wq_done, 1)

            def take_x(t):
                dve.wait_ge(xt_turned, t + 1)
                nc.vector.tensor_scalar(xt[:, t % 3, :, :].rearrange("p c q -> p (c q)"), m.bank[0][:, 0:D], -128.0, None, ALU.max).then_inc(xt_ready, 1)

            def residual(t):
                dve.wait_ge(down_ready, t + 1)
                nc.vector.scalar_tensor_tensor(m.x[:, t, :], m.bank[1][:, 0:D], hdq[:, t % 2:t % 2 + 1], m.x[:, t, :], ALU.mult, ALU.add).then_inc(x_done, 1)

            take_x(0)
            take_x(1)
            for t in range(NX):
                dve.wait_ge(up_ready, t + 1)
                dve.wait_ge(silu_done, t + 1)
                nc.vector.scalar_tensor_tensor(hh[:, t % 2, :], m.slot[1][:, :], us[:, t:t + 1], sg[:, t % 2, :],
                                               ALU.mult, ALU.mult).then_inc(h_done, 1)
                dve.wait_ge(h_done, t + 1)
                mx = hmax[:, t % 2:t % 2 + 1]
                link(nc.vector.tensor_reduce(mx, hh[:, t % 2, :], AX.X, ALU.max, apply_absolute_value=True))
                link(nc.vector.tensor_scalar(mx, mx, 1e-5, 1.0 / 127.0, ALU.max, ALU.mult))
                link(nc.vector.reciprocal(hscale[:, t % 2:t % 2 + 1], mx))
                link(nc.vector.tensor_scalar(hh[:, t % 2, :], hh[:, t % 2, :], hscale[:, t % 2:t % 2 + 1], ROUND, ALU.mult, ALU.add))
                nc.vector.tensor_scalar(hh[:, t % 2, :], hh[:, t % 2, :], ROUND, 127.0, ALU.subtract, ALU.min).then_inc(hi_ready, 1)
                link(nc.vector.tensor_scalar(hdq[:, t % 2:t % 2 + 1], mx, gain[:, :], None, ALU.mult))
                if t:
                    residual(t - 1)
                if t + 2 < NX:
                    take_x(t + 2)
            residual(NX - 1)

        @block.gpsimd
        def _(pool):
            pool.wait_ge(scales_ready, 1)
            for t in range(NX):
                if t >= 2:
                    pool.wait_ge(xt_turned, t - 1)
                nc.gpsimd.tensor_scalar(xi[:, t % 2, :], xn[:, t, :], ascale[:, t:t + 1], ROUND, ALU.mult, ALU.add).then_inc(xi_part, 1)
                pool.wait_ge(xi_part, t + 1)
                nc.gpsimd.tensor_scalar(xi[:, t % 2, :], xi[:, t % 2, :], ROUND, 127.0, ALU.subtract, ALU.min).then_inc(xi_ready, 1)

        def take_h(t, act):
            act.wait_ge(h_turned, t + 1)
            if t >= 2:
                act.wait_ge(down_ready, t - 1)
            nc.scalar.activation(ht[:, t % 2, :, :].rearrange("p k q -> p (k q)"), m.wide[:, :], ACT.Copy).then_inc(ht_ready, 1)

        @block.scalar
        def _(act):
            act.wait_ge(scales_ready, 1)
            for t in range(NX):
                act.wait_ge(gate_ready, t + 1)
                if t >= 2:
                    act.wait_ge(h_done, t - 1)
                nc.scalar.activation(sg[:, t % 2, :], m.slot[0][:, :], ACT.Silu, scale=gs[:, t:t + 1]).then_inc(silu_done, 1)
                if t:
                    take_h(t - 1, act)
            take_h(NX - 1, act)

        @block.tensor
        def _(pe):
            pe.wait_ge(wsum_done, 1)
            nc.tensor.matmul(m.bank[0][:, 0:3], ones[:, :], wsum[:, :], start=True, stop=True).then_inc(wmean_done, 1)

            def turn_x(t):
                pe.wait_ge(xi_ready, t + 1)
                pe.wait_ge(scales_ready, 1) if t == 0 else pe.wait_ge(xt_ready, t)
                for c in range(DC):
                    ins = nc.tensor.transpose(m.bank[0][:, c * P:(c + 1) * P], xi[:, t % 2, c * P:(c + 1) * P], m.ident[:, :])
                ins.then_inc(xt_turned, 1)

            def gate_up(t):
                pe.wait_ge(xt_ready, t + 1)
                for n, (slot, used, ready) in enumerate(((m.slot[0], silu_done, gate_ready), (m.slot[1], h_done, up_ready))):
                    if t == 0:
                        pe.wait_ge(wq_done, n + 1)
                    else:
                        pe.wait_ge(used, t)
                    for z in range(2):
                        for c in range(DC):
                            ins = nc.tensor.matmul(slot[:, z * 512:(z + 1) * 512], xt[:, t % 3, c, :],
                                                   wq[n][:, c * FF + z * 512:c * FF + (z + 1) * 512], start=(c == 0), stop=(c == DC - 1))
                    ins.then_inc(ready, 1)

            def turn_h(t):
                pe.wait_ge(hi_ready, t + 1)
                if t:
                    pe.wait_ge(ht_ready, t)
                for k in range(KF):
                    ins = nc.tensor.transpose(m.wide[:, k * P:(k + 1) * P], hh[:, t % 2, k * P:(k + 1) * P], m.ident[:, :])
                ins.then_inc(h_turned, 1)

            def down(t):
                pe.wait_ge(ht_ready, t + 1)
                if t == 0:
                    pe.wait_ge(wq_done, 3)
                else:
                    pe.wait_ge(x_done, t)
                for k in range(KF):
                    ins = nc.tensor.matmul(m.bank[1][:, 0:D], ht[:, t % 2, k, :], wq[2][:, k * D:(k + 1) * D], start=(k == 0), stop=(k == KF - 1))
                ins.then_inc(down_ready, 1)

            turn_x(0)
            turn_x(1)
            gate_up(0)
            for t in range(NX):
                if t + 1 < NX:
                    gate_up(t + 1)
                if t + 2 < NX:
                    turn_x(t + 2)
                turn_h(t)
                down(t)


def flamingo_kernel(nc, t, out, stages=4):
    with ExitStack() as ctx:
        m = allocate(nc, ctx)
        with nc.sbuf_tensor("ctx_rows", [P, NCT, D], FP32) as rows:
            stage_setup(nc, m, t["x"], t["gates"], rows, t["ctx"])
            stage_norm(nc, m, "nc0", rows, NCT, m.ch, m.cl, affine=t["gb1"])
        if stages >= 1:
            stage_norm(nc, m, "nx0", m.x, NX, m.xh, m.xl, norms=2, affine=t["gb2"])
            stage_attention(nc, m, Attention("a0", True, 64, 2, 0.125, False, 0), t["w0"], t["wo0"], (t["mask_row"], t["mask_cols"]))
        if stages >= 2:
            with ExitStack() as moe:
                experts, fetch = expert_weights(nc, moe, t["rw"], t["rb"], t["w1"], t["eb1"], t["w2"], t["eb2"])
                stage_norm(nc, m, "nx1", m.x, NX, m.xh, m.xl, ahead_of_use=fetch, context=t["ctxt"])
                stage_experts(nc, m, 2, experts)
        if stages >= 3:
            stage_norm(nc, m, "nx2", m.x, NX, m.xh, m.xl)
            wf = [ctx.enter_context(nc.sbuf_tensor(f"ffn_w{n}", [P, FF * DC], FP32)) for n in range(3)]
            chunks = (DC, DC, FF // P)
            fetch = [(w[:, :].rearrange("p (c f) -> p c f", c=c), src.rearrange("(c p) f -> p c f", p=P))
                     for w, c, src in zip(wf, chunks, (t["wg"], t["wu"], t["wd"]))]
            stage_attention(nc, m, Attention("a1", False, 16, 4, 0.25, True, 1), t["w1a"], t["wo1"], (t["all_row"], t["all_cols"]),
                            t["bv"], t["bo"], fetch)
        if stages >= 4:
            with nc.sbuf_tensor("xn_rows", [P, NX, D], FP32) as rows:
                stage_norm(nc, m, "nx3", m.x, NX, rows=rows)
                stage_quantised(nc, m, rows, 3, wf, out)
        else:
            stage_store(nc, m, out)


def lay_out(x, ctx_1024, mask_BxS2_bk0, g_xattn, g_ffn, L0_xattn_g1, L0_xattn_b1, L0_xattn_g2, L0_xattn_b2, L0_xattn_Wq,
            L0_xattn_Wkv, L0_xattn_Wout, L0_ffn_router_w, L0_ffn_router_b, L0_ffn_W1, L0_ffn_b1, L0_ffn_W2, L0_ffn_b2,
            L1_xattn_Wq, L1_xattn_bq, L1_xattn_Wk, L1_xattn_bk, L1_xattn_Wv, L1_xattn_bv, L1_xattn_Wo, L1_xattn_bo,
            L1_ffn_w_gate, L1_ffn_w_up, L1_ffn_w_down):
    import numpy as np

    def iterations(wq, wk, wv, *biases):
        n = wq.shape[1] // P

        def blocks(w):
            return w.reshape(DC, P, n, P).transpose(2, 1, 0, 3)
        out = np.zeros((n + 1, P, 3, DC, P), wq.dtype)
        out[:n, :, 0] = blocks(wq)
        out[:n, :, 1] = blocks(wk)
        out[1:, :, 2] = blocks(wv)
        out = out.reshape(n + 1, P, 3 * DC * P)
        if biases:
            own = np.zeros((n + 1, P, 2), wq.dtype)
            for j, b in enumerate(biases):
                own[:n, :, j] = b.reshape(n, P)
            out = np.concatenate([out, own], axis=2)
        return out

    def pad_heads(a):
        out = np.zeros((*a.shape[:-1], 16, 32), a.dtype)
        out[..., :16] = a.reshape(*a.shape[:-1], 16, 16)
        return out.reshape(*a.shape[:-1], 16 * 32)

    def columns(*rows):
        return np.stack([r.reshape(-1, P).T for r in rows], axis=1)

    def pad_mask(mask):
        row = np.zeros((1, CTXP), bool)
        row[:, :CTX] = mask
        return row, row.reshape(NCT, P).T

    mask_row, mask_cols = pad_mask(mask_BxS2_bk0)
    all_row, all_cols = pad_mask(np.ones((1, CTX), bool))
    inner = L0_xattn_Wq.shape[1]
    expert_b2 = np.zeros((P, D), L0_ffn_b2.dtype)
    expert_b2[:NE] = L0_ffn_b2
    return {
        "x": x[0], "ctx": ctx_1024[0], "ctxt": ctx_1024[0].T, "mask_row": mask_row, "mask_cols": mask_cols,
        "all_row": all_row, "all_cols": all_cols,
        "gates": np.stack([g_xattn[0], g_xattn[1], g_ffn[0], g_ffn[1]])[None],
        "gb1": columns(L0_xattn_g1, L0_xattn_b1), "gb2": columns(L0_xattn_g2, L0_xattn_b2),
        "w0": iterations(L0_xattn_Wq, L0_xattn_Wkv[:, :inner], L0_xattn_Wkv[:, inner:]),
        "wo0": L0_xattn_Wout.reshape(-1, P, D),
        "rw": L0_ffn_router_w, "rb": L0_ffn_router_b[None], "w1": L0_ffn_W1, "eb1": L0_ffn_b1.T, "w2": L0_ffn_W2, "eb2": expert_b2,
        "w1a": iterations(pad_heads(L1_xattn_Wq.T), pad_heads(L1_xattn_Wk.T), pad_heads(L1_xattn_Wv.T),
                          pad_heads(L1_xattn_bq), pad_heads(L1_xattn_bk)),
        "wo1": pad_heads(L1_xattn_Wo).T.reshape(-1, P, D),
        "bv": pad_heads(L1_xattn_bv)[None], "bo": L1_xattn_bo[None],
        "wg": L1_ffn_w_gate.T, "wu": L1_ffn_w_up.T, "wd": L1_ffn_w_down.T,
    }


def kernel(**inputs):
    import numpy as np
    import concourse.bacc as bacc
    from concourse.bass_utils import run_bass_kernel_spmd

    arrays = {f"in_{k}": np.ascontiguousarray(v) for k, v in lay_out(**{k: np.asarray(v) for k, v in inputs.items()}).items()}
    nc = bacc.Bacc("TRN2", target_bir_lowering=False, num_devices=1)
    t = {k[3:]: nc.dram_tensor(k, v.shape, mybir.dt.from_np(v.dtype), kind="ExternalInput").ap() for k, v in arrays.items()}
    out = nc.dram_tensor("out_x", (TOK, D), FP32, kind="ExternalOutput").ap()
    flamingo_kernel(nc, t, out)
    result = run_bass_kernel_spmd(nc, [arrays], core_ids=[0])
    return result.results[0]["out_x"].reshape(1, TOK, D)
```
